# Optimizing a Trainium2 kernel written in Bass

```python
import numpy as np
import jax
import jax.numpy as jnp

def _softmax(x, axis=-1):
    return jax.nn.softmax(x, axis=axis)

def _gelu(x):
    return jax.nn.gelu(x, approximate=True)

def _silu(x):
    return jax.nn.silu(x)

def _sigmoid(x):
    return jax.nn.sigmoid(x)

def _layernorm(x, axis=-1, eps=1e-05):
    m = jnp.mean(x, axis=axis, keepdims=True)
    v = jnp.var(x, axis=axis, keepdims=True)
    return (x - m) / jnp.sqrt(v + eps)

def _scatter_add(tgt, idx, src, axis=0):
    return tgt.at[idx].add(src)

def _segment_sum(src, seg, n):
    return jax.ops.segment_sum(src, seg, n)
kernel_name = 'mk_gnn_ffn_d1_gnn_r8_85a42b'

def setup_inputs(seed: int=0):
    np.random.seed(seed)
    _w = jnp.asarray

    def _rec_inputs():
        import jax
        import jax.numpy as jnp
        _gk = jax.random.key(seed)
        x = -0.0006008 + 1.001 * jax.random.normal(jax.random.fold_in(_gk, 1), (6250, 256), jnp.float32)
        src = jax.random.randint(jax.random.fold_in(_gk, 2), (200000,), 0, 6250, jnp.int32)
        dst = jax.random.randint(jax.random.fold_in(_gk, 3), (200000,), 0, 6250, jnp.int32)
        _o = jnp.argsort(dst, stable=True)
        src = src[_o]
        dst = dst[_o]
        return (x, src, dst)
    x, src, dst = _rec_inputs()

    def _L0_gnn_setup():
        import jax, jax.numpy as jnp
        import numpy as np
        N_NODES = 1250
        N_EDGES = 40000
        D = 256
        key = jax.random.key(seed)
        k_x, k_w, k_m, k_s, k_d = jax.random.split(key, 5)
        x = jax.random.normal(k_x, (N_NODES, D), dtype=jnp.float32)
        W = jax.random.normal(k_w, (D, D), dtype=jnp.float32)
        M = jax.random.normal(k_m, (D, D), dtype=jnp.float32)
        edge_src = jax.random.randint(k_s, (N_EDGES,), 0, N_NODES, dtype=jnp.int64)
        edge_dst = jax.random.randint(k_d, (N_EDGES,), 0, N_NODES, dtype=jnp.int64)
        return {'x': x, 'W': W, 'M': M, 'edge_src': edge_src, 'edge_dst': edge_dst}
    _L0_gnn_all = _L0_gnn_setup()
    _L0_gnn_in = {k: v for k, v in _L0_gnn_all.items() if k in ('W', 'M')}
    del _L0_gnn_all

    def _L0_ffn_setup():
        import jax, jax.numpy as jnp
        import numpy as np
        B, N, D = (16, 512, 256)
        NUM_EXPERTS, TOP_K, HEADS = (4, 2, 4)
        N_EDGES = 131072
        LN_EPS = 1e-05

        def _layernorm(x, g, b):
            mu = x.mean(-1, keepdims=True)
            var = ((x - mu) ** 2).mean(-1, keepdims=True)
            return (x - mu) * jax.lax.rsqrt(var + LN_EPS) * g + b

        def _forward(x, edge_index, W_gat, att_src, att_dst, b_gat, ln_gamma, ln_beta, W1, b1, W2, b2):
            Bc, Nc, Dc = x.shape
            M = Bc * Nc
            x_flat = x.reshape(M, Dc)
            h = (x_flat @ W_gat).reshape(M, HEADS, NUM_EXPERTS)
            loops = jnp.arange(M, dtype=edge_index.dtype)
            src = jnp.concatenate([edge_index[0], loops])
            dst = jnp.concatenate([edge_index[1], loops])
            a_src = (h * att_src).sum(-1)
            a_dst = (h * att_dst).sum(-1)
            e = jax.nn.leaky_relu(a_src[src] + a_dst[dst], negative_slope=0.2)
            e_max = jax.ops.segment_max(e, dst, num_segments=M)
            ee = jnp.exp(e - e_max[dst])
            denom = jax.ops.segment_sum(ee, dst, num_segments=M)
            alpha = ee / (denom[dst] + 1e-16)
            msg = h[src] * alpha[:, :, None]
            agg = jax.ops.segment_sum(msg, dst, num_segments=M).reshape(M, HEADS * NUM_EXPERTS) + b_gat
            scores = _layernorm(agg, ln_gamma, ln_beta).reshape(M, HEADS, NUM_EXPERTS).mean(1)
            scores = scores.reshape(Bc, Nc, NUM_EXPERTS)
            topk_s, topk_i = jax.lax.top_k(scores, TOP_K)
            w = jax.nn.softmax(topk_s, axis=-1)
            out = jnp.zeros_like(x)
            for ei in range(NUM_EXPERTS):
                g = jnp.where(topk_i == ei, w, 0.0).sum(-1)
                hh = jax.nn.gelu(x @ W1[ei] + b1[ei], approximate=False)
                out = out + g[..., None] * (hh @ W2[ei] + b2[ei])
            return out
        key = jax.random.key(seed)
        ks = jax.random.split(key, 8)
        s = 0.05
        return {'x': jax.random.normal(ks[0], (B, N, D), jnp.float32), 'W_gat': jax.random.normal(ks[1], (D, HEADS * NUM_EXPERTS), jnp.float32) * s, 'att_src': jax.random.normal(ks[2], (HEADS, NUM_EXPERTS), jnp.float32) * s, 'att_dst': jax.random.normal(ks[3], (HEADS, NUM_EXPERTS), jnp.float32) * s, 'b_gat': jnp.zeros((HEADS * NUM_EXPERTS,), jnp.float32), 'ln_gamma': jnp.ones((HEADS * NUM_EXPERTS,), jnp.float32), 'ln_beta': jnp.zeros((HEADS * NUM_EXPERTS,), jnp.float32), 'W1': jax.random.normal(ks[4], (NUM_EXPERTS, D, 2 * D), jnp.float32) * s, 'b1': jnp.zeros((NUM_EXPERTS, 2 * D), jnp.float32), 'W2': jax.random.normal(ks[5], (NUM_EXPERTS, 2 * D, D), jnp.float32) * s, 'b2': jnp.zeros((NUM_EXPERTS, D), jnp.float32), 'edge_index': jax.random.randint(ks[6], (2, N_EDGES), 0, B * N, jnp.int32)}
    _L0_ffn_all = _L0_ffn_setup()
    _L0_ffn_in = {k: v for k, v in _L0_ffn_all.items() if k in ('W_gat', 'att_src', 'att_dst', 'b_gat', 'ln_gamma', 'ln_beta', 'W1', 'b1', 'W2', 'b2', 'edge_index')}
    del _L0_ffn_all
    return {'x': x, 'src': src, 'dst': dst, 'L0_gnn_W': _L0_gnn_in['W'], 'L0_gnn_M': _L0_gnn_in['M'], 'L0_ffn_W_gat': _L0_ffn_in['W_gat'], 'L0_ffn_att_src': _L0_ffn_in['att_src'], 'L0_ffn_att_dst': _L0_ffn_in['att_dst'], 'L0_ffn_b_gat': _L0_ffn_in['b_gat'], 'L0_ffn_ln_gamma': _L0_ffn_in['ln_gamma'], 'L0_ffn_ln_beta': _L0_ffn_in['ln_beta'], 'L0_ffn_W1': _L0_ffn_in['W1'], 'L0_ffn_b1': _L0_ffn_in['b1'], 'L0_ffn_W2': _L0_ffn_in['W2'], 'L0_ffn_b2': _L0_ffn_in['b2'], 'L0_ffn_edge_index': _L0_ffn_in['edge_index']}

def reference(x, src, dst, L0_gnn_W, L0_gnn_M, L0_ffn_W_gat, L0_ffn_att_src, L0_ffn_att_dst, L0_ffn_b_gat, L0_ffn_ln_gamma, L0_ffn_ln_beta, L0_ffn_W1, L0_ffn_b1, L0_ffn_W2, L0_ffn_b2, L0_ffn_edge_index):
    import jax
    import jax.numpy as jnp

    def _L0_gnn_ref(x, W, M, edge_src, edge_dst):
        import jax, jax.numpy as jnp
        import numpy as np
        N_NODES = 1250
        N_EDGES = 40000
        D = 256
        self_term = x @ W
        msg = x @ M
        agg = jax.ops.segment_sum(msg[edge_src], edge_dst, num_segments=x.shape[0])
        return jax.nn.relu(self_term + agg)

    def _L0_ffn_ref(x, W_gat, att_src, att_dst, b_gat, ln_gamma, ln_beta, W1, b1, W2, b2, edge_index):
        import jax, jax.numpy as jnp
        import numpy as np
        B, N, D = (16, 512, 256)
        NUM_EXPERTS, TOP_K, HEADS = (4, 2, 4)
        N_EDGES = 131072
        LN_EPS = 1e-05

        def _layernorm(x, g, b):
            mu = x.mean(-1, keepdims=True)
            var = ((x - mu) ** 2).mean(-1, keepdims=True)
            return (x - mu) * jax.lax.rsqrt(var + LN_EPS) * g + b

        def _forward(x, edge_index, W_gat, att_src, att_dst, b_gat, ln_gamma, ln_beta, W1, b1, W2, b2):
            Bc, Nc, Dc = x.shape
            M = Bc * Nc
            x_flat = x.reshape(M, Dc)
            h = (x_flat @ W_gat).reshape(M, HEADS, NUM_EXPERTS)
            loops = jnp.arange(M, dtype=edge_index.dtype)
            src = jnp.concatenate([edge_index[0], loops])
            dst = jnp.concatenate([edge_index[1], loops])
            a_src = (h * att_src).sum(-1)
            a_dst = (h * att_dst).sum(-1)
            e = jax.nn.leaky_relu(a_src[src] + a_dst[dst], negative_slope=0.2)
            e_max = jax.ops.segment_max(e, dst, num_segments=M)
            ee = jnp.exp(e - e_max[dst])
            denom = jax.ops.segment_sum(ee, dst, num_segments=M)
            alpha = ee / (denom[dst] + 1e-16)
            msg = h[src] * alpha[:, :, None]
            agg = jax.ops.segment_sum(msg, dst, num_segments=M).reshape(M, HEADS * NUM_EXPERTS) + b_gat
            scores = _layernorm(agg, ln_gamma, ln_beta).reshape(M, HEADS, NUM_EXPERTS).mean(1)
            scores = scores.reshape(Bc, Nc, NUM_EXPERTS)
            topk_s, topk_i = jax.lax.top_k(scores, TOP_K)
            w = jax.nn.softmax(topk_s, axis=-1)
            out = jnp.zeros_like(x)
            for ei in range(NUM_EXPERTS):
                g = jnp.where(topk_i == ei, w, 0.0).sum(-1)
                hh = jax.nn.gelu(x @ W1[ei] + b1[ei], approximate=False)
                out = out + g[..., None] * (hh @ W2[ei] + b2[ei])
            return out
        return _forward(x, edge_index, W_gat, att_src, att_dst, b_gat, ln_gamma, ln_beta, W1, b1, W2, b2)
    x = x + _L0_gnn_ref(_layernorm(x, axis=-1), L0_gnn_W, L0_gnn_M, src, dst)
    x = x + _L0_ffn_ref(_layernorm(x, axis=-1)[None], L0_ffn_W_gat, L0_ffn_att_src, L0_ffn_att_dst, L0_ffn_b_gat, L0_ffn_ln_gamma, L0_ffn_ln_beta, L0_ffn_W1, L0_ffn_b1, L0_ffn_W2, L0_ffn_b2, L0_ffn_edge_index)[0]
    return x

_drawn_inputs = setup_inputs


def setup_inputs(seed=0):
    import zlib

    import numpy as np

    out = dict(_drawn_inputs(seed))
    spreads = {'L0_ffn_b_gat': (0.0, 0.8),
     'L0_ffn_ln_gamma': (1.0, 0.6),
     'L0_ffn_ln_beta': (0.0, 0.8),
     'L0_ffn_b1': (0.0, 0.8),
     'L0_ffn_b2': (0.0, 0.8)}
    factors = {'L0_ffn_W_gat': 8.0,
     'L0_ffn_att_src': 8.0,
     'L0_ffn_att_dst': 8.0,
     'L0_ffn_W1': 8.0,
     'L0_ffn_W2': 8.0}
    for name, (base, spread) in spreads.items():
        noise = np.random.default_rng([zlib.crc32(name.encode()), seed]).standard_normal(out[name].shape)
        drawn = base * np.exp(spread * noise) if base else spread * noise
        out[name] = jnp.asarray(drawn.astype(out[name].dtype))
    for name, factor in factors.items():
        out[name] = (out[name] * factor).astype(out[name].dtype)
    return out
```

```python
import concourse.bass as bass
from concourse import mybir

F32 = mybir.dt.float32
BF16 = mybir.dt.bfloat16
I32 = mybir.dt.int32
ALU = mybir.AluOpType
ACT = mybir.ActivationFunctionType
AXX = mybir.AxisListType.X

P = 128
EPS = 1e-5
BIG = 1.0e30
FAR = 1 << 21
RING = 4
JC = 8
GB = 4
HEADS = 4


class Marks:

    def __init__(self, nc):
        self.nc, self.sems = nc, {}

    def sem(self, name):
        if name not in self.sems:
            self.sems[name] = self.nc.alloc_semaphore(name)
        return self.sems[name]


class Queue:

    lanes = None

    def __init__(self, marks, eng, name):
        self.m, self.eng, self.name, self.n, self.passed = marks, eng, name, 0, {}

    def wait(self, *marks):
        for name, value in marks:
            if self.passed.get(name, 0) < value:
                self.eng.wait_ge(self.m.sem(name), value)
                self.passed[name] = value

    def run(self, ins):
        ins.then_inc(self.m.sem(self.name), 1)
        self.n += 1
        return (self.name, self.n)

    def sent(self, lane, ins):
        ins.then_inc(self.m.sem(lane), 16)
        self.lanes[lane] = self.lanes.get(lane, 0) + 16
        return (lane, self.lanes[lane])

    def dma(self, lane, out, in_):
        return self.sent(lane, self.eng.dma_start(out, in_))


def build(nc, x, src, dst, W, M, W_gat, att_src, att_dst, b_gat, ln_gamma, ln_beta,
          W1, b1, W2, b2, edge_index, out):
    N, D = x.shape
    E1, E2 = src.shape[0], edge_index.shape[1]
    NX, _, F = W1.shape
    HX = HEADS * NX
    KD, KF = D // P, F // P
    NT = -(-N // P)
    NPAD = NT * P
    C1 = -(-E1 // P)
    C1 = -(-C1 // JC) * JC
    C2 = E2 // P
    NCH = C1 // JC
    NG = C2 // GB
    XG = 7
    FE = HX + HEADS
    FULL = (N // P) * P
    assert NT % XG == 0 and E2 % P == 0 and C2 % (2 * GB) == 0 and N < NPAD and D == 256

    def dram(name, shape, dt):
        return nc.dram_tensor(name, shape, dt).ap()

    xn_d = dram("xn_d", [NPAD, D], F32)
    run_d = dram("run_d", [P * C1, D], F32)
    dst_d = dram("dst_d", [P, C1], I32)
    sorted_d = dram("sorted_d", [E2, 2], I32)
    tab_d = dram("tab_d", [NPAD, FE], F32)
    x1_d = dram("x1_d", [NPAD, D], F32)
    xT_d = dram("xT_d", [P, KD, NPAD], F32)
    y_d = dram("y_d", [NX, NPAD, D], F32)
    max_d = dram("max_d", [E2, HEADS], F32)
    node_d = dram("node_d", [NPAD, 2 * HEADS], F32)
    start_d = dram("start_d", [E2, 2 * HEADS], F32)
    sum_d = dram("sum_d", [E2, FE], F32)

    base = -(-nc.sbuf_base // 64) * 64
    top = nc.sbuf_base + nc.sbuf_bytes_remaining

    class Region:
        def __init__(self, at):
            self.at = at

        def take(self, name, shape, dt):
            n = 1
            for s in shape[1:]:
                n *= s
            size = -(-n * mybir.dt.size(dt) // 32) * 32
            t = nc.alloc_sbuf_tensor_at(name, shape, dt, offset=self.at)
            self.at += size
            assert self.at <= top, (name, self.at, top)
            return t

    r = Region(base)
    iota_i = r.take("iota_i", [P, P], I32)
    iota_b = r.take("iota_b", [P, P], BF16)
    ident = r.take("ident", [P, P], F32)
    ident_b = r.take("ident_b", [P, P], BF16)
    ones = r.take("ones", [P, P], F32)
    before = r.take("before", [P, P], F32)
    after = r.take("after", [P, P], F32)
    shift1 = r.take("shift1", [P, P], F32)
    wrap1 = r.take("wrap1", [P, P], F32)
    node_id = r.take("node_id", [P, NT], F32)
    node_ii = r.take("node_ii", [P, NT], I32)
    row_at = r.take("row_at", [P, 2], I32)
    idx_g = r.take("idx_g", [P, NT], I32)
    has_g = r.take("has_g", [P, NT], F32)
    idx_f = r.take("idx_f", [P, NT], I32)
    idx_s = r.take("idx_s", [P, NT], I32)
    has_f = r.take("has_f", [P, NT], F32)
    sm = r.take("sm", [P, 64], F32)
    smi = r.take("smi", [P, 16], I32)
    smt = r.take("smt", [P, 8, NT], F32)
    feat = r.take("feat", [P, NT, FE + HEADS], F32)
    attb = r.take("attb", [P, 2, HX], F32)
    gln = r.take("gln", [P, 3, HX], F32)
    wgat = r.take("wgat", [P, KD, HX], F32)
    wself = r.take("wself", [P, KD, D], F32)
    wmsg = r.take("wmsg", [P, KD, D], F32)
    b1c = r.take("b1c", [P, NX, KF], F32)
    b2b = r.take("b2b", [P, NX, D], F32)
    tmask = r.take("tmask", [P, P], F32)
    cfix = r.take("cfix", [P, D], F32)
    r4 = r.at
    ed = r.take("ed", [P, C2, 2], I32)
    dl = r.take("dl", [P, C2], BF16)
    dh = r.take("dh", [P, C2], BF16)
    place = r.take("place", [P, C2], I32)
    q = Region(r4)
    srt = q.take("srt", [P, C2, 2], I32)
    same_f = q.take("same_f", [P, C2], F32)
    reset_f = q.take("reset_f", [P, C2], F32)
    assert q.at <= r.at
    raw_e = Region(r.at).take("raw_e", [P, 2, C2], I32)
    runmax = r.take("runmax", [P, C2, HEADS], F32)
    r2 = r.at
    w1s = r.take("w1s", [P, NX, KD, F], F32)
    w2s = r.take("w2s", [P, NX, KF, D], F32)
    q = Region(r2)
    dsti = q.take("dsti", [P, C1], I32)
    srci = q.take("srci", [P, C1], I32)
    same_g = q.take("same_g", [P, C1], F32)
    rows = q.take("rows", [P, 2, C1], I32)
    assert q.at <= r.at
    r3 = r.at
    hh = r.take("hh", [P, 2, KF, 4 * P], F32)
    xt = r.take("xt", [P, 2, KD, 4 * P], F32)
    yo = r.take("yo", [P, 4, D], F32)
    agg = r.take("agg", [P, 4, D], F32)
    xno = r.take("xno", [P, 4, D], F32)
    tin = r.take("tin", [P, 2, 4, P], F32)
    q = Region(r3)
    oh = q.take("oh", [P, 4, GB, P], BF16)
    dhh = q.take("dhh", [P, 4, GB, NT], BF16)
    oht = q.take("oht", [P, 3, GB, P], F32)
    eqm = q.take("eqm", [P, 2, GB, P], BF16)
    hist = q.take("hist", [P, 3, GB, NT], F32)
    prod = q.take("prod", [P, GB, NT], F32)
    hinit = q.take("hinit", [P, NT], F32)
    cmpb = q.take("cmpb", [P, XG, P], F32)
    assert q.at <= r.at
    q = Region(r2)
    edge_n = q.take("edge_n", [P, C2, 2 * HEADS], F32)
    fin = q.take("fin", [P, 10, NT, HX], F32)
    fsum = q.take("fsum", [P, NT, FE], F32)
    assert q.at <= r.at
    r1 = r.at
    xs = r.take("xs", [P, NT, D], F32)
    ring = r.take("ring", [P, RING, JC, D], F32)
    q = Region(r1)
    g = q.take("g", [P, C2, FE], F32)
    assert q.at <= r.at
    q = Region(r1)
    comb = q.take("comb", [P, 2, NX + 1, XG // 7 * 7, D], F32)

    bank = [nc.alloc_psum_tensor(f"bank{i}", [P, 512], F32) for i in range(7)]
    bank_t = nc.alloc_psum_tensor("bank_t", [P, GB, P], BF16)

    marks = Marks(nc)
    Queue.lanes = {}
    pe, dve, act, pool, sp = (Queue(marks, e, n) for e, n in (
        (nc.tensor, "pe_done"), (nc.vector, "dve_done"), (nc.scalar, "act_done"),
        (nc.gpsimd, "pool_done"), (nc.sync, "sp_done")))
    V, S, T, G = nc.vector, nc.scalar, nc.tensor, nc.gpsimd

    def vrun(ins, *_):
        m = dve.run(ins)
        dve.wait(m)
        return m

    def at_rows(ap):
        return bass.IndirectOffsetOnAxis(ap=ap, axis=0)

    pool.run(G.iota(iota_i[:, :], pattern=[[1, P]], base=0, channel_multiplier=0))
    pool.run(G.iota(node_ii[:, :], pattern=[[P, NT]], base=0, channel_multiplier=1))
    pool.run(G.iota(row_at[:, 0:1], pattern=[[0, 1]], base=0, channel_multiplier=C1))
    pool.run(G.iota(row_at[:, 1:2], pattern=[[0, 1]], base=0, channel_multiplier=C2))
    for t in (ident, shift1, wrap1):
        pool.run(G.memset(t[:, :], 0.0))
    m = pool.run(G.memset(ones[:, :], 1.0))
    pool.wait(m)
    pool.run(G.affine_select(out=ident[:, :], in_=ident[:, :], compare_op=ALU.not_equal, fill=1.0, base=0,
                             pattern=[[-1, P]], channel_multiplier=1))
    pool.run(G.affine_select(out=shift1[:, :], in_=shift1[:, :], compare_op=ALU.not_equal, fill=1.0, base=1,
                             pattern=[[-1, P]], channel_multiplier=1))
    pool.run(G.affine_select(out=wrap1[:, :], in_=wrap1[:, :], compare_op=ALU.not_equal, fill=1.0,
                             base=-(P - 1), pattern=[[P, P]], channel_multiplier=1))
    pool.run(G.affine_select(out=before[:, :], in_=ones[:, :], compare_op=ALU.is_gt, fill=0.0, base=0,
                             pattern=[[1, P]], channel_multiplier=-1))
    consts = pool.run(G.affine_select(out=after[:, :], in_=ones[:, :], compare_op=ALU.is_gt, fill=0.0, base=0,
                                      pattern=[[-1, P]], channel_multiplier=1))

    pad_x = dve.run(V.memset(xs[:, NT - 1, :], 0.0))
    dve.run(V.memset(dsti[:, :], N))
    pad_e = dve.run(V.memset(srci[:, :], 0))
    sp.wait(pad_x)
    x_in = []
    for c in range(NT // XG):
        t0, t1 = c * XG, min((c + 1) * XG, FULL // P)
        m = sp.dma(f"x_in{c}", xs[:, t0:t1, :], x[t0 * P:t1 * P, :].rearrange("(t p) d -> p t d", p=P))
        if c == NT // XG - 1:
            m = sp.dma(f"x_in{c}", xs[0:N - FULL, NT - 1, :], x[FULL:N, :])
        x_in.append(m)
    act.wait(pad_e)
    fullrows = E1 // C1
    cut = fullrows // 16 * 16
    for a, t in ((dst, dsti), (src, srci)):
        lane = "dst_in" if a is dst else "src_in"
        full = a[0:fullrows * C1].rearrange("(p j) -> p j", j=C1)
        act.dma(lane, t[0:cut, :], full[0:cut, :])
        act.dma(lane, t[cut:fullrows, :], full[cut:fullrows, :])
        act.dma(lane, t[fullrows:fullrows + 1, 0:E1 - fullrows * C1],
                a[fullrows * C1:E1].rearrange("(a j) -> a j", a=1))
    dst_in, src_in = ("dst_in", 48), ("src_in", 48)
    for c in range(2):
        e_in = act.dma("e_in", raw_e[:, c, :], edge_index[c, :].rearrange("(p j) -> p j", j=C2))
    act.wait(dst_in)
    dst_out = act.dma("dst_out", dst_d, dsti[:, :])
    act.dma("w_in", wself[:, :, :], W.rearrange("(k p) n -> p k n", p=P))
    act.dma("w_in", wmsg[:, :, :], M.rearrange("(k p) n -> p k n", p=P))
    act.dma("w_in", wgat[:, :, :], W_gat.rearrange("(k p) n -> p k n", p=P))
    for k, a in enumerate((att_src, att_dst)):
        act.dma("w_in", attb[:, k, :], a.rearrange("h e -> (h e)").partition_broadcast(P))
    for k, a in enumerate((b_gat, ln_gamma, ln_beta)):
        act.dma("w_in", gln[:, k, :], a.partition_broadcast(P))
    with nc.allow_non_contiguous_dma(reason="b1 by column, 8 KB once"):
        act.dma("w_in", b1c[:, :, :], b1.rearrange("e (f p) -> p e f", p=P))
    for e in range(NX):
        w_in = act.dma("w_in", b2b[:, e, :], b2[e, :].partition_broadcast(P))

    def norm_scalars(c, stats, aggr):
        m = vrun(V.tensor_scalar(aggr[:, :, 1], aggr[:, :, 1], EPS, None, ALU.add))
        act.wait(m)
        m = act.run(S.activation(aggr[:, :, 1], aggr[:, :, 1], ACT.Sqrt))
        dve.wait(m)
        vrun(V.reciprocal(aggr[:, :, 1], aggr[:, :, 1]))
        return dve.run(V.scalar_tensor_tensor(out=aggr[:, :, 0], in0=aggr[:, :, 0], scalar=-1.0,
                                              in1=aggr[:, :, 1], op0=ALU.mult, op1=ALU.mult))

    stat = r.take("stat", [P, XG, 6], F32)
    aggr = r.take("aggr", [P, NT, 2], F32)
    xn_out = []
    for c in range(NT // XG):
        dve.wait(x_in[c])
        for k in range(XG):
            m = dve.run(V.bn_stats(stat[:, k, :], xs[:, c * XG + k, :]))
        dve.wait(m)
        for k in range(XG):
            m = dve.run(V.bn_aggr(aggr[:, c * XG + k, :], stat[:, k, :]))
        dve.wait(m)
        m = norm_scalars(c, stat, aggr[:, c * XG:(c + 1) * XG, :])
        act.wait(m)
        if c >= RING:
            act.wait(xn_out[c - RING])
        for k in range(XG):
            t = c * XG + k
            m = act.run(S.activation(ring[:, c % RING, k, :], xs[:, t, :], ACT.Identity,
                                     bias=aggr[:, t, 0:1], scale=aggr[:, t, 1:2]))
        sp.wait(m)
        xn_out.append(sp.dma(f"xn_out{c % RING}",
                             xn_d[c * XG * P:(c + 1) * XG * P, :].rearrange("(t p) d -> p t d", p=P),
                             ring[:, c % RING, 0:XG, :]))

    dve.wait(consts, dst_in)
    dve.run(V.tensor_copy(iota_b[:, :], iota_i[:, :]))
    dve.run(V.tensor_copy(node_id[:, :], node_ii[:, :]))
    dve.run(V.tensor_copy(ident_b[:, :], ident[:, :]))
    dve.run(V.memset(same_g[:, 0:1], 0.0))
    vrun(V.tensor_tensor(same_g[:, 1:C1], dsti[:, 1:C1], dsti[:, 0:C1 - 1], ALU.is_equal))

    def broadcast_cols(col, free, bank_out, m_free=None):
        m = vrun(V.tensor_scalar(tmask[:, :], ident[:, :], col, None, ALU.mult))
        pe.wait(m, *free)
        return pe.run(T.matmul(bank_out, ones[:, :], tmask[:, :], start=True, stop=True))

    vrun(V.tensor_copy(sm[:, 0:1], dsti[:, 0:1]))
    vrun(V.tensor_copy(sm[:, 1:2], dsti[:, C1 - 1:C1]))
    m_rowheads = broadcast_cols(sm[:, 0:1], (), bank[6][:, 0:P])
    dve.wait(m_rowheads)
    for c in range(NT // XG):
        vrun(V.tensor_tensor(cmpb[:, :, :], bank[6][:, None, 0:P].broadcast_to([P, XG, P]),
                             node_id[:, c * XG:(c + 1) * XG, None].broadcast_to([P, XG, P]), ALU.is_le))
        m = vrun(V.tensor_reduce(smt[:, 0, c * XG:(c + 1) * XG], cmpb[:, :, :], AXX, ALU.add))
    vrun(V.tensor_scalar(smt[:, 1, :], smt[:, 0, :], -1.0, 0.0, ALU.add, ALU.max))
    row_of = vrun(V.tensor_copy(idx_g[:, :], smt[:, 1, :]))
    half_up = dve.run(V.tensor_scalar(smt[:, 2, :], node_id[:, :], 0.5, None, ALU.add))

    found = []

    def search(t):
        pool.wait(dst_out, row_of)
        if t >= 2:
            pool.wait(found[t - 2])
        m = pool.sent(f"rows_in{t % 2}", G.indirect_dma_start(
            out=rows[:, t % 2, :], out_offset=None, in_=dst_d, in_offset=at_rows(idx_g[:, t:t + 1])))
        act.wait(m, half_up)
        found.append(act.run(S.activation(rows[:, t % 2, :].bitcast(F32), rows[:, t % 2, :], ACT.Sign,
                                          bias=smt[:, 2, t:t + 1], scale=-1.0, accum_out=smt[:, 3, t:t + 1])))

    def graph_ends():
        dve.wait(found[-1])
        vrun(V.tensor_scalar(smt[:, 3, :], smt[:, 3, :], float(C1), 0.5, ALU.add, ALU.mult))
        vrun(V.scalar_tensor_tensor(out=smt[:, 4, :], in0=smt[:, 1, :], scalar=float(C1), in1=smt[:, 3, :],
                                    op0=ALU.mult, op1=ALU.add))
        vrun(V.tensor_scalar(smt[:, 0, :], smt[:, 0, :], 0.5, None, ALU.is_gt))
        m = vrun(V.tensor_tensor(smt[:, 4, :], smt[:, 4, :], smt[:, 0, :], ALU.mult))
        pe.wait(m)
        pe.run(T.matmul(bank[6][:, 0:NT], shift1[:, :], smt[:, 4, :], start=True, stop=False))
        m = pe.run(T.matmul(bank[6][:, 1:NT], wrap1[:, :], smt[:, 4, 0:NT - 1], start=False, stop=True))
        dve.wait(m)
        vrun(V.tensor_tensor(has_g[:, :], smt[:, 4, :], bank[6][:, 0:NT], ALU.is_gt))
        vrun(V.tensor_scalar(smt[:, 4, :], smt[:, 4, :], -1.0, 0.0, ALU.add, ALU.max))
        return vrun(V.tensor_copy(idx_g[:, :], smt[:, 4, :]))

    places = []
    sort_state = {}

    def sort_steps():
        dve.wait(e_in)
        vrun(V.tensor_scalar(ed[:, :, 1], raw_e[:, 1, :], N, None, ALU.min))
        vrun(V.tensor_scalar(ed[:, :, 0], raw_e[:, 0, :], N - 1, None, ALU.min))
        yield
        vrun(V.tensor_single_scalar(place[:, :], ed[:, :, 1], P - 1, ALU.bitwise_and))
        vrun(V.tensor_copy(dl[:, :], place[:, :]))
        yield
        vrun(V.tensor_single_scalar(place[:, :], ed[:, :, 1], P.bit_length() - 1, ALU.logical_shift_right))
        vrun(V.tensor_copy(dh[:, :], place[:, :]))
        yield
        freed = {}

        def hot(b0, n, slot):
            for k in range(slot, slot + n // GB):
                dve.wait(*freed.get(k, ()))
            o = oh[:, slot:slot + n // GB, :, :].rearrange("p a b c -> p (a b) c")
            h = dhh[:, slot:slot + n // GB, :, :].rearrange("p a b c -> p (a b) c")
            dve.run(V.tensor_tensor(o, iota_b[:, None, :].broadcast_to([P, n, P]),
                                    dl[:, b0:b0 + n, None].broadcast_to([P, n, P]), ALU.is_equal))
            return dve.run(V.tensor_tensor(h, iota_b[:, None, 0:NT].broadcast_to([P, n, NT]),
                                           dh[:, b0:b0 + n, None].broadcast_to([P, n, NT]), ALU.is_equal))

        n = 2 * GB
        for i in range(C2 // n):
            slot = i % 2 * 2
            m = hot(i * n, n, slot)
            pe.wait(m)
            for k in range(n):
                m = pe.run(T.matmul(bank[5][:, 0:NT], oh[:, slot + k // GB, k % GB, :],
                                    dhh[:, slot + k // GB, k % GB, :],
                                    start=(i == 0 and k == 0), stop=(i == C2 // n - 1 and k == n - 1)))
            freed[slot] = freed[slot + 1] = (m,)
            yield
        dve.wait(m)
        m = vrun(V.tensor_copy(smt[:, 6, :], bank[5][:, 0:NT]))
        pe.wait(m)
        pe.run(T.matmul(bank[5][:, 64:64 + NT], before[:, :], smt[:, 6, :], start=True, stop=True))
        m = pe.run(T.matmul(bank[5][:, 128:128 + NT], ones[:, :], smt[:, 6, :], start=True, stop=True))
        dve.wait(m)
        yield
        vrun(V.tensor_copy(smt[:, 7, :], bank[5][:, 128:128 + NT]))
        vrun(V.tensor_tensor_scan(hinit[:, :], ones[:, 0:NT], smt[:, 7, :], 0.0, ALU.mult, ALU.add))
        vrun(V.tensor_tensor(hinit[:, :], hinit[:, :], smt[:, 7, :], ALU.subtract))
        vrun(V.tensor_tensor(hinit[:, :], hinit[:, :], bank[5][:, 64:64 + NT], ALU.add))
        yield
        vrun(V.tensor_scalar(has_f[:, :], smt[:, 6, :], 0.5, None, ALU.is_gt))
        vrun(V.tensor_scalar(smt[:, 7, :], has_f[:, :], -float(FAR), float(FAR), ALU.mult, ALU.add))
        vrun(V.tensor_tensor(idx_s[:, :], smt[:, 7, :], hinit[:, :], ALU.add))
        vrun(V.tensor_tensor(smt[:, 6, :], smt[:, 6, :], hinit[:, :], ALU.add))
        vrun(V.tensor_scalar(idx_f[:, :], smt[:, 6, :], -1.0, 0.0, ALU.add, ALU.max))
        yield

        turned, spread, counted, hsum, eqs, masked, looked, ends = {}, {}, {}, {}, {}, {}, {}, {}

        def prev_hist(i):
            return hinit[:, :] if i == 0 else hist[:, (i - 1) % 3, GB - 1, :]

        for i in range(NG + 2):
            if i < NG:
                freed_by = [looked[i - 4], ends[i - 4]] if i >= 4 else []
                freed[i % 4] = (*freed.get(i % 4, ()), *freed_by)
                hotted = hot(i * GB, GB, i % 4)
                yield
                pe.wait(hotted)
                if i >= 1:
                    pe.wait(spread[i - 1])
                if i >= 2:
                    pe.wait(hsum[i - 2])
                for k in range(GB):
                    m = pe.run(T.transpose(bank_t[:, k, :], oh[:, i % 4, k, :], ident_b[:, :]))
                turned[i] = m
                for k in range(GB):
                    for j in range(k + 1):
                        m = pe.run(T.matmul(bank[3 * (i % 2)][:, k * NT:(k + 1) * NT],
                                            oh[:, i % 4, j, :], dhh[:, i % 4, j, :],
                                            start=(j == 0), stop=(j == k)))
                counted[i] = m
                act.wait(turned[i])
                if i >= 3:
                    act.wait(looked[i - 3])
                spread[i] = act.run(S.activation(oht[:, i % 3, :, :], bank_t[:, :, :], ACT.Copy))
                pe.wait(spread[i])
                if i >= 2:
                    pe.wait(masked[i - 2])
                for k in range(GB):
                    m = pe.run(T.matmul(bank[1 + i % 2][:, k * P:(k + 1) * P], oht[:, i % 3, k, :],
                                        oht[:, i % 3, k, :], start=True, stop=True))
                eqs[i] = m
            if 1 <= i <= NG:
                n = i - 1
                dve.wait(eqs[n])
                if n >= 2:
                    dve.wait(looked[n - 2])
                masked[n] = dve.run(V.tensor_tensor(
                    eqm[:, n % 2, :, :], bank[1 + n % 2][:, :].rearrange("p (k e) -> p k e", k=GB),
                    before[:, None, :].broadcast_to([P, GB, P]), ALU.mult))
                yield
                dve.wait(counted[n])
                if n >= 1:
                    dve.wait(hsum[n - 1])
                if n >= 3:
                    dve.wait(looked[n - 3], looked[n - 2])
                hsum[n] = dve.run(V.tensor_tensor(
                    hist[:, n % 3, :, :],
                    bank[3 * (n % 2)][:, 0:GB * NT].rearrange("p (k t) -> p k t", k=GB),
                    prev_hist(n)[:, None, :].broadcast_to([P, GB, NT]), ALU.add))
                pe.wait(masked[n], hsum[n])
                if n >= 2:
                    pe.wait(ends[n - 2])
                for k in range(GB):
                    o = bank[4 + n % 2][:, k * NT:(k + 1) * NT]
                    so_far = prev_hist(n) if k == 0 else hist[:, n % 3, k - 1, :]
                    pe.run(T.matmul(o, oht[:, n % 3, k, :], so_far, start=True, stop=False))
                    m = pe.run(T.matmul(o, eqm[:, n % 2, k, :], dhh[:, n % 4, k, :], start=False, stop=True))
                looked[n] = m
                yield
            if i >= 2:
                n = i - 2
                dve.wait(looked[n])
                if n >= 1:
                    dve.wait(ends[n - 1])
                m = dve.run(V.tensor_tensor(
                    prod[:, :, :], bank[4 + n % 2][:, 0:GB * NT].rearrange("p (k t) -> p k t", k=GB),
                    dhh[:, n % 4, :, :], ALU.mult))
                yield
                dve.wait(m)
                with nc.allow_low_precision(reason="whole numbers under 2^24"):
                    ends[n] = dve.run(V.tensor_reduce(place[:, n * GB:(n + 1) * GB], prod[:, :, :], AXX, ALU.add))
                places.append(ends[n])
                yield

    sort = sort_steps()
    pool.wait(src_in, pad_e, *xn_out)
    summed, stored = {}, {}
    prev = None
    for c in range(NCH):
        s = c % RING
        if c >= RING:
            pool.wait(stored[c - RING], summed[c - RING + 1][0])
        for k in range(JC):
            j = c * JC + k
            got = pool.sent(f"gather{s}", G.indirect_dma_start(
                out=ring[:, s, k, :], out_offset=None, in_=xn_d, in_offset=at_rows(srci[:, j:j + 1])))
        if 2 <= c < 2 + NT:
            search(c - 2)
        marks_c = []
        for k in range(JC):
            j = c * JC + k
            dve.wait(got)
            if j > 0:
                dve.wait(prev[1])
                prev_row = prev[0]
                m = dve.run(V.scalar_tensor_tensor(out=ring[:, s, k, :], in0=prev_row, scalar=same_g[:, j:j + 1],
                                                   in1=ring[:, s, k, :], op0=ALU.mult, op1=ALU.add))
                prev = (ring[:, s, k, :], m)
            else:
                m = pad_e
                prev = (ring[:, s, k, :], m)
            marks_c.append(m)
            next(sort, None)
        summed[c] = (marks_c[0] if c else marks_c[1], marks_c[-1])
        sp.wait(summed[c][1])
        stored[c] = sp.dma(f"stored{s}", run_d.rearrange("(p j) d -> p j d", p=P)[:, c * JC:(c + 1) * JC, :],
                           ring[:, s, :, :])
        if c == 2 + NT:
            graph_at = graph_ends()
    for _ in sort:
        pass

    def row_ends(d_row, cols, scr, row0, head, last, nxt, pos_i, far_i, ready):
        dve.wait(*ready)
        vrun(V.tensor_scalar(scr, d_row, head, None, ALU.is_equal))
        vrun(V.tensor_reduce(sm[:, 8:9], scr, AXX, ALU.add))
        m = vrun(V.tensor_scalar(sm[:, 9:10], head, 1.0, None, ALU.add))
        pe.wait(m)
        m = pe.run(T.transpose(bank[6][:, 256:384], shift1[:, :], ident[:, :]))
        dve.wait(m)
        m = vrun(V.tensor_copy(tmask[:, :], bank[6][:, 256:384]))
        pe.wait(m)
        m = pe.run(T.matmul(bank[6][:, 400:401], tmask[:, :], sm[:, 9:10], start=True, stop=True))
        dve.wait(m)
        vrun(V.tensor_scalar(sm[:, 10:11], bank[6][:, 400:401], -1.0, None, ALU.add))
        vrun(V.tensor_tensor(sm[:, 11:12], head, last, ALU.is_equal))
        vrun(V.tensor_tensor(sm[:, 12:13], head, sm[:, 10:11], ALU.is_equal))
        vrun(V.tensor_tensor(sm[:, 11:12], sm[:, 11:12], sm[:, 12:13], ALU.mult))
        vrun(V.tensor_copy(sm[:, 13:14], row0))
        vrun(V.scalar_tensor_tensor(out=sm[:, 13:14], in0=sm[:, 8:9], scalar=-1.0, in1=sm[:, 13:14],
                                    op0=ALU.add, op1=ALU.add))
        vrun(V.scalar_tensor_tensor(out=sm[:, 14:15], in0=sm[:, 11:12], scalar=float(FAR), in1=sm[:, 13:14],
                                    op0=ALU.mult, op1=ALU.add))
        vrun(V.tensor_copy(pos_i, sm[:, 13:14]))
        return vrun(V.tensor_copy(far_i, sm[:, 14:15]))

    scr_g = rows[:, 0, :].bitcast(F32)
    fix_at = row_ends(dsti[:, :], C1, scr_g, row_at[:, 0:1], sm[:, 0:1], sm[:, 1:2], None,
                      smi[:, 0:1], smi[:, 1:2], (found[-1],))
    m = broadcast_cols(sm[:, 0:1], (), bank[6][:, 0:P])
    dve.wait(m)
    m = vrun(V.scalar_tensor_tensor(out=tmask[:, :], in0=bank[6][:, 0:P], scalar=sm[:, 1:2], in1=before[:, :],
                                    op0=ALU.is_equal, op1=ALU.mult))
    pe.wait(m, summed[NCH - 1][1])
    carried = pe.run(T.matmul(bank[5][:, 0:D], tmask[:, :], prev[0], start=True, stop=True))
    pool.wait(fix_at, *(stored[c] for c in range(NCH - RING, NCH)))
    m = pool.sent("fix_in", G.indirect_dma_start(out=cfix[:, :], out_offset=None, in_=run_d,
                                                 in_offset=at_rows(smi[:, 0:1])))
    dve.wait(m, carried)
    m = vrun(V.tensor_tensor(cfix[:, :], cfix[:, :], bank[5][:, 0:D], ALU.add))
    pool.wait(m)
    run_fixed = pool.sent("fix_out", G.indirect_dma_start(
        out=run_d, out_offset=at_rows(smi[:, 1:2]), in_=cfix[:, :], in_offset=None,
        bounds_check=P * C1 - 1, oob_is_err=False))

    sp.wait(got, ("dve_done", dve.n), found[-1], dst_out)
    for e in range(NX):
        sp.dma("w12_in", w1s[:, e, :, :], W1[e].rearrange("(k p) f -> p k f", p=P))
        w12_in = sp.dma("w12_in", w2s[:, e, :, :], W2[e].rearrange("(f p) n -> p f n", p=P))
    pool.wait(run_fixed, graph_at)
    r3_free = [places[-1], ("pe_done", pe.n), ("act_done", act.n)]
    agg_used, xno_used, tin_used, out_used, x2_used, xt_out, feat_at = {}, {}, {}, {}, {}, {}, {}
    x1_out = {}

    def ready_tile(t):
        s = t % 4
        if t < 4:
            pool.wait(*r3_free)
            sp.wait(*r3_free)
        else:
            pool.wait(agg_used[t - 4])
            sp.wait(xno_used[t - 4])
        a = pool.sent(f"agg_in{s}", G.indirect_dma_start(out=agg[:, s, :], out_offset=None, in_=run_d,
                                                         in_offset=at_rows(idx_g[:, t:t + 1])))
        b = sp.dma(f"xno_in{s}", xno[:, s, :], xn_d[t * P:(t + 1) * P, :])
        return a, b

    ahead = {t: ready_tile(t) for t in range(2)}
    act.wait(*r3_free)
    pe.wait(*r3_free, w_in)
    chunk_first = {}
    for t in range(NT):
        s, c, w = t % 4, t // 4, t % 4
        if t + 2 < NT:
            ahead[t + 2] = ready_tile(t + 2)
        a, b = ahead.pop(t)
        dve.wait(a)
        masked_agg = vrun(V.tensor_scalar(agg[:, s, :], agg[:, s, :], has_g[:, t:t + 1], None, ALU.mult))
        pe.wait(masked_agg, b)
        tb = bank[t % 2]
        if t >= 2:
            pe.wait(tin_used[t - 2])
        for k in range(KD):
            pe.run(T.transpose(tb[:, k * P:(k + 1) * P], xno[:, s, k * P:(k + 1) * P], ident[:, :]))
        for k in range(KD):
            m = pe.run(T.transpose(tb[:, (KD + k) * P:(KD + k + 1) * P], agg[:, s, k * P:(k + 1) * P], ident[:, :]))
        xno_used[t] = agg_used[t] = m
        act.wait(m)
        if t >= 2:
            act.wait(out_used[t - 2])
        tin_used[t] = act.run(S.activation(tin[:, t % 2, :, :], tb[:, :].rearrange("p (k n) -> p k n", k=4), ACT.Copy))
        pe.wait(tin_used[t])
        o = bank[2 + t % 2][:, 0:D]
        if t >= 2:
            pe.wait(x2_used[t - 2])
        for k in range(KD):
            pe.run(T.matmul(o, tin[:, t % 2, k, :], wself[:, k, :], start=(k == 0), stop=False))
        for k in range(KD):
            out_used[t] = pe.run(T.matmul(o, tin[:, t % 2, KD + k, :], wmsg[:, k, :], start=False, stop=(k == KD - 1)))
        dve.wait(out_used[t])
        x1m = vrun(V.scalar_tensor_tensor(out=xs[:, t, :], in0=o, scalar=0.0, in1=xs[:, t, :],
                                          op0=ALU.max, op1=ALU.add))
        x2_used[t] = x1m
        sp.wait(x1m)
        x1_out[t] = sp.dma("x1_out", x1_d[t * P:(t + 1) * P, :], xs[:, t, :])
        vrun(V.bn_stats(stat[:, t % 2, :], xs[:, t, :]))
        vrun(V.bn_aggr(aggr[:, t, :], stat[:, t % 2, :]))
        m = norm_scalars(0, stat, aggr[:, t:t + 1, :])
        act.wait(m)
        act.wait(xno_used[t])
        m = act.run(S.activation(xno[:, s, :], xs[:, t, :], ACT.Identity, bias=aggr[:, t, 0:1],
                                 scale=aggr[:, t, 1:2]))
        pe.wait(m)
        if t >= 1:
            pe.wait(chunk_first[t - 1])
        for k in range(KD):
            m = pe.run(T.transpose(bank[4][:, k * P:(k + 1) * P], xno[:, s, k * P:(k + 1) * P], ident[:, :]))
        xno_used[t] = m
        act.wait(m)
        if w == 0 and c >= 2:
            act.wait(xt_out[c - 2])
        m = act.run(S.activation(xt[:, c % 2, :, w * P:(w + 1) * P],
                                 bank[4][:, 0:KD * P].rearrange("p (k n) -> p k n", k=KD), ACT.Copy))
        chunk_first[t] = m
        pe.wait(m)
        if t >= 1:
            pe.wait(feat_at[t - 1])
        for k in range(KD):
            m = pe.run(T.matmul(bank[5][:, 0:HX], xt[:, c % 2, k, w * P:(w + 1) * P], wgat[:, k, :],
                                start=(k == 0), stop=(k == KD - 1)))
        if w == 3 or t == NT - 1:
            sp.wait(chunk_first[t])
            xt_out[c] = sp.dma(f"xt_out{c % 2}", xT_d[:, :, c * 4 * P:c * 4 * P + (w + 1) * P],
                               xt[:, c % 2, :, 0:(w + 1) * P])
            xt_out[c] = (xt_out[c])
            last_h = m
        dve.wait(m)
        feat_at[t] = vrun(V.tensor_copy(feat[:, t, 0:HX], bank[5][:, 0:HX]))
        for k in range(2):
            vrun(V.tensor_tensor(sm[:, 16 + 16 * k:32 + 16 * k], feat[:, t, 0:HX], attb[:, k, :], ALU.mult))
            m = vrun(V.tensor_reduce(feat[:, t, HX + HEADS * k:HX + HEADS * (k + 1)],
                                     sm[:, 16 + 16 * k:32 + 16 * k].rearrange("p (h e) -> p h e", h=HEADS),
                                     AXX, ALU.add))
        feat_done = m
    sp.wait(feat_done)
    tab_out = sp.dma("tab_out", tab_d.rearrange("(t p) f -> p t f", p=P), feat[:, :, 0:FE])
    agg_all = a

    for b in range(C2):
        pool.wait(places[b // GB])
        permuted = pool.sent("permute", G.indirect_dma_start(
            out=sorted_d, out_offset=at_rows(place[:, b:b + 1]), in_=ed[:, b, :], in_offset=None))
    sp.wait(permuted)
    srt_in = sp.dma("srt_in", srt[:, :, :], sorted_d.rearrange("(p j) c -> p j c", p=P))

    def expert_steps():
        chunks = [(c * 4, min(4, NT - c * 4)) for c in range(-(-NT // 4))]
        jobs = [(c, e) for c in range(len(chunks)) for e in range(NX)]
        loaded, activated, projected, y_used, y_out, l1_used = {}, {}, {}, {}, {}, {}
        sp.wait(("pe_done", pe.n), *(xt_out[c] for c in range(len(chunks))))
        pe.wait(("dve_done", dve.n), ("act_done", act.n), w12_in)
        act.wait(("pe_done", pe.n))
        ny = 0
        nl = 0

        def load(c):
            t0, n = chunks[c]
            if c >= 2:
                sp.wait(projected[(c - 2, "l1")])
            loaded[c] = sp.dma(f"xt_in{c % 2}", xt[:, c % 2, :, 0:n * P], xT_d[:, :, t0 * P:(t0 + n) * P])

        load(0)
        load(1)
        for i in range(len(jobs) + 1):
            if i < len(jobs):
                c, e = jobs[i]
                t0, n = chunks[c]
                if e == 0 and 1 <= c and c + 1 < len(chunks):
                    load(c + 1)
                pe.wait(loaded[c])
                if i >= 2:
                    act.wait(projected[i - 2])
                for f in range(KF):
                    if nl >= 2:
                        pe.wait(l1_used[nl - 2])
                    o = bank[nl % 2][:, 0:n * P]
                    for k in range(KD):
                        m = pe.run(T.matmul(o, w1s[:, e, k, f * P:(f + 1) * P], xt[:, c % 2, k, 0:n * P],
                                            start=(k == 0), stop=(k == KD - 1)))
                    act.wait(m)
                    l1_used[nl] = act.run(S.activation(hh[:, i % 2, f, 0:n * P], o, ACT.Gelu,
                                                       bias=b1c[:, e, f:f + 1], scale=1.0))
                    nl += 1
                activated[i] = l1_used[nl - 1]
                if e == NX - 1:
                    projected[(c, "l1")] = m
            if i >= 1:
                c, e = jobs[i - 1]
                t0, n = chunks[c]
                pe.wait(activated[i - 1])
                for k in range(n):
                    if ny >= 2:
                        pe.wait(y_used[ny - 2])
                    o = bank[2 + ny % 2][:, 0:D]
                    for f in range(KF):
                        m = pe.run(T.matmul(o, hh[:, (i - 1) % 2, f, k * P:(k + 1) * P], w2s[:, e, f, :],
                                            start=(f == 0), stop=(f == KF - 1)))
                    dve.wait(m)
                    if ny >= 4:
                        dve.wait(y_out[ny - 4])
                    y_used[ny] = dve.run(V.tensor_tensor(yo[:, ny % 4, :], o, b2b[:, e, :], ALU.add))
                    sp.wait(y_used[ny])
                    y_out[ny] = sp.dma(f"y_out{ny % 4}", y_d[e, (t0 + k) * P:(t0 + k + 1) * P, :], yo[:, ny % 4, :])
                    ny += 1
                    yield
                projected[i - 1] = m
        sort_state["y_out"] = [y_out[ny - 1 - k] for k in range(4)]

    experts = expert_steps()
    for _ in range(120):
        next(experts, None)

    dve.wait(srt_in)
    dve.run(V.memset(same_f[:, 0:1], 0.0))
    vrun(V.tensor_tensor(same_f[:, 1:C2], srt[:, 1:C2, 1], srt[:, 0:C2 - 1, 1], ALU.is_equal))
    vrun(V.tensor_scalar(reset_f[:, :], same_f[:, :], -1.0, BIG, ALU.add, ALU.mult))
    pool.wait(srt_in, tab_out, x1_out[NT - 1], agg_all)
    FC = 64
    zero_start = None
    prev_m = None
    for c in range(C2 // FC):
        for j in range(c * FC, (c + 1) * FC):
            got = pool.sent(f"feat_in{c % 8}", G.indirect_dma_start(
                out=g[:, j, :], out_offset=None, in_=tab_d, in_offset=at_rows(srt[:, j, 0:1])))
        dve.wait(got)
        a, b = c * FC, (c + 1) * FC
        if prev_m:
            dve.wait(prev_m)
        for h in range(HEADS):
            prev_m = dve.run(V.tensor_tensor_scan(
                runmax[:, a:b, h], reset_f[:, a:b], g[:, a:b, HX + h],
                -BIG if c == 0 else runmax[:, a - 1:a, h], ALU.add, ALU.max))
        for _ in range(6):
            next(experts, None)
    for _ in experts:
        pass

    vrun(V.tensor_copy(sm[:, 0:1], srt[:, 0:1, 1]))
    vrun(V.tensor_copy(sm[:, 1:2], srt[:, C2 - 1:C2, 1]))
    mlp_done = [("pe_done", pe.n), ("act_done", act.n), *sort_state["y_out"]]
    dve.wait(*mlp_done)
    fix_f = row_ends(srt[:, :, 1], C2, edge_n[:, :, 0], row_at[:, 1:2], sm[:, 0:1], sm[:, 1:2], None,
                     smi[:, 2:3], smi[:, 3:4], ())
    pe.wait(("dve_done", dve.n))
    m = broadcast_cols(sm[:, 1:2], (), bank[0][:, 0:P])
    dve.wait(m)
    sel = vrun(V.scalar_tensor_tensor(out=cfix[:, 0:P], in0=bank[0][:, 0:P], scalar=sm[:, 0:1], in1=after[:, :],
                                      op0=ALU.is_equal, op1=ALU.mult))
    vrun(V.tensor_scalar(cfix[:, P:2 * P], cfix[:, 0:P], -1.0, BIG, ALU.add, ALU.mult))
    for h in range(HEADS):
        m = broadcast_cols(runmax[:, C2 - 1, h:h + 1], (("dve_done", dve.n),), bank[0][:, 0:P])
        dve.wait(m)
        vrun(V.tensor_tensor(edge_n[:, 0:P, 0], bank[0][:, 0:P], cfix[:, 0:P], ALU.mult))
        vrun(V.tensor_tensor(edge_n[:, 0:P, 0], edge_n[:, 0:P, 0], cfix[:, P:2 * P], ALU.add))
        vrun(V.tensor_reduce(sm[:, 20 + h:21 + h], edge_n[:, 0:P, 0], AXX, ALU.max))
    sp.wait(prev_m)
    m = sp.dma("max_out", max_d.rearrange("(p j) h -> p (j h)", p=P), runmax[:, :, :].rearrange("p j h -> p (j h)"))
    pool.wait(m, fix_f)
    m = pool.sent("fix_in", G.indirect_dma_start(out=sm[:, 24:28], out_offset=None, in_=max_d,
                                                 in_offset=at_rows(smi[:, 2:3])))
    dve.wait(m)
    m = vrun(V.tensor_tensor(sm[:, 24:28], sm[:, 24:28], sm[:, 20:24], ALU.max))
    pool.wait(m)
    m = pool.sent("fix_out", G.indirect_dma_start(
        out=max_d, out_offset=at_rows(smi[:, 3:4]), in_=sm[:, 24:28], in_offset=None,
        bounds_check=E2 - 1, oob_is_err=False))
    pool.wait(m)

    nmax = fin[:, 0, :, 0:HEADS]
    dve.wait(*mlp_done)
    pool.wait(*mlp_done, ("dve_done", dve.n))
    fmax = fin[:, 9, :, 0:HEADS]
    for t in range(NT):
        m = pool.sent("node_in", G.indirect_dma_start(out=fin[:, 9, t, 0:HEADS], out_offset=None, in_=max_d,
                                                      in_offset=at_rows(idx_f[:, t:t + 1])))
    dve.wait(m)
    has3 = has_f[:, :, None].broadcast_to([P, NT, HEADS])
    a_s, a_d = feat[:, :, HX:FE], feat[:, :, FE:FE + HEADS]
    vrun(V.tensor_scalar(fin[:, 1, :, 0:1], has_f[:, :, None], -1.0, BIG, ALU.add, ALU.mult))
    vrun(V.tensor_tensor(fin[:, 2, :, 0:HEADS], fmax, has3, ALU.mult))
    vrun(V.tensor_tensor(fin[:, 2, :, 0:HEADS], fin[:, 2, :, 0:HEADS],
                         fin[:, 1, :, 0:1].broadcast_to([P, NT, HEADS]), ALU.add))
    vrun(V.tensor_tensor(nmax, fin[:, 2, :, 0:HEADS], a_s, ALU.max))
    vrun(V.tensor_tensor(nmax, nmax, a_d, ALU.add))
    vrun(V.scalar_tensor_tensor(out=nmax, in0=nmax, scalar=0.2, in1=nmax, op0=ALU.mult, op1=ALU.max))
    vrun(V.tensor_copy(fin[:, 3, :, 0:HEADS], a_d))
    m = vrun(V.tensor_copy(fin[:, 3, :, HEADS:2 * HEADS], nmax))
    sp.wait(m)
    node_out = sp.dma("node_out", node_d.rearrange("(t p) f -> p t f", p=P), fin[:, 3, :, 0:2 * HEADS])
    z = vrun(V.memset(edge_n[:, :, :], 0.0))
    sp.wait(z)
    m = sp.dma("zero_out", start_d.rearrange("(p j) f -> p (j f)", p=P), edge_n[:, :, :].rearrange("p j f -> p (j f)"))
    pool.wait(m, z)
    for t in range(NT):
        m = pool.sent("start_out", G.indirect_dma_start(
            out=start_d, out_offset=at_rows(idx_s[:, t:t + 1]), in_=fin[:, 3, t, 0:2 * HEADS], in_offset=None,
            bounds_check=E2 - 1, oob_is_err=False))
    sp.wait(m)
    m = sp.dma("edge_in", edge_n[:, :, :].rearrange("p j f -> p (j f)"), start_d.rearrange("(p j) f -> p (j f)", p=P))
    pool.wait(node_out, m)
    m = vrun(V.tensor_copy(smi[:, 4:5], srt[:, 0:1, 1]))
    pool.wait(m)
    m = pool.sent("fix_in", G.indirect_dma_start(out=edge_n[:, 0, :], out_offset=None, in_=node_d,
                                                 in_offset=at_rows(smi[:, 4:5])))
    dve.wait(m)
    for f in range(2 * HEADS):
        m = dve.run(V.tensor_tensor_scan(edge_n[:, :, f], same_f[:, :], edge_n[:, :, f], 0.0, ALU.mult, ALU.add))
    dve.wait(m)

    ea, en, ex = g[:, :, HX:FE], edge_n[:, :, 0:HEADS], edge_n[:, :, HEADS:2 * HEADS]
    vrun(V.tensor_tensor(ea, ea, en, ALU.add))
    vrun(V.scalar_tensor_tensor(out=ea, in0=ea, scalar=0.2, in1=ea, op0=ALU.mult, op1=ALU.max))
    m = vrun(V.tensor_tensor(ea, ea, ex, ALU.subtract))
    act.wait(m)
    m = act.run(S.activation(ea, ea, ACT.Exp))
    dve.wait(m)
    for h in range(HEADS):
        o = g[:, :, h * NX:(h + 1) * NX]
        m = dve.run(V.tensor_tensor(o, o, g[:, :, HX + h:HX + h + 1].broadcast_to([P, C2, NX]), ALU.mult))
    dve.wait(m)
    for f in range(FE):
        m = dve.run(V.tensor_tensor_scan(g[:, :, f], same_f[:, :], g[:, :, f], 0.0, ALU.mult, ALU.add))
    dve.wait(m)
    sp.wait(m)
    m_sum = sp.dma("sum_out", sum_d.rearrange("(p j) f -> p (j f)", p=P), g[:, :, :].rearrange("p j f -> p (j f)"))
    m = broadcast_cols(sm[:, 0:1], (), bank[0][:, 0:P])
    dve.wait(m)
    m = vrun(V.scalar_tensor_tensor(out=tmask[:, :], in0=bank[0][:, 0:P], scalar=sm[:, 1:2], in1=before[:, :],
                                    op0=ALU.is_equal, op1=ALU.mult))
    pe.wait(m)
    carried = pe.run(T.matmul(bank[1][:, 0:FE], tmask[:, :], g[:, C2 - 1, :], start=True, stop=True))
    pool.wait(m_sum)
    m = pool.sent("fix_in", G.indirect_dma_start(out=sm[:, 32:32 + FE], out_offset=None, in_=sum_d,
                                                 in_offset=at_rows(smi[:, 2:3])))
    dve.wait(m, carried)
    m = vrun(V.tensor_tensor(sm[:, 32:32 + FE], sm[:, 32:32 + FE], bank[1][:, 0:FE], ALU.add))
    pool.wait(m)
    m = pool.sent("fix_out", G.indirect_dma_start(
        out=sum_d, out_offset=at_rows(smi[:, 3:4]), in_=sm[:, 32:32 + FE], in_offset=None,
        bounds_check=E2 - 1, oob_is_err=False))
    pool.wait(m)
    for t in range(NT):
        m = pool.sent("node_in", G.indirect_dma_start(out=fsum[:, t, :], out_offset=None, in_=sum_d,
                                                      in_offset=at_rows(idx_f[:, t:t + 1])))
    dve.wait(m)

    f_ = lambda i: fin[:, i, :, :]
    f4 = lambda i: fin[:, i, :, 0:HEADS]
    full = [P, NT, HX]
    vrun(V.tensor_tensor(fsum[:, :, :], fsum[:, :, :], has_f[:, :, None].broadcast_to([P, NT, FE]), ALU.mult))
    vrun(V.tensor_tensor(f4(4), a_s, a_d, ALU.add))
    vrun(V.scalar_tensor_tensor(out=f4(4), in0=f4(4), scalar=0.2, in1=f4(4), op0=ALU.mult, op1=ALU.max))
    m = vrun(V.tensor_tensor(f4(4), f4(4), nmax, ALU.subtract))
    act.wait(m)
    m = act.run(S.activation(f4(4), f4(4), ACT.Exp))
    dve.wait(m)
    per_head = lambda ap: ap[:, :, :, None].broadcast_to([P, NT, HEADS, NX])
    h4 = lambda ap: ap.rearrange("p t (h e) -> p t h e", h=HEADS)

    def heads_times(o, a, b):
        for h in range(HEADS):
            m = dve.run(V.tensor_tensor(o[:, :, h * NX:(h + 1) * NX], a[:, :, h * NX:(h + 1) * NX],
                                        b[:, :, h:h + 1].broadcast_to([P, NT, NX]), ALU.mult))
        dve.wait(m)

    heads_times(f_(5), feat[:, :, 0:HX], f4(4))
    vrun(V.tensor_tensor(f_(5), f_(5), fsum[:, :, 0:HX], ALU.add))
    vrun(V.tensor_tensor(f4(6), f4(4), fsum[:, :, HX:FE], ALU.add))
    vrun(V.tensor_scalar(f4(6), f4(6), 1e-16, None, ALU.add))
    vrun(V.reciprocal(f4(6), f4(6)))
    heads_times(f_(5), f_(5), f4(6))
    vrun(V.tensor_tensor(f_(5), f_(5), gln[:, 0:1, :].broadcast_to(full), ALU.add))
    one = lambda i: fin[:, i, :, 0:1]
    vrun(V.tensor_reduce(fin[:, 6, :, 0], f_(5), AXX, ALU.add))
    vrun(V.tensor_scalar(one(6), one(6), 1.0 / HX, None, ALU.mult))
    vrun(V.tensor_tensor(f_(5), f_(5), one(6).broadcast_to(full), ALU.subtract))
    vrun(V.tensor_tensor(f_(7), f_(5), f_(5), ALU.mult))
    vrun(V.tensor_reduce(fin[:, 6, :, 1], f_(7), AXX, ALU.add))
    vrun(V.tensor_scalar(fin[:, 6, :, 1:2], fin[:, 6, :, 1:2], 1.0 / HX, EPS, ALU.mult, ALU.add))
    act.wait(("dve_done", dve.n))
    m = act.run(S.activation(fin[:, 6, :, 1:2], fin[:, 6, :, 1:2], ACT.Sqrt))
    dve.wait(m)
    vrun(V.reciprocal(fin[:, 6, :, 1:2], fin[:, 6, :, 1:2]))
    vrun(V.tensor_tensor(f_(5), f_(5), fin[:, 6, :, 1:2].broadcast_to(full), ALU.mult))
    vrun(V.tensor_tensor(f_(5), f_(5), gln[:, 1:2, :].broadcast_to(full), ALU.mult))
    vrun(V.tensor_tensor(f_(5), f_(5), gln[:, 2:3, :].broadcast_to(full), ALU.add))
    sc = fin[:, 7, :, 0:NX]
    vrun(V.tensor_tensor(sc, fin[:, 5, :, 0:NX], fin[:, 5, :, NX:2 * NX], ALU.add))
    for h in range(2, HEADS):
        vrun(V.tensor_tensor(sc, sc, fin[:, 5, :, h * NX:(h + 1) * NX], ALU.add))
    vrun(V.tensor_scalar(sc, sc, 1.0 / HEADS, None, ALU.mult))
    vrun(V.memset(fin[:, 8, :, 0:NX], 0.0))
    for e in range(NX):
        for o in range(NX):
            if o == e:
                continue
            vrun(V.tensor_tensor(one(6), fin[:, 7, :, o:o + 1], fin[:, 7, :, e:e + 1],
                                 ALU.is_ge if o < e else ALU.is_gt))
            vrun(V.tensor_tensor(fin[:, 8, :, e:e + 1], fin[:, 8, :, e:e + 1], one(6), ALU.add))
    vrun(V.tensor_scalar(fin[:, 8, :, 0:NX], fin[:, 8, :, 0:NX], 1.5, None, ALU.is_lt))
    vrun(V.tensor_reduce(fin[:, 6, :, 0], sc, AXX, ALU.max))
    m = vrun(V.tensor_tensor(sc, sc, one(6).broadcast_to([P, NT, NX]), ALU.subtract))
    act.wait(m)
    m = act.run(S.activation(sc, sc, ACT.Exp))
    dve.wait(m)
    vrun(V.tensor_tensor(sc, sc, fin[:, 8, :, 0:NX], ALU.mult))
    vrun(V.tensor_reduce(fin[:, 6, :, 0], sc, AXX, ALU.add))
    vrun(V.reciprocal(one(6), one(6)))
    gates = vrun(V.tensor_tensor(sc, sc, one(6).broadcast_to([P, NT, NX]), ALU.mult))

    sp.wait(("pe_done", pe.n), gates, m_sum, ("dve_done", dve.n), x1_out[NT - 1], *sort_state["y_out"])
    act.wait(("pe_done", pe.n), gates, m_sum)
    CT = XG
    outs, loaded = {}, {}

    def load_comb(c):
        s = c % 2
        if c >= 2:
            sp.wait(outs[c - 2])
        rows_ = slice(c * CT * P, (c + 1) * CT * P)
        for e in range(NX):
            sp.dma(f"comb_in{s}", comb[:, s, e, :, :], y_d[e, rows_, :].rearrange("(t p) d -> p t d", p=P))
        loaded[c] = sp.dma(f"comb_in{s}", comb[:, s, NX, :, :], x1_d[rows_, :].rearrange("(t p) d -> p t d", p=P))

    load_comb(0)
    for c in range(NT // CT):
        if c + 1 < NT // CT:
            load_comb(c + 1)
        s = c % 2
        dve.wait(loaded[c])
        for e in range(NX):
            for k in range(CT):
                t = c * CT + k
                m = dve.run(V.scalar_tensor_tensor(
                    out=comb[:, s, NX, k, :], in0=comb[:, s, e, k, :], scalar=fin[:, 7, t, e:e + 1],
                    in1=comb[:, s, NX, k, :], op0=ALU.mult, op1=ALU.add))
            dve.wait(m)
        act.wait(m)
        n = min(CT, FULL // P - c * CT)
        outs[c] = act.dma(f"out{s}", out[c * CT * P:(c * CT + n) * P, :].rearrange("(t p) d -> p t d", p=P),
                          comb[:, s, NX, 0:n, :])
        if n < CT:
            outs[c] = act.dma(f"out{s}", out[FULL:N, :], comb[0:N - FULL, s, NX, n, :])
    for lane in sorted(Queue.lanes):
        act.wait((lane, Queue.lanes[lane]))


_INS = ["x", "src", "dst", "L0_gnn_W", "L0_gnn_M", "L0_ffn_W_gat", "L0_ffn_att_src", "L0_ffn_att_dst",
        "L0_ffn_b_gat", "L0_ffn_ln_gamma", "L0_ffn_ln_beta", "L0_ffn_W1", "L0_ffn_b1", "L0_ffn_W2",
        "L0_ffn_b2", "L0_ffn_edge_index"]


def kernel(**inputs):
    import numpy as np
    import concourse.bacc as bacc
    from concourse.bass_utils import run_bass_kernel_spmd

    nc = bacc.Bacc("TRN2", target_bir_lowering=False, num_devices=1)
    arrays, args = {}, []
    for name in _INS:
        a = np.ascontiguousarray(inputs[name])
        arrays[f"in_{name}"] = a
        args.append(nc.dram_tensor(f"in_{name}", a.shape, mybir.dt.from_np(a.dtype), kind="ExternalInput").ap())
    args.append(nc.dram_tensor("out_x", inputs["x"].shape, F32, kind="ExternalOutput").ap())
    build(nc, *args)
    r = run_bass_kernel_spmd(nc, [arrays], core_ids=[0])
    return r.results[0]["out_x"]
```

```python
import concourse.bass as bass
from concourse import mybir

F32 = mybir.dt.float32
BF16 = mybir.dt.bfloat16
F16 = mybir.dt.float16
I16 = mybir.dt.int16
I32 = mybir.dt.int32
ALU = mybir.AluOpType
ACT = mybir.ActivationFunctionType
AXX = mybir.AxisListType.X

P = 128
EPS = 1e-5
BIG = 1.0e30
FAR = 1 << 21
RING = 4
JC = 8
GB = 4
PB = 32
MR = 5
DR = 6
HEADS = 4


class Marks:

    def __init__(self, nc):
        self.nc, self.sems = nc, {}

    def sem(self, name):
        if name not in self.sems:
            self.sems[name] = self.nc.alloc_semaphore(name)
        return self.sems[name]


class Queue:

    lanes = None

    def __init__(self, marks, eng, name):
        self.m, self.eng, self.name, self.n, self.passed = marks, eng, name, 0, {}

    def wait(self, *marks):
        for name, value in marks:
            if self.passed.get(name, 0) < value:
                self.eng.wait_ge(self.m.sem(name), value)
                self.passed[name] = value

    def run(self, ins):
        ins.then_inc(self.m.sem(self.name), 1)
        self.n += 1
        return (self.name, self.n)

    def sent(self, lane, ins):
        ins.then_inc(self.m.sem(lane), 16)
        self.lanes[lane] = self.lanes.get(lane, 0) + 16
        return (lane, self.lanes[lane])

    def dma(self, lane, out, in_):
        return self.sent(lane, self.eng.dma_start(out, in_))


def build(nc, x, src, dst, W, M, W_gat, att_src, att_dst, b_gat, ln_gamma, ln_beta,
          W1, b1, W2, b2, edge_index, out):
    N, D = x.shape
    E1, E2 = src.shape[0], edge_index.shape[1]
    NX, _, F = W1.shape
    HX = HEADS * NX
    KD, KF = D // P, F // P
    NT = -(-N // P)
    NPAD = NT * P
    C1 = -(-E1 // P)
    C1 = -(-C1 // JC) * JC
    C2 = E2 // P
    NCH = C1 // JC
    NG = C2 // GB
    XG = 7
    FE = HX + HEADS
    FG = FE + HEADS
    FS = 2 * HEADS + 1
    FULL = (N // P) * P
    assert NT % XG == 0 and E2 % P == 0 and C2 % (2 * GB) == 0 and N < NPAD and D == 256

    def dram(name, shape, dt):
        return nc.dram_tensor(name, shape, dt).ap()

    xn_d = dram("xn_d", [NPAD, D], F32)
    run_d = dram("run_d", [P * C1 + 1, D], F32)
    run_rows = run_d[0:P * C1, :].rearrange("(p j) d -> p j d", p=P)
    dst_d = dram("dst_d", [P, C1], I32)
    tab_d = dram("tab_d", [NPAD, FE], F32)
    x1_d = dram("x1_d", [NPAD, D], F32)
    xT_d = dram("xT_d", [P, KD, NPAD], F32)
    y_d = dram("y_d", [NX, NPAD, D], F32)
    node_d = dram("node_d", [NPAD, 2 * HEADS], F32)
    start_d = dram("start_d", [E2, FS], F32)
    sum_d = dram("sum_d", [E2, FG], F32)

    base = -(-nc.sbuf_base // 64) * 64
    top = nc.sbuf_base + nc.sbuf_bytes_remaining

    class Region:
        def __init__(self, at):
            self.at = at

        def take(self, name, shape, dt):
            n = 1
            for s in shape[1:]:
                n *= s
            size = -(-n * mybir.dt.size(dt) // 32) * 32
            t = nc.alloc_sbuf_tensor_at(name, shape, dt, offset=self.at)
            self.at += size
            assert self.at <= top, (name, self.at, top)
            return t

    r = Region(base)
    iota_i = r.take("iota_i", [P, P], I32)
    iota_b = r.take("iota_b", [P, P], BF16)
    ident = r.take("ident", [P, P], F32)
    ident_b = r.take("ident_b", [P, P], BF16)
    ones = r.take("ones", [P, P], F32)
    before = r.take("before", [P, P], F32)
    not_before = r.take("not_before", [P, P], BF16)
    shift1 = r.take("shift1", [P, P], F32)
    up1 = r.take("up1", [P, P], F32)
    wrap1 = r.take("wrap1", [P, P], F32)
    node_id = r.take("node_id", [P, NT], F32)
    node_ii = r.take("node_ii", [P, NT], I32)
    row_at = r.take("row_at", [P, 2], I32)
    idx_g = r.take("idx_g", [P, NT], I32)
    idx_f = r.take("idx_f", [P, NT], I32)
    idx_s = r.take("idx_s", [P, NT], I32)
    has_f = r.take("has_f", [P, NT], F32)
    sm = r.take("sm", [P, 96], F32)
    smi = r.take("smi", [P, 16], I32)
    smt = r.take("smt", [P, 8, NT], F32)
    feat = r.take("feat", [P, NT, FG + 1], F32)
    attb = r.take("attb", [P, 2, HX], F32)
    gln = r.take("gln", [P, 3, HX], F32)
    wgat = r.take("wgat", [P, KD, HX], F32)
    b1c = r.take("b1c", [P, NX, KF], F32)
    b2b = r.take("b2b", [P, NX, D], F32)
    tmask = r.take("tmask", [P, P], F32)
    cfix = r.take("cfix", [P, D], F32)
    stat = r.take("stat", [P, XG, 6], F32)
    aggr = r.take("aggr", [P, NT, 2], F32)
    r4 = r.at
    dlneg = r.take("dlneg", [P, C2], F32)
    dh = r.take("dh", [P, C2], BF16)
    code = r.take("code", [P, C2], F32)
    place = r.take("place", [P, C2], I32)
    q = Region(r4)
    same_f = q.take("same_f", [P, C2], F32)
    reset_f = q.take("reset_f", [P, C2 + 1], F32)
    assert q.at <= r.at
    srt = r.take("srt", [P, C2], I32)
    r2 = r.at
    w1s = r.take("w1s", [P, NX, KD, F], F32)
    w2s = r.take("w2s", [P, NX, KF, D], F32)
    q = Region(r2)
    dsti = q.take("dsti", [P, C1], I32)
    srci = q.take("srci", [P, C1], I32)
    same_g = q.take("same_g", [P, C1], F32)
    rows = q.take("rows", [P, 2, C1], I32)
    assert q.at <= r.at
    r3 = r.at
    hh = r.take("hh", [P, 2, KF, 4 * P], F32)
    xt = r.take("xt", [P, 2, KD, 4 * P], F32)
    yo = r.take("yo", [P, 4, D], F32)
    agg = r.take("agg", [P, 4, D], F32)
    xno = r.take("xno", [P, 4, D], F32)
    tin = r.take("tin", [P, 2, 4, P], F32)
    x2 = r.take("x2", [P, 2, D], F32)
    q = Region(r3)
    raw_e = q.take("raw_e", [P, 2, C2], I32)
    q = Region(r3)
    oh = q.take("oh", [P, DR, GB, P], BF16)
    dhh = q.take("dhh", [P, DR, GB, NT], BF16)
    dsq = q.take("dsq", [P, 2, 2 * GB, P], BF16)
    oht = q.take("oht", [P, 4, GB, P], F32)
    ohtb = q.take("ohtb", [P, 2, GB, P], BF16)
    eqm = q.take("eqm", [P, 3, GB, P], BF16)
    hist = q.take("hist", [P, 4, GB, NT], F32)
    prod = q.take("prod", [P, GB, NT], F32)
    hinit = q.take("hinit", [P, NT], F32)
    iota_h = q.take("iota_h", [P, C2], F16)
    row_hot = q.take("row_hot", [P, MR, P], F16)
    rc_i = q.take("rc_i", [P, 2, PB], I32)
    rc = q.take("rc", [P, 2, 2, PB], F32)
    cmpb = q.take("cmpb", [P, XG, P], F32)
    zeros = q.take("zeros", [P, C2], F32)
    assert q.at <= r.at, (q.at, r.at)
    q = Region(r2)
    edge_n = q.take("edge_n", [P, C2, FS], F32)
    id_run = q.take("id_run", [P, C2], F32)
    segm = q.take("segm", [P, 4, P], F32)
    hm = q.take("hm", [P, 3, HEADS, P], F32)
    first_f = q.take("first_f", [P, C2], F32)
    last_f = q.take("last_f", [P, C2], F32)
    fsum = q.take("fsum", [P, NT, FG], F32)
    q2 = Region(r2)
    fin = q2.take("fin", [P, 9, NT, HX], F32)
    assert q2.at <= q.at - 4 * NT * FG and q.at <= r.at, (q.at, r.at)
    r1 = r.at
    g = r.take("g", [P, C2, FG], F32)
    q = Region(r1)
    xs = q.take("xs", [P, NT, D], F32)
    ring = q.take("ring", [P, RING, JC, D], F32)
    wself = q.take("wself", [P, KD, D], F32)
    wmsg = q.take("wmsg", [P, KD, D], F32)
    col_hot = q.take("col_hot", [P, MR, C2], F16)
    assert q.at <= r.at
    q = Region(r1)
    comb = q.take("comb", [P, 2, NX + 1, XG, D], F32)
    assert q.at <= r.at

    bank = [nc.alloc_psum_tensor(f"bank{i}", [P, 512], F32) for i in range(7)]
    bank_t = nc.alloc_psum_tensor("bank_t", [P, GB, P], BF16)

    marks = Marks(nc)
    Queue.lanes = {}
    pe, dve, act, pool, sp = (Queue(marks, e, n) for e, n in (
        (nc.tensor, "pe_done"), (nc.vector, "dve_done"), (nc.scalar, "act_done"),
        (nc.gpsimd, "pool_done"), (nc.sync, "sp_done")))
    V, S, T, G = nc.vector, nc.scalar, nc.tensor, nc.gpsimd

    def vrun(ins, *_):
        m = dve.run(ins)
        dve.wait(m)
        return m

    def at_rows(ap):
        return bass.IndirectOffsetOnAxis(ap=ap, axis=0)

    pool.run(G.iota(iota_i[:, :], pattern=[[1, P]], base=0, channel_multiplier=0))
    pool.run(G.iota(node_ii[:, :], pattern=[[P, NT]], base=0, channel_multiplier=1))
    pool.run(G.iota(row_at[:, 0:1], pattern=[[0, 1]], base=0, channel_multiplier=C1))
    pool.run(G.iota(row_at[:, 1:2], pattern=[[0, 1]], base=0, channel_multiplier=C2))
    for t in (ident, shift1, up1, wrap1):
        pool.run(G.memset(t[:, :], 0.0))
    m = pool.run(G.memset(ones[:, :], 1.0))
    pool.wait(m)
    pool.run(G.affine_select(out=ident[:, :], in_=ident[:, :], compare_op=ALU.not_equal, fill=1.0, base=0,
                             pattern=[[-1, P]], channel_multiplier=1))
    pool.run(G.affine_select(out=shift1[:, :], in_=shift1[:, :], compare_op=ALU.not_equal, fill=1.0, base=1,
                             pattern=[[-1, P]], channel_multiplier=1))
    pool.run(G.affine_select(out=wrap1[:, :], in_=wrap1[:, :], compare_op=ALU.not_equal, fill=1.0,
                             base=-(P - 1), pattern=[[P, P]], channel_multiplier=1))
    pool.run(G.affine_select(out=up1[:, :], in_=up1[:, :], compare_op=ALU.not_equal, fill=1.0, base=-1,
                             pattern=[[-1, P]], channel_multiplier=1))
    consts = pool.run(G.affine_select(out=before[:, :], in_=ones[:, :], compare_op=ALU.is_gt, fill=0.0, base=0,
                                      pattern=[[1, P]], channel_multiplier=-1))

    pad_x = dve.run(V.memset(xs[:, NT - 1, :], 0.0))
    dve.run(V.memset(dsti[:, :], N))
    pad_e = dve.run(V.memset(srci[:, :], 0))
    sp.wait(pad_x)
    x_in = []
    for c in range(NT // XG):
        t0, t1 = c * XG, min((c + 1) * XG, FULL // P)
        m = sp.dma(f"x_in{c}", xs[:, t0:t1, :], x[t0 * P:t1 * P, :].rearrange("(t p) d -> p t d", p=P))
        if c == NT // XG - 1:
            m = sp.dma(f"x_in{c}", xs[0:N - FULL, NT - 1, :], x[FULL:N, :])
        x_in.append(m)
    act.wait(pad_e)
    fullrows = E1 // C1
    cut = fullrows // 16 * 16
    for a, t in ((dst, dsti), (src, srci)):
        lane = "dst_in" if a is dst else "src_in"
        full = a[0:fullrows * C1].rearrange("(p j) -> p j", j=C1)
        act.dma(lane, t[0:cut, :], full[0:cut, :])
        act.dma(lane, t[cut:fullrows, :], full[cut:fullrows, :])
        act.dma(lane, t[fullrows:fullrows + 1, 0:E1 - fullrows * C1],
                a[fullrows * C1:E1].rearrange("(a j) -> a j", a=1))
    dst_in, src_in = ("dst_in", 48), ("src_in", 48)
    for c in range(2):
        e_in = act.dma("e_in", raw_e[:, c, :], edge_index[c, :].rearrange("(p j) -> p j", j=C2))
    act.wait(dst_in)
    dst_out = act.dma("dst_out", dst_d, dsti[:, :])
    act.dma("w_in", wself[:, :, :], W.rearrange("(k p) n -> p k n", p=P))
    act.dma("w_in", wmsg[:, :, :], M.rearrange("(k p) n -> p k n", p=P))
    act.dma("w_in", wgat[:, :, :], W_gat.rearrange("(k p) n -> p k n", p=P))
    for k, a in enumerate((att_src, att_dst)):
        act.dma("w_in", attb[:, k, :], a.rearrange("h e -> (h e)").partition_broadcast(P))
    for k, a in enumerate((b_gat, ln_gamma, ln_beta)):
        act.dma("w_in", gln[:, k, :], a.partition_broadcast(P))
    with nc.allow_non_contiguous_dma(reason="b1 by column, 8 KB once"):
        act.dma("w_in", b1c[:, :, :], b1.rearrange("e (f p) -> p e f", p=P))
    for e in range(NX):
        w_in = act.dma("w_in", b2b[:, e, :], b2[e, :].partition_broadcast(P))

    def norm_scalars(c, stats, aggr):
        m = vrun(V.tensor_scalar(aggr[:, :, 1], aggr[:, :, 1], EPS, None, ALU.add))
        act.wait(m)
        m = act.run(S.activation(aggr[:, :, 1], aggr[:, :, 1], ACT.Sqrt))
        dve.wait(m)
        vrun(V.reciprocal(aggr[:, :, 1], aggr[:, :, 1]))
        return dve.run(V.scalar_tensor_tensor(out=aggr[:, :, 0], in0=aggr[:, :, 0], scalar=-1.0,
                                              in1=aggr[:, :, 1], op0=ALU.mult, op1=ALU.mult))

    xn_out = []
    for c in range(NT // XG):
        dve.wait(x_in[c])
        for k in range(XG):
            m = dve.run(V.bn_stats(stat[:, k, :], xs[:, c * XG + k, :]))
        dve.wait(m)
        for k in range(XG):
            m = dve.run(V.bn_aggr(aggr[:, c * XG + k, :], stat[:, k, :]))
        dve.wait(m)
        m = norm_scalars(c, stat, aggr[:, c * XG:(c + 1) * XG, :])
        act.wait(m)
        if c >= RING:
            act.wait(xn_out[c - RING])
        for k in range(XG):
            t = c * XG + k
            m = act.run(S.activation(ring[:, c % RING, k, :], xs[:, t, :], ACT.Identity,
                                     bias=aggr[:, t, 0:1], scale=aggr[:, t, 1:2]))
        sp.wait(m)
        xn_out.append(sp.dma(f"xn_out{c % RING}",
                             xn_d[c * XG * P:(c + 1) * XG * P, :].rearrange("(t p) d -> p t d", p=P),
                             ring[:, c % RING, 0:XG, :]))

    dve.wait(consts, dst_in)
    dve.run(V.tensor_copy(iota_b[:, :], iota_i[:, :]))
    dve.run(V.tensor_copy(node_id[:, :], node_ii[:, :]))
    dve.run(V.tensor_copy(ident_b[:, :], ident[:, :]))
    dve.run(V.tensor_scalar(not_before[:, :], before[:, :], -1.0, None, ALU.add))
    dve.run(V.tensor_scalar(feat[:, :, FG], node_ii[:, :], 1, None, ALU.add))
    dve.run(V.memset(same_g[:, 0:1], 0.0))
    vrun(V.tensor_tensor(same_g[:, 1:C1], dsti[:, 1:C1], dsti[:, 0:C1 - 1], ALU.is_equal))

    def broadcast_cols(col, free, bank_out, m_free=None):
        m = vrun(V.tensor_scalar(tmask[:, :], ident[:, :], col, None, ALU.mult))
        pe.wait(m, *free)
        return pe.run(T.matmul(bank_out, ones[:, :], tmask[:, :], start=True, stop=True))

    vrun(V.tensor_copy(sm[:, 0:1], dsti[:, 0:1]))
    vrun(V.tensor_copy(sm[:, 1:2], dsti[:, C1 - 1:C1]))
    m_rowheads = broadcast_cols(sm[:, 0:1], (), bank[6][:, 0:P])
    dve.wait(m_rowheads)
    for c in range(NT // XG):
        vrun(V.tensor_tensor(cmpb[:, :, :], bank[6][:, None, 0:P].broadcast_to([P, XG, P]),
                             node_id[:, c * XG:(c + 1) * XG, None].broadcast_to([P, XG, P]), ALU.is_le))
        m = vrun(V.tensor_reduce(smt[:, 0, c * XG:(c + 1) * XG], cmpb[:, :, :], AXX, ALU.add))
    vrun(V.tensor_scalar(smt[:, 1, :], smt[:, 0, :], -1.0, 0.0, ALU.add, ALU.max))
    row_of = vrun(V.tensor_copy(idx_g[:, :], smt[:, 1, :]))
    half_up = dve.run(V.tensor_scalar(smt[:, 2, :], node_id[:, :], 0.5, None, ALU.add))

    found = []

    def search(t):
        pool.wait(dst_out, row_of)
        if t >= 2:
            pool.wait(found[t - 2])
        m = pool.sent(f"rows_in{t % 2}", G.indirect_dma_start(
            out=rows[:, t % 2, :], out_offset=None, in_=dst_d, in_offset=at_rows(idx_g[:, t:t + 1])))
        act.wait(m, half_up)
        found.append(act.run(S.activation(rows[:, t % 2, :].bitcast(F32), rows[:, t % 2, :], ACT.Sign,
                                          bias=smt[:, 2, t:t + 1], scale=-1.0, accum_out=smt[:, 3, t:t + 1])))

    def graph_ends():
        dve.wait(found[-1])
        vrun(V.tensor_scalar(smt[:, 3, :], smt[:, 3, :], float(C1), 0.5, ALU.add, ALU.mult))
        vrun(V.scalar_tensor_tensor(out=smt[:, 4, :], in0=smt[:, 1, :], scalar=float(C1), in1=smt[:, 3, :],
                                    op0=ALU.mult, op1=ALU.add))
        vrun(V.tensor_scalar(smt[:, 0, :], smt[:, 0, :], 0.5, None, ALU.is_gt))
        m = vrun(V.tensor_tensor(smt[:, 4, :], smt[:, 4, :], smt[:, 0, :], ALU.mult))
        pe.wait(m)
        pe.run(T.matmul(bank[6][:, 0:NT], shift1[:, :], smt[:, 4, :], start=True, stop=False))
        m = pe.run(T.matmul(bank[6][:, 1:NT], wrap1[:, :], smt[:, 4, 0:NT - 1], start=False, stop=True))
        dve.wait(m)
        vrun(V.tensor_tensor(smt[:, 5, :], smt[:, 4, :], bank[6][:, 0:NT], ALU.is_gt))
        vrun(V.tensor_scalar(smt[:, 4, :], smt[:, 4, :], -1.0 - P * C1, None, ALU.add))
        vrun(V.tensor_tensor(smt[:, 4, :], smt[:, 4, :], smt[:, 5, :], ALU.mult))
        vrun(V.tensor_scalar(smt[:, 4, :], smt[:, 4, :], float(P * C1), None, ALU.add))
        return vrun(V.tensor_copy(idx_g[:, :], smt[:, 4, :]))

    made = {}

    def sort_steps():
        dve.wait(e_in)
        dst_c, src_c = raw_e[:, 1, :], raw_e[:, 0, :]
        vrun(V.tensor_scalar(dst_c, dst_c, N, None, ALU.min))
        vrun(V.tensor_scalar(src_c, src_c, N - 1, 1024, ALU.min, ALU.add))
        bits = place[:, 0:C2 // 2].bitcast(I16)
        vrun(V.tensor_copy(bits, src_c))
        vrun(V.tensor_copy(code[:, :], bits.bitcast(F16)))
        vrun(V.tensor_single_scalar(place[:, :], dst_c, P.bit_length() - 1, ALU.logical_shift_right))
        vrun(V.tensor_copy(dh[:, :], place[:, :]))
        vrun(V.tensor_single_scalar(place[:, :], dst_c, P - 1, ALU.bitwise_and))
        low = vrun(V.tensor_scalar(dlneg[:, :], place[:, :], -1, None, ALU.mult))
        pool.wait(low)
        m = pool.run(G.iota(raw_e[:, 0, :], pattern=[[1, C2]], base=0, channel_multiplier=0))
        dve.wait(m)
        vrun(V.tensor_copy(iota_h[:, :], raw_e[:, 0, :]))
        z = vrun(V.memset(zeros[:, :], 0.0))
        sp.wait(z)
        flat = start_d.rearrange("(p a) f -> p (a f)", p=P)
        for k in range(FS):
            sp.dma("zero_out", flat[:, k * C2:(k + 1) * C2], zeros[:, :])
        made["zero_out"] = sp.dma("zero_out", run_d[P * C1:P * C1 + 1, :], zeros[0:1, 0:D])
        yield
        freed, squared = {}, {}
        act.wait(low, consts, ("dve_done", dve.n))
        turn = [0]

        def hot(b0, n, slot, on_act):
            q = dve if not on_act else act
            for k in range(slot, slot + n // GB):
                dve.wait(*freed.get(k, ()))
                q.wait(*freed.get(k, ()))
            o = oh[:, slot:slot + n // GB, :, :].rearrange("p a b c -> p (a b) c")
            h = dhh[:, slot:slot + n // GB, :, :].rearrange("p a b c -> p (a b) c")
            if on_act:
                w = turn[0] % 2
                turn[0] += 1
                act.wait(squared.get(w, low))
                for k in range(n):
                    m = act.run(S.activation(dsq[:, w, k, :], iota_b[:, :], ACT.Square,
                                             bias=dlneg[:, b0 + k:b0 + k + 1], scale=1.0))
                act.wait(m)
                squared[w] = m1 = act.run(S.activation(o, dsq[:, w, 0:n, :], ACT.Relu, bias=ones[:, 0:1], scale=-1.0))
            else:
                for k in range(n):
                    m1 = dve.run(V.tensor_scalar(o[:, k, :], iota_b[:, :], dlneg[:, b0 + k:b0 + k + 1], 0.0,
                                                 ALU.add, ALU.is_equal))
            m2 = dve.run(V.tensor_tensor(h, iota_b[:, None, 0:NT].broadcast_to([P, n, NT]),
                                         dh[:, b0:b0 + n, None].broadcast_to([P, n, NT]), ALU.is_equal))
            return m1, m2

        n = 2 * GB
        for i in range(C2 // n):
            slot = i % 2 * 2
            pe.wait(*hot(i * n, n, slot, i % 2 == 0))
            for k in range(n):
                m = pe.run(T.matmul(bank[5][:, 0:NT], oh[:, slot + k // GB, k % GB, :],
                                    dhh[:, slot + k // GB, k % GB, :],
                                    start=(i == 0 and k == 0), stop=(i == C2 // n - 1 and k == n - 1)))
            freed[slot] = freed[slot + 1] = (m,)
            yield
        dve.wait(m)
        m = vrun(V.tensor_copy(smt[:, 6, :], bank[5][:, 0:NT]))
        pe.wait(m)
        pe.run(T.matmul(bank[5][:, 64:64 + NT], before[:, :], smt[:, 6, :], start=True, stop=True))
        m = pe.run(T.matmul(bank[5][:, 128:128 + NT], ones[:, :], smt[:, 6, :], start=True, stop=True))
        dve.wait(m)
        vrun(V.tensor_copy(smt[:, 7, :], bank[5][:, 128:128 + NT]))
        vrun(V.tensor_tensor_scan(hinit[:, :], ones[:, 0:NT], smt[:, 7, :], 0.0, ALU.mult, ALU.add))
        vrun(V.tensor_tensor(hinit[:, :], hinit[:, :], smt[:, 7, :], ALU.subtract))
        first_place = vrun(V.tensor_tensor(hinit[:, :], hinit[:, :], bank[5][:, 64:64 + NT], ALU.add))
        yield
        made["counted"] = True
        vrun(V.tensor_scalar(has_f[:, :], smt[:, 6, :], 0.5, None, ALU.is_gt))
        vrun(V.tensor_scalar(smt[:, 7, :], has_f[:, :], -float(FAR), float(FAR), ALU.mult, ALU.add))
        vrun(V.tensor_tensor(idx_s[:, :], smt[:, 7, :], hinit[:, :], ALU.add))
        vrun(V.tensor_tensor(smt[:, 6, :], smt[:, 6, :], hinit[:, :], ALU.add))
        vrun(V.tensor_scalar(idx_f[:, :], smt[:, 6, :], -1.0, 0.0, ALU.add, ALU.max))
        yield

        turned, spread, counted, hsum, eqs, masked, looked, ends = {}, {}, {}, {}, {}, {}, {}, {}
        moved, rc_used = {}, {}
        pe.wait(first_place)

        def prev_hist(i):
            return hinit[:, :] if i == 0 else hist[:, (i - 1) % 4, GB - 1, :]

        def move(b0):
            w = b0 // PB % 2
            dve.wait(ends[(b0 + PB) // GB - 1], *rc_used.get(w, ()))
            at = place[:, b0:b0 + PB]
            vrun(V.tensor_single_scalar(rc_i[:, 0, :], at, C2.bit_length() - 1, ALU.logical_shift_right))
            vrun(V.tensor_single_scalar(rc_i[:, 1, :], at, C2 - 1, ALU.bitwise_and))
            vrun(V.tensor_copy(rc[:, w, :, :], rc_i[:, :, :]))
            yield
            for k in range(PB):
                b = b0 + k
                if b >= MR:
                    dve.wait(moved[b - MR])
                dve.run(V.tensor_scalar(row_hot[:, b % MR, :], iota_h[:, 0:P], rc[:, w, 0, k:k + 1],
                                        code[:, b:b + 1], ALU.is_equal, ALU.mult))
                m = dve.run(V.tensor_scalar(col_hot[:, b % MR, :], iota_h[:, :], rc[:, w, 1, k:k + 1], None,
                                            ALU.is_equal))
                pe.wait(m)
                for half, bk in ((0, bank[0]), (1, bank[5])):
                    m2 = pe.run(T.matmul(bk[:, :], row_hot[:, b % MR, :],
                                         col_hot[:, b % MR, half * 512:(half + 1) * 512],
                                         start=(b == 0), stop=(b == C2 - 1)))
                moved[b] = m2
                yield
            rc_used[w] = (m,)

        movers = []

        def move_some(count):
            while movers and count:
                try:
                    next(movers[0])
                    count -= 1
                    yield
                except StopIteration:
                    movers.pop(0)

        def hot_rows(i):
            if i >= DR:
                freed[i % DR] = (looked[i - DR], ends[i - DR])
            made["hot", i] = hot(i * GB, GB, i % DR, True)

        def turn_blocks(i):
            pe.wait(*made["hot", i])
            if i >= 1:
                pe.wait(*spread[i - 1])
            for k in range(GB):
                m = pe.run(T.transpose(bank_t[:, k, :], oh[:, i % DR, k, :], ident_b[:, :]))
            turned[i] = m
            if i >= 1:
                pe.wait(hsum[i - 1])
            for k in range(GB):
                for j in range(k + 1):
                    m = pe.run(T.matmul(bank[3][:, k * NT:(k + 1) * NT], oh[:, i % DR, j, :],
                                        dhh[:, i % DR, j, :], start=(j == 0), stop=(j == k)))
            counted[i] = m
            act.wait(turned[i])
            if i >= 2:
                act.wait(eqs[i - 2])
            if i >= 4:
                act.wait(looked[i - 4])
            spread[i] = (act.run(S.activation(ohtb[:, i % 2, :, :], bank_t[:, :, :], ACT.Copy)),
                         act.run(S.activation(oht[:, i % 4, :, :], bank_t[:, :, :], ACT.Copy)))

        def compare(i):
            pe.wait(spread[i][0])
            if i >= 2:
                pe.wait(masked[i - 2])
            for k in range(GB):
                o = bank[1 + i % 2][:, k * P:(k + 1) * P]
                pe.run(T.matmul(o, ohtb[:, i % 2, k, :], ohtb[:, i % 2, k, :], start=True, stop=False))
                m = pe.run(T.matmul(o, ident_b[:, :], not_before[:, :], start=False, stop=True))
            eqs[i] = m
            act.wait(eqs[i])
            if i >= 3:
                act.wait(looked[i - 3])
            masked[i] = act.run(S.activation(eqm[:, i % 3, :, :],
                                             bank[1 + i % 2][:, :].rearrange("p (k e) -> p k e", k=GB), ACT.Relu))

        def add_counts(i):
            dve.wait(counted[i])
            if i >= 1:
                dve.wait(hsum[i - 1])
            if i >= 3:
                dve.wait(looked[i - 3])
            if i >= 4:
                dve.wait(looked[i - 4])
            hsum[i] = dve.run(V.tensor_tensor(
                hist[:, i % 4, :, :], bank[3][:, 0:GB * NT].rearrange("p (k t) -> p k t", k=GB),
                prev_hist(i)[:, None, :].broadcast_to([P, GB, NT]), ALU.add))

        def look_up(n):
            pe.wait(masked[n], hsum[n])
            if n >= 1:
                pe.wait(made["prod", n - 1])
            for k in range(GB):
                o = bank[4][:, k * NT:(k + 1) * NT]
                so_far = prev_hist(n) if k == 0 else hist[:, n % 4, k - 1, :]
                pe.run(T.matmul(o, oht[:, n % 4, k, :], so_far, start=True, stop=False))
                m = pe.run(T.matmul(o, eqm[:, n % 3, k, :], dhh[:, n % DR, k, :], start=False, stop=True))
            looked[n] = m

        for i in range(NG + 4):
            if i < NG:
                hot_rows(i)
            yield
            if i >= 4:
                n = i - 4
                dve.wait(looked[n])
                if n >= 1:
                    dve.wait(ends[n - 1])
                made["prod", n] = dve.run(V.tensor_tensor(
                    prod[:, :, :], bank[4][:, 0:GB * NT].rearrange("p (k t) -> p k t", k=GB),
                    dhh[:, n % DR, :, :], ALU.mult))
            if 3 <= i < NG + 3:
                look_up(i - 3)
            if 1 <= i <= NG:
                turn_blocks(i - 1)
            if 2 <= i < NG + 2:
                compare(i - 2)
            yield from move_some(2)
            if 1 <= i <= NG:
                add_counts(i - 1)
            if i >= 4:
                dve.wait(made["prod", n])
                with nc.allow_low_precision(reason="whole numbers under 2^24"):
                    ends[n] = dve.run(V.tensor_reduce(place[:, n * GB:(n + 1) * GB], prod[:, :, :], AXX, ALU.add))
                if (n + 1) * GB % PB == 0:
                    movers.append(move((n + 1) * GB - PB))
            yield from move_some(2)
        yield from move_some(-1)
        dve.wait(moved[C2 - 1])
        half_bits = place[:, 0:C2 // 2].bitcast(F16)
        vrun(V.tensor_copy(half_bits[:, 0:512], bank[0][:, :]))
        vrun(V.tensor_copy(half_bits[:, 512:1024], bank[5][:, :]))
        made["sorted"] = vrun(V.tensor_scalar(srt[:, :], half_bits.bitcast(I16), -1024, None, ALU.add))

    sort = sort_steps()
    pool.wait(src_in, pad_e, *xn_out)
    summed, stored = {}, {}
    prev = None
    paced = 0
    for c in range(NCH):
        s = c % RING
        if c >= RING:
            pool.wait(stored[c - RING], summed[c - RING + 1][0])
        for k in range(JC):
            j = c * JC + k
            got = pool.sent(f"gather{s}", G.indirect_dma_start(
                out=ring[:, s, k, :], out_offset=None, in_=xn_d, in_offset=at_rows(srci[:, j:j + 1])))
        if 2 <= c < 2 + NT:
            search(c - 2)
        marks_c = []
        for k in range(JC):
            j = c * JC + k
            dve.wait(got)
            if j > 0:
                dve.wait(prev[1])
                prev_row = prev[0]
                m = dve.run(V.scalar_tensor_tensor(out=ring[:, s, k, :], in0=prev_row, scalar=same_g[:, j:j + 1],
                                                   in1=ring[:, s, k, :], op0=ALU.mult, op1=ALU.add))
                prev = (ring[:, s, k, :], m)
            else:
                m = pad_e
                prev = (ring[:, s, k, :], m)
            marks_c.append(m)
            paced += 0.55 if not made.get("counted") else 1.25
            while paced >= 1:
                next(sort, None)
                paced -= 1
        summed[c] = (marks_c[0] if c else marks_c[1], marks_c[-1])
        sp.wait(summed[c][1])
        stored[c] = sp.dma(f"stored{s}", run_rows[:, c * JC:(c + 1) * JC, :],
                           ring[:, s, :, :])
        if c == 2 + NT:
            graph_at = graph_ends()
    def row_ends(count, row0, head, last, pos_i, far_i):
        m = vrun(V.tensor_scalar(sm[:, 9:10], head, 1.0, None, ALU.add))
        pe.wait(m)
        m = pe.run(T.matmul(bank[6][:, 400:401], up1[:, :], sm[:, 9:10], start=True, stop=True))
        dve.wait(m)
        vrun(V.tensor_scalar(sm[:, 10:11], bank[6][:, 400:401], -1.0, None, ALU.add))
        vrun(V.tensor_tensor(sm[:, 11:12], head, last, ALU.is_equal))
        vrun(V.tensor_tensor(sm[:, 12:13], head, sm[:, 10:11], ALU.is_equal))
        vrun(V.tensor_tensor(sm[:, 11:12], sm[:, 11:12], sm[:, 12:13], ALU.mult))
        vrun(V.tensor_copy(sm[:, 13:14], row0))
        vrun(V.scalar_tensor_tensor(out=sm[:, 13:14], in0=count, scalar=-1.0, in1=sm[:, 13:14],
                                    op0=ALU.add, op1=ALU.add))
        vrun(V.scalar_tensor_tensor(out=sm[:, 14:15], in0=sm[:, 11:12], scalar=float(FAR), in1=sm[:, 13:14],
                                    op0=ALU.mult, op1=ALU.add))
        vrun(V.tensor_copy(pos_i, sm[:, 13:14]))
        return vrun(V.tensor_copy(far_i, sm[:, 14:15]))

    dve.wait(found[-1])
    vrun(V.tensor_scalar(rows[:, 0, :].bitcast(F32), dsti[:, :], sm[:, 0:1], None, ALU.is_equal))
    vrun(V.tensor_reduce(sm[:, 8:9], rows[:, 0, :].bitcast(F32), AXX, ALU.add))
    fix_at = row_ends(sm[:, 8:9], row_at[:, 0:1], sm[:, 0:1], sm[:, 1:2], smi[:, 0:1], smi[:, 1:2])
    m = broadcast_cols(sm[:, 0:1], (), bank[6][:, 0:P])
    dve.wait(m)
    m = vrun(V.scalar_tensor_tensor(out=tmask[:, :], in0=bank[6][:, 0:P], scalar=sm[:, 1:2], in1=before[:, :],
                                    op0=ALU.is_equal, op1=ALU.mult))
    pe.wait(m, summed[NCH - 1][1])
    carried = pe.run(T.matmul(bank[6][:, 0:D], tmask[:, :], prev[0], start=True, stop=True))
    pool.wait(fix_at, *(stored[c] for c in range(NCH - RING, NCH)))
    m = pool.sent("fix_in", G.indirect_dma_start(out=cfix[:, :], out_offset=None, in_=run_d,
                                                 in_offset=at_rows(smi[:, 0:1])))
    dve.wait(m, carried)
    m = vrun(V.tensor_tensor(cfix[:, :], cfix[:, :], bank[6][:, 0:D], ALU.add))
    pool.wait(m)
    run_fixed = pool.sent("fix_out", G.indirect_dma_start(
        out=run_d[0:P * C1 + 1, :], out_offset=at_rows(smi[:, 1:2]), in_=cfix[:, :], in_offset=None,
        bounds_check=P * C1 - 1, oob_is_err=False))

    sp.wait(got, ("dve_done", dve.n), found[-1], dst_out)
    for e in range(NX):
        sp.dma("w12_in", w1s[:, e, :, :], W1[e].rearrange("(k p) f -> p k f", p=P))
        w12_in = sp.dma("w12_in", w2s[:, e, :, :], W2[e].rearrange("(f p) n -> p f n", p=P))
    for _ in sort:
        pass
    pool.wait(run_fixed, graph_at, made["zero_out"])
    r3_free = [("dve_done", dve.n), ("pe_done", pe.n), ("act_done", act.n), made["zero_out"]]
    for e in (pool, sp, act, pe, dve):
        e.wait(*(m for m in r3_free if m[0] != e.name))
    agg_in, xno_in, turned_in, tin_at, out_at, x1_at, x1_out = {}, {}, {}, {}, {}, {}, {}
    scaled, x2_at, x2_turned, xt_at, h_at, xt_out, feat_at = {}, {}, {}, {}, {}, {}, {}
    chunk_of = lambda t: t // 4
    last_of = lambda c: min(4 * c + 3, NT - 1)

    def fetch(t):
        if t >= 4:
            pool.wait(turned_in[t - 4])
            sp.wait(turned_in[t - 4])
        agg_in[t] = pool.sent(f"agg_in{t % 4}", G.indirect_dma_start(
            out=agg[:, t % 4, :], out_offset=None, in_=run_d, in_offset=at_rows(idx_g[:, t:t + 1])))
        xno_in[t] = sp.dma(f"xno_in{t % 4}", xno[:, t % 4, :], xn_d[t * P:(t + 1) * P, :])

    def turn_rows(t):
        pe.wait(agg_in[t], xno_in[t])
        if t >= 2:
            pe.wait(tin_at[t - 2])
        tb = bank[t % 2]
        for k in range(KD):
            pe.run(T.transpose(tb[:, k * P:(k + 1) * P], xno[:, t % 4, k * P:(k + 1) * P], ident[:, :]))
        for k in range(KD):
            m = pe.run(T.transpose(tb[:, (KD + k) * P:(KD + k + 1) * P], agg[:, t % 4, k * P:(k + 1) * P], ident[:, :]))
        turned_in[t] = m
        act.wait(m)
        if t >= 2:
            act.wait(out_at[t - 2])
        tin_at[t] = act.run(S.activation(tin[:, t % 2, :, :], tb[:, :].rearrange("p (k n) -> p k n", k=4), ACT.Copy))

    def layer(t):
        pe.wait(tin_at[t])
        if t >= 2:
            pe.wait(x1_at[t - 2])
        o = bank[2 + t % 2][:, 0:D]
        for k in range(KD):
            pe.run(T.matmul(o, tin[:, t % 2, k, :], wself[:, k, :], start=(k == 0), stop=False))
        for k in range(KD):
            m = pe.run(T.matmul(o, tin[:, t % 2, KD + k, :], wmsg[:, k, :], start=False, stop=(k == KD - 1)))
        out_at[t] = m
        dve.wait(m)
        x1_at[t] = vrun(V.scalar_tensor_tensor(out=xs[:, t, :], in0=o, scalar=0.0, in1=xs[:, t, :],
                                               op0=ALU.max, op1=ALU.add))
        sp.wait(x1_at[t])
        x1_out[t] = sp.dma("x1_out", x1_d[t * P:(t + 1) * P, :], xs[:, t, :])
        vrun(V.bn_stats(stat[:, t % 4, :], xs[:, t, :]))
        m = dve.run(V.bn_aggr(aggr[:, t, :], stat[:, t % 4, :]))
        if t == last_of(chunk_of(t)):
            dve.wait(m)
            scaled[chunk_of(t)] = norm_scalars(0, stat, aggr[:, 4 * chunk_of(t):t + 1, :])

    def norm(t):
        c, w = chunk_of(t), t % 4
        act.wait(scaled[c])
        if t >= 2:
            act.wait(x2_turned[t - 2])
        x2_at[t] = act.run(S.activation(x2[:, t % 2, :], xs[:, t, :], ACT.Identity, bias=aggr[:, t, 0:1],
                                        scale=aggr[:, t, 1:2]))
        pe.wait(x2_at[t])
        if t >= 1:
            pe.wait(xt_at[t - 1])
        for k in range(KD):
            m = pe.run(T.transpose(bank[4][:, k * P:(k + 1) * P], x2[:, t % 2, k * P:(k + 1) * P], ident[:, :]))
        x2_turned[t] = m
        act.wait(m)
        if w == 0 and c >= 2:
            act.wait(xt_out[c - 2], h_at[last_of(c - 2)])
        xt_at[t] = act.run(S.activation(xt[:, c % 2, :, w * P:(w + 1) * P],
                                        bank[4][:, 0:KD * P].rearrange("p (k n) -> p k n", k=KD), ACT.Copy))

    def heads(t):
        c, w = chunk_of(t), t % 4
        pe.wait(xt_at[t])
        hb = bank[5 + c % 2]
        if w == 0 and c >= 2:
            pe.wait(feat_at[c - 2])
        for k in range(KD):
            m = pe.run(T.matmul(hb[:, w * HX:(w + 1) * HX], xt[:, c % 2, k, w * P:(w + 1) * P], wgat[:, k, :],
                                start=(k == 0), stop=(k == KD - 1)))
        h_at[t] = m
        if t == last_of(c):
            sp.wait(xt_at[t])
            xt_out[c] = sp.dma(f"xt_out{c % 2}", xT_d[:, :, c * 4 * P:c * 4 * P + (w + 1) * P],
                               xt[:, c % 2, :, 0:(w + 1) * P])
            n = w + 1
            dve.wait(m)
            fc = feat[:, 4 * c:4 * c + n, :]
            feat_at[c] = vrun(V.tensor_copy(fc[:, :, 0:HX], hb[:, 0:n * HX].rearrange("p (t f) -> p t f", t=n)))
            scr = [cfix[:, 64 * k:64 * k + n * HX].rearrange("p (t f) -> p t f", t=n) for k in range(2)]
            for k in range(2):
                m = dve.run(V.tensor_tensor(scr[k], fc[:, :, 0:HX], attb[:, k:k + 1, :].broadcast_to([P, n, HX]), ALU.mult))
            dve.wait(m)
            for k in range(2):
                m = dve.run(V.tensor_reduce(fc[:, :, HX + HEADS * k:HX + HEADS * (k + 1)],
                                            scr[k].rearrange("p t (h e) -> p t h e", h=HEADS), AXX, ALU.add))
            dve.wait(m)
            made["feat"] = m

    pe.wait(w_in)
    dve.wait(w_in)
    act.wait(w_in)
    for t in range(4):
        fetch(t)
    LAG = 7
    for t in range(NT + LAG + 2):
        if t < NT:
            turn_rows(t)
            if t + 4 < NT:
                fetch(t + 4)
        if 1 <= t <= NT:
            layer(t - 1)
        if LAG <= t < NT + LAG:
            norm(t - LAG)
        if LAG + 1 <= t < NT + LAG + 1:
            heads(t - LAG - 1)
    sp.wait(made["feat"])
    with nc.allow_non_contiguous_dma(reason="rows of the table"):
        tab_out = sp.dma("tab_out", tab_d.rearrange("(t p) f -> p t f", p=P), feat[:, :, 0:FE])
        node_out = sp.dma("node_out", node_d.rearrange("(t p) f -> p t f", p=P), feat[:, :, HX:FG])

    def expert_steps():
        chunks = [(c * 4, min(4, NT - c * 4)) for c in range(-(-NT // 4))]
        jobs = [(c, e) for c in range(len(chunks)) for e in range(NX)]
        loaded, activated, projected, y_used, y_out, l1_used = {}, {}, {}, {}, {}, {}
        sp.wait(("pe_done", pe.n), *(xt_out[c] for c in range(len(chunks))))
        pe.wait(("dve_done", dve.n), ("act_done", act.n), w12_in)
        act.wait(("pe_done", pe.n))
        ny = 0
        nl = 0

        def load(c):
            t0, n = chunks[c]
            if c >= 2:
                sp.wait(projected[(c - 2, "l1")])
            loaded[c] = sp.dma(f"xt_in{c % 2}", xt[:, c % 2, :, 0:n * P], xT_d[:, :, t0 * P:(t0 + n) * P])

        load(0)
        load(1)
        for i in range(len(jobs) + 1):
            if i < len(jobs):
                c, e = jobs[i]
                t0, n = chunks[c]
                if e == 0 and 1 <= c and c + 1 < len(chunks):
                    load(c + 1)
                pe.wait(loaded[c])
                if i >= 2:
                    act.wait(projected[i - 2])
                for f in range(KF):
                    if nl >= 2:
                        pe.wait(l1_used[nl - 2])
                    o = bank[nl % 2][:, 0:n * P]
                    for k in range(KD):
                        m = pe.run(T.matmul(o, w1s[:, e, k, f * P:(f + 1) * P], xt[:, c % 2, k, 0:n * P],
                                            start=(k == 0), stop=(k == KD - 1)))
                    act.wait(m)
                    l1_used[nl] = act.run(S.activation(hh[:, i % 2, f, 0:n * P], o, ACT.Gelu,
                                                       bias=b1c[:, e, f:f + 1], scale=1.0))
                    nl += 1
                activated[i] = l1_used[nl - 1]
                if e == NX - 1:
                    projected[(c, "l1")] = m
            if i >= 1:
                c, e = jobs[i - 1]
                t0, n = chunks[c]
                pe.wait(activated[i - 1])
                for k in range(n):
                    if ny >= 2:
                        pe.wait(y_used[ny - 2])
                    o = bank[2 + ny % 2][:, 0:D]
                    for f in range(KF):
                        m = pe.run(T.matmul(o, hh[:, (i - 1) % 2, f, k * P:(k + 1) * P], w2s[:, e, f, :],
                                            start=(f == 0), stop=(f == KF - 1)))
                    dve.wait(m)
                    if ny >= 4:
                        dve.wait(y_out[ny - 4])
                    y_used[ny] = dve.run(V.tensor_tensor(yo[:, ny % 4, :], o, b2b[:, e, :], ALU.add))
                    sp.wait(y_used[ny])
                    y_out[ny] = sp.dma(f"y_out{ny % 4}", y_d[e, (t0 + k) * P:(t0 + k + 1) * P, :], yo[:, ny % 4, :])
                    ny += 1
                    yield
                projected[i - 1] = m
        made["y_out"] = [y_out[ny - 1 - k] for k in range(4)]

    FC = 64
    QC = C2 // 4
    NCF = C2 // FC
    pool.wait(made["sorted"], tab_out, x1_out[NT - 1])
    feat_in = {}
    for c in range(NCF):
        for j in range(c * FC, (c + 1) * FC):
            feat_in[c] = pool.sent(f"feat_in{c}", G.indirect_dma_start(
                out=g[:, j, 0:FE], out_offset=None, in_=tab_d, in_offset=at_rows(srt[:, j:j + 1])))
        if c == 0:
            for t in range(NT):
                start_out = pool.sent("start_out", G.indirect_dma_start(
                    out=start_d, out_offset=at_rows(idx_s[:, t:t + 1]), in_=feat[:, t, HX:FG + 1], in_offset=None,
                    bounds_check=E2 - 1, oob_is_err=False))

    for _ in expert_steps():
        pass

    mlp_done = [("pe_done", pe.n), ("act_done", act.n), *made["y_out"]]
    sp.wait(start_out, ("dve_done", dve.n), *mlp_done)
    m = sp.dma("edge_in", edge_n[:, :, :].rearrange("p j f -> p (j f)"), start_d.rearrange("(p j) f -> p (j f)", p=P))
    dve.wait(m, *mlp_done)
    ids = edge_n[:, :, 2 * HEADS]
    vrun(V.tensor_scalar(same_f[:, :], ids, 0.0, None, ALU.is_equal))
    vrun(V.tensor_scalar(reset_f[:, 0:C2], ids, 0.0, -BIG, ALU.is_gt, ALU.mult))
    vrun(V.memset(reset_f[:, C2:C2 + 1], 0.0))
    vrun(V.tensor_reduce(sm[:, 2:3], ids, AXX, ALU.max))
    HEAD, LAST = sm[:, 0:1], sm[:, 1:2]

    def turned_mask(cond_bank, scalar, out):
        return vrun(V.tensor_scalar(out, cond_bank, scalar, None, ALU.is_equal))

    m = broadcast_cols(sm[:, 2:3], (), bank[6][:, 0:P])
    pe.wait(m)
    m = pe.run(T.transpose(bank[5][:, 0:P], before[:, :], ident[:, :]))
    dve.wait(m)
    vrun(V.tensor_copy(segm[:, 0, :], bank[5][:, 0:P]))
    vrun(V.tensor_tensor(segm[:, 0, :], bank[6][:, 0:P], segm[:, 0, :], ALU.mult))
    vrun(V.tensor_reduce(sm[:, 3:4], segm[:, 0, :], AXX, ALU.max))
    vrun(V.tensor_tensor(HEAD, edge_n[:, 0:1, 2 * HEADS], sm[:, 3:4], ALU.max))
    vrun(V.tensor_tensor(LAST, sm[:, 2:3], sm[:, 3:4], ALU.max))
    m = vrun(V.tensor_scalar(smi[:, 4:5], HEAD, -1.0, None, ALU.add))
    pool.wait(m, node_out)
    m_row = pool.sent("row_in", G.indirect_dma_start(out=sm[:, 80:88], out_offset=None, in_=node_d,
                                                     in_offset=at_rows(smi[:, 4:5])))
    vrun(V.tensor_tensor_scan(id_run[:, :], ids, ids, HEAD, ALU.max, ALU.max))
    vrun(V.tensor_scalar(first_f[:, :], id_run[:, :], HEAD, None, ALU.is_equal))
    vrun(V.tensor_reduce(sm[:, 8:9], first_f[:, :], AXX, ALU.add))
    vrun(V.tensor_scalar(first_f[:, :], first_f[:, :], -1.0, BIG, ALU.add, ALU.mult))
    vrun(V.tensor_scalar(last_f[:, :], id_run[:, :], LAST, None, ALU.is_equal))
    vrun(V.tensor_scalar(last_f[:, :], last_f[:, :], -1.0, BIG, ALU.add, ALU.mult))
    fix_f = row_ends(sm[:, 8:9], row_at[:, 1:2], HEAD, LAST, smi[:, 2:3], smi[:, 3:4])
    m = broadcast_cols(HEAD, (), bank[6][:, 0:P])
    dve.wait(m)
    m = broadcast_cols(LAST, (m,), bank[6][:, P:2 * P])
    dve.wait(m)
    for k in range(4):
        turned_mask(bank[6][:, k % 2 * P:(k % 2 + 1) * P], HEAD if k < 2 else LAST, segm[:, k, :])
    sum_mask = vrun(V.scalar_tensor_tensor(out=tmask[:, :], in0=bank[6][:, 0:P], scalar=LAST, in1=before[:, :],
                                           op0=ALU.is_equal, op1=ALU.mult))
    dve.wait(m_row)
    for f in range(2 * HEADS):
        m = dve.run(V.tensor_tensor_scan(edge_n[:, :, f], same_f[:, :], edge_n[:, :, f], sm[:, 80 + f:81 + f],
                                         ALU.mult, ALU.add))
    dve.wait(m)
    a_self, a_dest = edge_n[:, :, 0:HEADS], edge_n[:, :, HEADS:2 * HEADS]

    prev_m = None
    for c in range(NCF):
        dve.wait(feat_in[c])
        a, b = c * FC, (c + 1) * FC
        if prev_m:
            dve.wait(prev_m)
        for h in range(HEADS):
            prev_m = dve.run(V.tensor_tensor_scan(
                g[:, a:b, FE + h], reset_f[:, a:b], g[:, a:b, HX + h],
                -BIG if c == 0 else g[:, a - 1:a, FE + h], ALU.add, ALU.max))
    dve.wait(prev_m)
    for h in range(HEADS):
        m = dve.run(V.tensor_tensor_scan(g[:, ::-1, FE + h], reset_f[:, C2:0:-1], g[:, ::-1, FE + h], -BIG,
                                         ALU.add, ALU.max))
    dve.wait(m)
    for k, col in ((0, 0), (1, C2 - 1)):
        m = vrun(V.tensor_tensor(hm[:, k, :, :], ident[:, None, :].broadcast_to([P, HEADS, P]),
                                 g[:, col, FE:FG, None].broadcast_to([P, HEADS, P]), ALU.mult))
        pe.wait(m)
        for h in range(HEADS):
            m = pe.run(T.matmul(bank[k][:, h * P:(h + 1) * P], ones[:, :], hm[:, k, h, :], start=True, stop=True))
    dve.wait(m)
    for k in range(4):
        mask = segm[:, k:k + 1, :].broadcast_to([P, HEADS, P])
        w = hm[:, 2, :, :]
        vrun(V.tensor_tensor(w, bank[k % 2][:, :].rearrange("p (h q) -> p h q", h=HEADS), mask, ALU.mult))
        m = vrun(V.tensor_scalar(segm[:, k, :], segm[:, k, :], -1.0, BIG, ALU.add, ALU.mult))
        vrun(V.tensor_tensor(w, w, mask, ALU.add))
        vrun(V.tensor_reduce(sm[:, 60 + 4 * k:64 + 4 * k], w, AXX, ALU.max))
    vrun(V.tensor_tensor(sm[:, 20:24], sm[:, 60:64], sm[:, 64:68], ALU.max))
    vrun(V.tensor_tensor(sm[:, 24:28], sm[:, 68:72], sm[:, 72:76], ALU.max))
    for part, at in ((first_f, 20), (last_f, 24)):
        for h in range(HEADS):
            m = dve.run(V.scalar_tensor_tensor(out=g[:, :, FE + h], in0=part[:, :], scalar=sm[:, at + h:at + h + 1],
                                               in1=g[:, :, FE + h], op0=ALU.add, op1=ALU.max))
        dve.wait(m)

    exped = {}
    for k in range(4):
        s_ = slice(k * QC, (k + 1) * QC)
        top_, e_ = g[:, s_, FE:FG], g[:, s_, HX:FE]
        vrun(V.tensor_tensor(e_, e_, a_dest[:, s_, :], ALU.add))
        vrun(V.tensor_tensor(top_, top_, a_self[:, s_, :], ALU.max))
        vrun(V.scalar_tensor_tensor(out=e_, in0=e_, scalar=0.2, in1=e_, op0=ALU.mult, op1=ALU.max))
        vrun(V.tensor_tensor(top_, top_, a_dest[:, s_, :], ALU.add))
        vrun(V.scalar_tensor_tensor(out=top_, in0=top_, scalar=0.2, in1=top_, op0=ALU.mult, op1=ALU.max))
        m = vrun(V.tensor_tensor(e_, e_, top_, ALU.subtract))
        act.wait(m)
        exped[k] = act.run(S.activation(e_, e_, ACT.Exp))
    sum_rows = sum_d.rearrange("(p j) f -> p j f", p=P)
    m = None
    for k in range(4):
        a, b = k * QC, (k + 1) * QC
        dve.wait(exped[k], *([m] if m else []))
        for h in range(HEADS):
            o = g[:, a:b, h * NX:(h + 1) * NX]
            m = dve.run(V.tensor_tensor(o, o, g[:, a:b, HX + h:HX + h + 1].broadcast_to([P, QC, NX]), ALU.mult))
        dve.wait(m)
        for f in range(FE):
            m = dve.run(V.tensor_tensor_scan(g[:, a:b, f], same_f[:, a:b], g[:, a:b, f],
                                             0.0 if k == 0 else g[:, a - 1:a, f], ALU.mult, ALU.add))
        sp.wait(m)
        m_sum = sp.dma("sum_out", sum_rows[:, a:b, :], g[:, a:b, :])
    pe.wait(m, sum_mask)
    carried = pe.run(T.matmul(bank[2][:, 0:FE], tmask[:, :], g[:, C2 - 1, 0:FE], start=True, stop=True))
    pool.wait(m_sum, fix_f)
    m = pool.sent("fix_in", G.indirect_dma_start(out=sm[:, 32:32 + FG], out_offset=None, in_=sum_d,
                                                 in_offset=at_rows(smi[:, 2:3])))
    dve.wait(m, carried)
    m = vrun(V.tensor_tensor(sm[:, 32:32 + FE], sm[:, 32:32 + FE], bank[2][:, 0:FE], ALU.add))
    pool.wait(m)
    m = pool.sent("fix_out", G.indirect_dma_start(
        out=sum_d, out_offset=at_rows(smi[:, 3:4]), in_=sm[:, 32:32 + FG], in_offset=None,
        bounds_check=E2 - 1, oob_is_err=False))
    pool.wait(m, ("dve_done", dve.n))
    for t in range(NT):
        m = pool.sent("node_in", G.indirect_dma_start(out=fsum[:, t, :], out_offset=None, in_=sum_d,
                                                      in_offset=at_rows(idx_f[:, t:t + 1])))
    dve.wait(m)

    f_ = lambda i: fin[:, i, :, :]
    f4 = lambda i: fin[:, i, :, 0:HEADS]
    full = [P, NT, HX]
    a_s, a_d = feat[:, :, HX:FE], feat[:, :, FE:FG]
    nmax = fsum[:, :, FE:FG]
    vrun(V.tensor_tensor(fsum[:, :, :], fsum[:, :, :], has_f[:, :, None].broadcast_to([P, NT, FG]), ALU.mult))
    vrun(V.tensor_tensor(f4(4), a_s, a_d, ALU.add))
    vrun(V.scalar_tensor_tensor(out=f4(4), in0=f4(4), scalar=0.2, in1=f4(4), op0=ALU.mult, op1=ALU.max))
    vrun(V.tensor_scalar(fin[:, 6, :, 0:1], has_f[:, :, None], -1.0, -1.0, ALU.add, ALU.mult))
    vrun(V.tensor_tensor(f4(5), f4(4), fin[:, 6, :, 0:1].broadcast_to([P, NT, HEADS]), ALU.mult))
    vrun(V.tensor_tensor(nmax, nmax, f4(5), ALU.add))
    m = vrun(V.tensor_tensor(f4(4), f4(4), nmax, ALU.subtract))
    act.wait(m)
    m = act.run(S.activation(f4(4), f4(4), ACT.Exp))
    dve.wait(m)
    per_head = lambda ap: ap[:, :, :, None].broadcast_to([P, NT, HEADS, NX])
    h4 = lambda ap: ap.rearrange("p t (h e) -> p t h e", h=HEADS)

    def heads_times(o, a, b):
        for h in range(HEADS):
            m = dve.run(V.tensor_tensor(o[:, :, h * NX:(h + 1) * NX], a[:, :, h * NX:(h + 1) * NX],
                                        b[:, :, h:h + 1].broadcast_to([P, NT, NX]), ALU.mult))
        dve.wait(m)

    heads_times(f_(5), feat[:, :, 0:HX], f4(4))
    vrun(V.tensor_tensor(f_(5), f_(5), fsum[:, :, 0:HX], ALU.add))
    vrun(V.tensor_tensor(f4(6), f4(4), fsum[:, :, HX:FE], ALU.add))
    vrun(V.tensor_scalar(f4(6), f4(6), 1e-16, None, ALU.add))
    vrun(V.reciprocal(f4(6), f4(6)))
    heads_times(f_(5), f_(5), f4(6))
    vrun(V.tensor_tensor(f_(5), f_(5), gln[:, 0:1, :].broadcast_to(full), ALU.add))
    one = lambda i: fin[:, i, :, 0:1]
    vrun(V.tensor_reduce(fin[:, 6, :, 0], f_(5), AXX, ALU.add))
    vrun(V.tensor_scalar(one(6), one(6), 1.0 / HX, None, ALU.mult))
    vrun(V.tensor_tensor(f_(5), f_(5), one(6).broadcast_to(full), ALU.subtract))
    vrun(V.tensor_tensor(f_(7), f_(5), f_(5), ALU.mult))
    vrun(V.tensor_reduce(fin[:, 6, :, 1], f_(7), AXX, ALU.add))
    vrun(V.tensor_scalar(fin[:, 6, :, 1:2], fin[:, 6, :, 1:2], 1.0 / HX, EPS, ALU.mult, ALU.add))
    act.wait(("dve_done", dve.n))
    m = act.run(S.activation(fin[:, 6, :, 1:2], fin[:, 6, :, 1:2], ACT.Sqrt))
    dve.wait(m)
    vrun(V.reciprocal(fin[:, 6, :, 1:2], fin[:, 6, :, 1:2]))
    vrun(V.tensor_tensor(f_(5), f_(5), fin[:, 6, :, 1:2].broadcast_to(full), ALU.mult))
    vrun(V.tensor_tensor(f_(5), f_(5), gln[:, 1:2, :].broadcast_to(full), ALU.mult))
    vrun(V.tensor_tensor(f_(5), f_(5), gln[:, 2:3, :].broadcast_to(full), ALU.add))
    sc = fin[:, 7, :, 0:NX]
    vrun(V.tensor_tensor(sc, fin[:, 5, :, 0:NX], fin[:, 5, :, NX:2 * NX], ALU.add))
    for h in range(2, HEADS):
        vrun(V.tensor_tensor(sc, sc, fin[:, 5, :, h * NX:(h + 1) * NX], ALU.add))
    vrun(V.tensor_scalar(sc, sc, 1.0 / HEADS, None, ALU.mult))
    vrun(V.memset(fin[:, 8, :, 0:NX], 0.0))
    for e in range(NX):
        for o in range(NX):
            if o == e:
                continue
            vrun(V.tensor_tensor(one(6), fin[:, 7, :, o:o + 1], fin[:, 7, :, e:e + 1],
                                 ALU.is_ge if o < e else ALU.is_gt))
            vrun(V.tensor_tensor(fin[:, 8, :, e:e + 1], fin[:, 8, :, e:e + 1], one(6), ALU.add))
    vrun(V.tensor_scalar(fin[:, 8, :, 0:NX], fin[:, 8, :, 0:NX], 1.5, None, ALU.is_lt))
    vrun(V.tensor_reduce(fin[:, 6, :, 0], sc, AXX, ALU.max))
    m = vrun(V.tensor_tensor(sc, sc, one(6).broadcast_to([P, NT, NX]), ALU.subtract))
    act.wait(m)
    m = act.run(S.activation(sc, sc, ACT.Exp))
    dve.wait(m)
    vrun(V.tensor_tensor(sc, sc, fin[:, 8, :, 0:NX], ALU.mult))
    vrun(V.tensor_reduce(fin[:, 6, :, 0], sc, AXX, ALU.add))
    vrun(V.reciprocal(one(6), one(6)))
    gates = vrun(V.tensor_tensor(sc, sc, one(6).broadcast_to([P, NT, NX]), ALU.mult))

    sp.wait(("pe_done", pe.n), gates, m_sum, ("dve_done", dve.n), x1_out[NT - 1], *made["y_out"])
    act.wait(("pe_done", pe.n), gates, m_sum)
    CT = XG
    outs, loaded = {}, {}

    def load_comb(c):
        s = c % 2
        if c >= 2:
            sp.wait(outs[c - 2])
        rows_ = slice(c * CT * P, (c + 1) * CT * P)
        for e in range(NX):
            sp.dma(f"comb_in{s}", comb[:, s, e, :, :], y_d[e, rows_, :].rearrange("(t p) d -> p t d", p=P))
        loaded[c] = sp.dma(f"comb_in{s}", comb[:, s, NX, :, :], x1_d[rows_, :].rearrange("(t p) d -> p t d", p=P))

    load_comb(0)
    for c in range(NT // CT):
        if c + 1 < NT // CT:
            load_comb(c + 1)
        s = c % 2
        dve.wait(loaded[c])
        for e in range(NX):
            for k in range(CT):
                t = c * CT + k
                m = dve.run(V.scalar_tensor_tensor(
                    out=comb[:, s, NX, k, :], in0=comb[:, s, e, k, :], scalar=fin[:, 7, t, e:e + 1],
                    in1=comb[:, s, NX, k, :], op0=ALU.mult, op1=ALU.add))
            dve.wait(m)
        act.wait(m)
        n = min(CT, FULL // P - c * CT)
        outs[c] = act.dma(f"out{s}", out[c * CT * P:(c * CT + n) * P, :].rearrange("(t p) d -> p t d", p=P),
                          comb[:, s, NX, 0:n, :])
        if n < CT:
            outs[c] = act.dma(f"out{s}", out[FULL:N, :], comb[0:N - FULL, s, NX, n, :])
    for lane in sorted(Queue.lanes):
        act.wait((lane, Queue.lanes[lane]))


_INS = ["x", "src", "dst", "L0_gnn_W", "L0_gnn_M", "L0_ffn_W_gat", "L0_ffn_att_src", "L0_ffn_att_dst",
        "L0_ffn_b_gat", "L0_ffn_ln_gamma", "L0_ffn_ln_beta", "L0_ffn_W1", "L0_ffn_b1", "L0_ffn_W2",
        "L0_ffn_b2", "L0_ffn_edge_index"]


def kernel(**inputs):
    import numpy as np
    import concourse.bacc as bacc
    from concourse.bass_utils import run_bass_kernel_spmd

    nc = bacc.Bacc("TRN2", target_bir_lowering=False, num_devices=1)
    arrays, args = {}, []
    for name in _INS:
        a = np.ascontiguousarray(inputs[name])
        arrays[f"in_{name}"] = a
        args.append(nc.dram_tensor(f"in_{name}", a.shape, mybir.dt.from_np(a.dtype), kind="ExternalInput").ap())
    args.append(nc.dram_tensor("out_x", inputs["x"].shape, F32, kind="ExternalOutput").ap())
    build(nc, *args)
    r = run_bass_kernel_spmd(nc, [arrays], core_ids=[0])
    return r.results[0]["out_x"]
```

```python
import concourse.bass as bass
from concourse import mybir

F32 = mybir.dt.float32
BF16 = mybir.dt.bfloat16
F16 = mybir.dt.float16
I16 = mybir.dt.int16
I32 = mybir.dt.int32
ALU = mybir.AluOpType
ACT = mybir.ActivationFunctionType
AXX = mybir.AxisListType.X

P = 128
EPS = 1e-5
BIG = 1.0e30
FAR = 1 << 21
HEADS = 4
RING = 4
JC = 8
GB = 4
DR = 6
PB = 32
POOL_MOVES = 1
MR = 5
MOVE_LAG = 2
PACE1 = 0.48
PACE2 = 0.94
LESS = 3
OUT_MOVES = 2
FIX_MOVES = 3
LAG = 8
W_AT = 30
PE_COLS = 84
CR = 3
PART = 3
POOL_TILES = 2


class Marks:

    def __init__(self, nc):
        self.nc, self.sems = nc, {}

    def sem(self, name):
        if name not in self.sems:
            self.sems[name] = self.nc.alloc_semaphore(name)
        return self.sems[name]


class Queue:

    lanes = None

    def __init__(self, marks, eng, name):
        self.m, self.eng, self.name, self.n, self.passed = marks, eng, name, 0, {}

    def wait(self, *marks):
        for name, value in marks:
            if self.passed.get(name, 0) < value:
                self.eng.wait_ge(self.m.sem(name), value)
                self.passed[name] = value

    def run(self, ins):
        ins.then_inc(self.m.sem(self.name), 1)
        self.n += 1
        return (self.name, self.n)

    def sent(self, lane, ins):
        ins.then_inc(self.m.sem(lane), 16)
        self.lanes[lane] = self.lanes.get(lane, 0) + 16
        return (lane, self.lanes[lane])

    def dma(self, lane, out, in_):
        return self.sent(lane, self.eng.dma_start(out, in_))


def build(nc, x, src, dst, W, M, W_gat, att_src, att_dst, b_gat, ln_gamma, ln_beta,
          W1, b1, W2, b2, edge_index, out):
    N, D = x.shape
    E1, E2 = src.shape[0], edge_index.shape[1]
    NX, _, F = W1.shape
    HX = HEADS * NX
    KD, KF = D // P, F // P
    NT = -(-N // P)
    NPAD = NT * P
    C1 = -(-E1 // P)
    C1 = -(-C1 // JC) * JC
    C2 = E2 // P
    HC = C2 // 2
    NCH = C1 // JC
    NG = C2 // GB
    XG = 7
    FE = HX + HEADS
    FG = FE + HEADS
    FS = HEADS + 1
    FULL = (N // P) * P
    FC = 64
    NCF = C2 // FC
    LATE = NCF - 2
    assert NT % XG == 0 and E2 % P == 0 and C2 % (2 * GB) == 0 and N < NPAD and D == 256

    def dram(name, shape, dt):
        return nc.dram_tensor(name, shape, dt).ap()

    xn_d = dram("xn_d", [NPAD, D], F32)
    run_d = dram("run_d", [P * C1 + 1, D], F32)
    run_rows = run_d[0:P * C1, :].rearrange("(p j) d -> p j d", p=P)
    dst_d = dram("dst_d", [P, C1], I32)
    tab_d = dram("tab_d", [NPAD, FE], F32)
    x1_d = dram("x1_d", [NPAD, D], F32)
    xT_d = dram("xT_d", [P, KD, NPAD], F32)
    y_d = dram("y_d", [NX, NPAD, D], F32)
    node_d = dram("node_d", [NPAD, HEADS], F32)
    self_d = dram("self_d", [NPAD, D], F32)
    code_d = dram("code_d", [E2, 1], F32)
    code_rows = code_d.rearrange("(p j) a -> p (j a)", p=P)
    start_d = dram("start_d", [E2, FS], F32)
    sum_d = dram("sum_d", [E2, FG], F32)

    base = -(-nc.sbuf_base // 64) * 64
    top = nc.sbuf_base + nc.sbuf_bytes_remaining

    class Region:
        def __init__(self, at):
            self.at = at

        def take(self, name, shape, dt):
            n = 1
            for s in shape[1:]:
                n *= s
            size = -(-n * mybir.dt.size(dt) // 32) * 32
            t = nc.alloc_sbuf_tensor_at(name, shape, dt, offset=self.at)
            self.at += size
            assert self.at <= top, (name, self.at, top)
            return t

    r = Region(base)
    iota_i = r.take("iota_i", [P, P], I32)
    iota_b = r.take("iota_b", [P, P], BF16)
    ident = r.take("ident", [P, P], F32)
    ident_b = r.take("ident_b", [P, P], BF16)
    ones = r.take("ones", [P, P], F32)
    before = r.take("before", [P, P], F32)
    not_before = r.take("not_before", [P, P], BF16)
    shift1 = r.take("shift1", [P, P], F32)
    up1 = r.take("up1", [P, P], F32)
    wrap1 = r.take("wrap1", [P, P], F32)
    node_id = r.take("node_id", [P, NT], F32)
    node_ii = r.take("node_ii", [P, NT], I32)
    row_at = r.take("row_at", [P, 2], I32)
    idx_g = r.take("idx_g", [P, NT], I32)
    idx_f = r.take("idx_f", [P, NT], I32)
    idx_s = r.take("idx_s", [P, NT], I32)
    has_f = r.take("has_f", [P, NT], F32)
    sm = r.take("sm", [P, 96], F32)
    smi = r.take("smi", [P, 16], I32)
    smt = r.take("smt", [P, 8, NT], F32)
    feat = r.take("feat", [P, NT, FG + 1], F32)
    attb = r.take("attb", [P, 2, HX], F32)
    gln = r.take("gln", [P, 3, HX], F32)
    wgat = r.take("wgat", [P, KD, HX], F32)
    b1c = r.take("b1c", [P, NX, KF], F32)
    b2b = r.take("b2b", [P, NX, D], F32)
    tmask = r.take("tmask", [P, P], F32)
    cfix = r.take("cfix", [P, D], F32)
    stat = r.take("stat", [P, XG, 6], F32)
    aggr = r.take("aggr", [P, NT, 2], F32)
    r4 = r.at
    dlneg = r.take("dlneg", [P, C2], F32)
    dh = r.take("dh", [P, C2], BF16)
    code = r.take("code", [P, C2], F32)
    place = r.take("place", [P, C2], I32)
    q = Region(r4)
    tab_parts = q.take("tab_parts", [P, 3, FE, NT], BF16)
    picked = q.take("picked", [P, 2, FE, NT], F32)
    assert q.at <= r.at
    q = Region(r4)
    same_f = q.take("same_f", [P, C2], F32)
    reset_f = q.take("reset_f", [P, C2 + 1], F32)
    assert q.at <= r.at
    srt = r.take("srt", [P, C2], I32)
    r2 = r.at
    w1s = r.take("w1s", [P, NX, KD, F], F32)
    w2s = r.take("w2s", [P, NX, KF, D], F32)
    q = Region(r2)
    dsti = q.take("dsti", [P, C1], I32)
    srci = q.take("srci", [P, C1], I32)
    same_g = q.take("same_g", [P, C1], F32)
    rows = q.take("rows", [P, 2, C1], I32)
    assert q.at <= r.at
    r3 = r.at
    hh = r.take("hh", [P, 2, KF, 4 * P], F32)
    xt = r.take("xt", [P, 2, KD, 4 * P], F32)
    yo = r.take("yo", [P, 4, D], F32)
    r5 = r.at
    agg = r.take("agg", [P, 4, D], F32)
    own = r.take("own", [P, 4, D], F32)
    tin = r.take("tin", [P, 2, KD, P], F32)
    x2 = r.take("x2", [P, 2, D], F32)
    q = Region(r5)
    digit_i = q.take("digit_i", [P, PE_COLS], I32)
    digits = q.take("digits", [P, 2, PE_COLS], F32)
    low_hot = q.take("low_hot", [P, 2, P], BF16)
    low_turned = q.take("low_turned", [P, 2, P], BF16)
    high_hot = q.take("high_hot", [P, 5, NT], BF16)
    assert q.at <= r.at
    q = Region(r3)
    half_h = q.take("half_h", [P, 2, P], F16)
    iota_h = q.take("iota_h", [P, HC], F16)
    row_hot = q.take("row_hot", [P, MR, 2, P], F16)
    rc_i = q.take("rc_i", [P, 2, PB], I32)
    rc = q.take("rc", [P, 2, 2, PB], F32)
    zeros = q.take("zeros", [P, C2], F32)
    moving = q.at
    assert moving <= r3 + 2 * KF * 4 * P * 4
    raw_e = q.take("raw_e", [P, 2, C2], I32)
    q = Region(moving)
    oh = q.take("oh", [P, DR, GB, P], BF16)
    dhh = q.take("dhh", [P, DR, GB, NT], BF16)
    dsq = q.take("dsq", [P, 2, 2 * GB, P], BF16)
    oht = q.take("oht", [P, 4, GB, P], F32)
    ohtb = q.take("ohtb", [P, 2, GB, P], BF16)
    eqm = q.take("eqm", [P, 3, GB, P], BF16)
    hist = q.take("hist", [P, 4, GB, NT], F32)
    prod = q.take("prod", [P, GB, NT], F32)
    hinit = q.take("hinit", [P, NT], F32)
    cmpb = q.take("cmpb", [P, XG, P], F32)
    r.at = max(r.at, q.at)
    q = Region(r2)
    edge_n = q.take("edge_n", [P, C2, FS], F32)
    id_run = q.take("id_run", [P, C2], F32)
    first_f = q.take("first_f", [P, C2], F32)
    step = q.take("step", [P, 2, FC, HEADS], F32)
    segm = q.take("segm", [P, 2, P], F32)
    hm = q.take("hm", [P, 2, HEADS, P], F32)
    fsum = q.take("fsum", [P, NT, FG], F32)
    fin = q.take("fin", [P, 8, NT, HX], F32)
    r.at = max(r.at, q.at)
    r6 = q.at
    r1 = r.at
    g = r.take("g", [P, C2, FG], F32)
    q = Region(r1)
    xs = q.take("xs", [P, NT, D], F32)
    ring = q.take("ring", [P, RING, JC, D], F32)
    wself = q.take("wself", [P, KD, D], F32)
    wmsg = q.take("wmsg", [P, KD, D], F32)
    col_hot = q.take("col_hot", [P, MR, HC], F16)
    assert q.at <= r.at
    q = Region(r6)
    comb = q.take("comb", [P, CR, NX + 1, XG, D], F32)

    bank = [nc.alloc_psum_tensor(f"bank{i}", [P, 512], F32) for i in range(8)]
    bank_t = bank[7][:, 0:GB * P // 2].bitcast(BF16).rearrange("p (k e) -> p k e", k=GB)

    marks = Marks(nc)
    Queue.lanes = {}
    pe, dve, act, pool, sp = (Queue(marks, e, n) for e, n in (
        (nc.tensor, "pe_done"), (nc.vector, "dve_done"), (nc.scalar, "act_done"),
        (nc.gpsimd, "pool_done"), (nc.sync, "sp_done")))
    V, S, T, G = nc.vector, nc.scalar, nc.tensor, nc.gpsimd

    def vrun(ins, *_):
        m = dve.run(ins)
        dve.wait(m)
        return m

    def at_rows(ap):
        return bass.IndirectOffsetOnAxis(ap=ap, axis=0)

    pool.run(G.iota(iota_i[:, :], pattern=[[1, P]], base=0, channel_multiplier=0))
    pool.run(G.iota(node_ii[:, :], pattern=[[P, NT]], base=0, channel_multiplier=1))
    pool.run(G.iota(row_at[:, 0:1], pattern=[[0, 1]], base=0, channel_multiplier=C1))
    pool.run(G.iota(row_at[:, 1:2], pattern=[[0, 1]], base=0, channel_multiplier=C2))
    for t in (ident, shift1, up1, wrap1):
        pool.run(G.memset(t[:, :], 0.0))
    m = pool.run(G.memset(ones[:, :], 1.0))
    pool.wait(m)
    pool.run(G.affine_select(out=ident[:, :], in_=ident[:, :], compare_op=ALU.not_equal, fill=1.0, base=0,
                             pattern=[[-1, P]], channel_multiplier=1))
    pool.run(G.affine_select(out=shift1[:, :], in_=shift1[:, :], compare_op=ALU.not_equal, fill=1.0, base=1,
                             pattern=[[-1, P]], channel_multiplier=1))
    pool.run(G.affine_select(out=wrap1[:, :], in_=wrap1[:, :], compare_op=ALU.not_equal, fill=1.0,
                             base=-(P - 1), pattern=[[P, P]], channel_multiplier=1))
    pool.run(G.affine_select(out=up1[:, :], in_=up1[:, :], compare_op=ALU.not_equal, fill=1.0, base=-1,
                             pattern=[[-1, P]], channel_multiplier=1))
    consts = pool.run(G.affine_select(out=before[:, :], in_=ones[:, :], compare_op=ALU.is_gt, fill=0.0, base=0,
                                      pattern=[[1, P]], channel_multiplier=-1))

    pad_x = dve.run(V.memset(xs[:, NT - 1, :], 0.0))
    dve.run(V.memset(dsti[:, :], N))
    pad_e = dve.run(V.memset(srci[:, :], 0))
    sp.wait(pad_x)
    x_in = []
    for c in range(NT // XG):
        t0, t1 = c * XG, min((c + 1) * XG, FULL // P)
        m = sp.dma(f"x_in{c}", xs[:, t0:t1, :], x[t0 * P:t1 * P, :].rearrange("(t p) d -> p t d", p=P))
        if c == NT // XG - 1:
            m = sp.dma(f"x_in{c}", xs[0:N - FULL, NT - 1, :], x[FULL:N, :])
        x_in.append(m)
    act.wait(pad_e)
    fullrows = E1 // C1
    cut = fullrows // 16 * 16
    for a, t in ((dst, dsti), (src, srci)):
        lane = "dst_in" if a is dst else "src_in"
        full = a[0:fullrows * C1].rearrange("(p j) -> p j", j=C1)
        act.dma(lane, t[0:cut, :], full[0:cut, :])
        act.dma(lane, t[cut:fullrows, :], full[cut:fullrows, :])
        act.dma(lane, t[fullrows:fullrows + 1, 0:E1 - fullrows * C1],
                a[fullrows * C1:E1].rearrange("(a j) -> a j", a=1))
    dst_in, src_in = ("dst_in", 48), ("src_in", 48)
    for c in range(2):
        e_in = act.dma("e_in", raw_e[:, c, :], edge_index[c, :].rearrange("(p j) -> p j", j=C2))

    def norm_scalars(aggr):
        m = vrun(V.tensor_scalar(aggr[:, :, 1], aggr[:, :, 1], EPS, None, ALU.add))
        act.wait(m)
        m = act.run(S.activation(aggr[:, :, 1], aggr[:, :, 1], ACT.Sqrt))
        dve.wait(m)
        vrun(V.reciprocal(aggr[:, :, 1], aggr[:, :, 1]))
        return dve.run(V.scalar_tensor_tensor(out=aggr[:, :, 0], in0=aggr[:, :, 0], scalar=-1.0,
                                              in1=aggr[:, :, 1], op0=ALU.mult, op1=ALU.mult))

    xn_out = []
    for c in range(NT // XG):
        dve.wait(x_in[c])
        for k in range(XG):
            m = dve.run(V.bn_stats(stat[:, k, :], xs[:, c * XG + k, :]))
        dve.wait(m)
        for k in range(XG):
            m = dve.run(V.bn_aggr(aggr[:, c * XG + k, :], stat[:, k, :]))
        dve.wait(m)
        m = norm_scalars(aggr[:, c * XG:(c + 1) * XG, :])
        act.wait(m)
        if c >= RING:
            act.wait(xn_out[c - RING])
        for k in range(XG):
            t = c * XG + k
            m = act.run(S.activation(ring[:, c % RING, k, :], xs[:, t, :], ACT.Identity,
                                     bias=aggr[:, t, 0:1], scale=aggr[:, t, 1:2]))
        sp.wait(m)
        xn_out.append(sp.dma(f"xn_out{c % RING}",
                             xn_d[c * XG * P:(c + 1) * XG * P, :].rearrange("(t p) d -> p t d", p=P),
                             ring[:, c % RING, 0:XG, :]))

    sp.wait(dst_in)
    dst_out = sp.dma("dst_out", dst_d, dsti[:, :])
    sp.dma("w_in", wself[:, :, :], W.rearrange("(k p) n -> p k n", p=P))
    sp.dma("w_in", wmsg[:, :, :], M.rearrange("(k p) n -> p k n", p=P))
    sp.dma("w_in", wgat[:, :, :], W_gat.rearrange("(k p) n -> p k n", p=P))
    for k, a in enumerate((att_src, att_dst)):
        sp.dma("w_in", attb[:, k, :], a.rearrange("h e -> (h e)").partition_broadcast(P))
    for k, a in enumerate((b_gat, ln_gamma, ln_beta)):
        sp.dma("w_in", gln[:, k, :], a.partition_broadcast(P))
    with nc.allow_non_contiguous_dma(reason="b1 by column, 8 KB once"):
        sp.dma("w_in", b1c[:, :, :], b1.rearrange("e (f p) -> p e f", p=P))
    for e in range(NX):
        w_in = sp.dma("w_in", b2b[:, e, :], b2[e, :].partition_broadcast(P))

    dve.wait(consts, dst_in)
    dve.run(V.tensor_copy(iota_b[:, :], iota_i[:, :]))
    dve.run(V.tensor_copy(node_id[:, :], node_ii[:, :]))
    dve.run(V.tensor_copy(ident_b[:, :], ident[:, :]))
    dve.run(V.tensor_scalar(not_before[:, :], before[:, :], -1.0, None, ALU.add))
    dve.run(V.tensor_scalar(feat[:, :, FG], node_ii[:, :], 1, None, ALU.add))
    dve.run(V.memset(same_g[:, 0:1], 0.0))
    vrun(V.tensor_tensor(same_g[:, 1:C1], dsti[:, 1:C1], dsti[:, 0:C1 - 1], ALU.is_equal))

    def broadcast_cols(col, free, bank_out, m_free=None):
        m = vrun(V.tensor_scalar(tmask[:, :], ident[:, :], col, None, ALU.mult))
        pe.wait(m, *free)
        return pe.run(T.matmul(bank_out, ones[:, :], tmask[:, :], start=True, stop=True))

    vrun(V.tensor_copy(sm[:, 0:1], dsti[:, 0:1]))
    vrun(V.tensor_copy(sm[:, 1:2], dsti[:, C1 - 1:C1]))
    m_rowheads = broadcast_cols(sm[:, 0:1], (), bank[6][:, 0:P])
    dve.wait(m_rowheads)
    for c in range(NT // XG):
        vrun(V.tensor_tensor(cmpb[:, :, :], bank[6][:, None, 0:P].broadcast_to([P, XG, P]),
                             node_id[:, c * XG:(c + 1) * XG, None].broadcast_to([P, XG, P]), ALU.is_le))
        m = vrun(V.tensor_reduce(smt[:, 0, c * XG:(c + 1) * XG], cmpb[:, :, :], AXX, ALU.add))
    vrun(V.tensor_scalar(smt[:, 1, :], smt[:, 0, :], -1.0, 0.0, ALU.add, ALU.max))
    row_of = vrun(V.tensor_copy(idx_g[:, :], smt[:, 1, :]))
    half_up = dve.run(V.tensor_scalar(smt[:, 2, :], node_id[:, :], 0.5, None, ALU.add))

    found = []

    def search(t):
        pool.wait(dst_out, row_of)
        if t >= 2:
            pool.wait(found[t - 2])
        m = pool.sent(f"rows_in{t % 2}", G.indirect_dma_start(
            out=rows[:, t % 2, :], out_offset=None, in_=dst_d, in_offset=at_rows(idx_g[:, t:t + 1])))
        act.wait(m, half_up)
        found.append(act.run(S.activation(rows[:, t % 2, :].bitcast(F32), rows[:, t % 2, :], ACT.Sign,
                                          bias=smt[:, 2, t:t + 1], scale=-1.0, accum_out=smt[:, 3, t:t + 1])))

    def graph_ends():
        dve.wait(found[-1])
        vrun(V.tensor_scalar(smt[:, 3, :], smt[:, 3, :], float(C1), 0.5, ALU.add, ALU.mult))
        vrun(V.scalar_tensor_tensor(out=smt[:, 4, :], in0=smt[:, 1, :], scalar=float(C1), in1=smt[:, 3, :],
                                    op0=ALU.mult, op1=ALU.add))
        vrun(V.tensor_scalar(smt[:, 0, :], smt[:, 0, :], 0.5, None, ALU.is_gt))
        m = vrun(V.tensor_tensor(smt[:, 4, :], smt[:, 4, :], smt[:, 0, :], ALU.mult))
        pe.wait(m)
        pe.run(T.matmul(bank[6][:, 0:NT], shift1[:, :], smt[:, 4, :], start=True, stop=False))
        m = pe.run(T.matmul(bank[6][:, 1:NT], wrap1[:, :], smt[:, 4, 0:NT - 1], start=False, stop=True))
        dve.wait(m)
        vrun(V.tensor_tensor(smt[:, 5, :], smt[:, 4, :], bank[6][:, 0:NT], ALU.is_gt))
        vrun(V.tensor_scalar(smt[:, 4, :], smt[:, 4, :], -1.0 - P * C1, None, ALU.add))
        vrun(V.tensor_tensor(smt[:, 4, :], smt[:, 4, :], smt[:, 5, :], ALU.mult))
        vrun(V.tensor_scalar(smt[:, 4, :], smt[:, 4, :], float(P * C1), None, ALU.add))
        return vrun(V.tensor_copy(idx_g[:, :], smt[:, 4, :]))

    made = {}
    scatters, here = [], [0]

    def scatter(before_chunk):
        while scatters and scatters[0][0] < before_chunk:
            _, b, m = scatters.pop(0)
            pool.wait(m, made["zero_out"])
            made["scattered"] = pool.sent("scattered", G.indirect_dma_start(
                out=code_d, out_offset=at_rows(place[:, b:b + 1]), in_=code[:, b:b + 1], in_offset=None))

    def sort_steps():
        dve.wait(e_in)
        dst_c, src_c = raw_e[:, 1, :], raw_e[:, 0, :]
        vrun(V.tensor_scalar(dst_c, dst_c, N, None, ALU.min))
        vrun(V.tensor_scalar(src_c, src_c, N - 1, 1024, ALU.min, ALU.add))
        bits = place[:, 0:C2 // 2].bitcast(I16)
        vrun(V.tensor_copy(bits, src_c))
        vrun(V.tensor_copy(code[:, :], bits.bitcast(F16)))
        vrun(V.tensor_single_scalar(place[:, :], dst_c, P.bit_length() - 1, ALU.logical_shift_right))
        vrun(V.tensor_copy(dh[:, :], place[:, :]))
        vrun(V.tensor_single_scalar(place[:, :], dst_c, P - 1, ALU.bitwise_and))
        low = vrun(V.tensor_scalar(dlneg[:, :], place[:, :], -1, None, ALU.mult))
        pool.wait(low)
        pool.run(G.iota(raw_e[:, 0, 0:2 * P], pattern=[[1, 2], [2, P]], base=0, channel_multiplier=0))
        m = pool.run(G.iota(raw_e[:, 0, HC:2 * HC], pattern=[[1, HC]], base=0, channel_multiplier=0))
        dve.wait(m)
        vrun(V.tensor_copy(half_h[:, :, :], raw_e[:, 0, 0:2 * P].rearrange("p (a b) -> p a b", a=2)))
        vrun(V.tensor_copy(iota_h[:, :], raw_e[:, 0, HC:2 * HC]))
        z = vrun(V.memset(zeros[:, :], 0.0))
        sp.wait(z)
        flat = start_d.rearrange("(p a) f -> p (a f)", p=P)
        for k in range(FS):
            sp.dma("zero_out", flat[:, k * C2:(k + 1) * C2], zeros[:, :])
        sp.dma("zero_out", code_rows, zeros[:, :])
        made["zero_out"] = sp.dma("zero_out", run_d[P * C1:P * C1 + 1, :], zeros[0:1, 0:D])
        yield
        freed, squared = {}, {}
        act.wait(low, consts, ("dve_done", dve.n))
        turn = [0]

        def hot(b0, n, slot, on_act):
            q = dve if not on_act else act
            for k in range(slot, slot + n // GB):
                dve.wait(*freed.get(k, ()))
                q.wait(*freed.get(k, ()))
            o = oh[:, slot:slot + n // GB, :, :].rearrange("p a b c -> p (a b) c")
            h = dhh[:, slot:slot + n // GB, :, :].rearrange("p a b c -> p (a b) c")
            if on_act:
                w = turn[0] % 2
                turn[0] += 1
                act.wait(squared.get(w, low))
                for k in range(n):
                    m = act.run(S.activation(dsq[:, w, k, :], iota_b[:, :], ACT.Square,
                                             bias=dlneg[:, b0 + k:b0 + k + 1], scale=1.0))
                act.wait(m)
                squared[w] = m1 = act.run(S.activation(o, dsq[:, w, 0:n, :], ACT.Relu, bias=ones[:, 0:1], scale=-1.0))
            else:
                for k in range(n):
                    m1 = dve.run(V.tensor_scalar(o[:, k, :], iota_b[:, :], dlneg[:, b0 + k:b0 + k + 1], 0.0,
                                                 ALU.add, ALU.is_equal))
            m2 = dve.run(V.tensor_tensor(h, iota_b[:, None, 0:NT].broadcast_to([P, n, NT]),
                                         dh[:, b0:b0 + n, None].broadcast_to([P, n, NT]), ALU.is_equal))
            return m1, m2

        n = 2 * GB
        for i in range(C2 // n):
            slot = i % 2 * 2
            pe.wait(*hot(i * n, n, slot, i % 2 == 0))
            for k in range(n):
                m = pe.run(T.matmul(bank[5][:, 0:NT], oh[:, slot + k // GB, k % GB, :],
                                    dhh[:, slot + k // GB, k % GB, :],
                                    start=(i == 0 and k == 0), stop=(i == C2 // n - 1 and k == n - 1)))
            freed[slot] = freed[slot + 1] = (m,)
            yield
        dve.wait(m)
        m = vrun(V.tensor_copy(smt[:, 6, :], bank[5][:, 0:NT]))
        pe.wait(m)
        pe.run(T.matmul(bank[5][:, 64:64 + NT], before[:, :], smt[:, 6, :], start=True, stop=True))
        m = pe.run(T.matmul(bank[5][:, 128:128 + NT], ones[:, :], smt[:, 6, :], start=True, stop=True))
        dve.wait(m)
        vrun(V.tensor_copy(smt[:, 7, :], bank[5][:, 128:128 + NT]))
        vrun(V.tensor_tensor_scan(hinit[:, :], ones[:, 0:NT], smt[:, 7, :], 0.0, ALU.mult, ALU.add))
        vrun(V.tensor_tensor(hinit[:, :], hinit[:, :], smt[:, 7, :], ALU.subtract))
        first_place = vrun(V.tensor_tensor(hinit[:, :], hinit[:, :], bank[5][:, 64:64 + NT], ALU.add))
        yield
        made["counted"] = True
        vrun(V.tensor_scalar(has_f[:, :], smt[:, 6, :], 0.5, None, ALU.is_gt))
        vrun(V.tensor_scalar(smt[:, 7, :], has_f[:, :], -float(FAR), float(FAR), ALU.mult, ALU.add))
        vrun(V.tensor_tensor(idx_s[:, :], smt[:, 7, :], hinit[:, :], ALU.add))
        vrun(V.tensor_tensor(smt[:, 6, :], smt[:, 6, :], hinit[:, :], ALU.add))
        vrun(V.tensor_scalar(idx_f[:, :], smt[:, 6, :], -1.0, 0.0, ALU.add, ALU.max))
        yield

        turned, spread, counted, hsum, eqs, masked, looked, ends = {}, {}, {}, {}, {}, {}, {}, {}
        moved = {}
        pe.wait(first_place)

        def prev_hist(i):
            return hinit[:, :] if i == 0 else hist[:, (i - 1) % 4, GB - 1, :]

        waiting = []

        def add_moved():
            b, turn, m = waiting.pop(0)
            pe.wait(m)
            for half, bk in ((0, bank[0]), (1, bank[5])):
                m2 = pe.run(T.matmul(bk[:, 0:HC], row_hot[:, turn, half, :], col_hot[:, turn, :],
                                     start=(b == POOL_MOVES), stop=(b == C2 - 1)))
            moved[turn] = (m2,)
            made["moved"] = m2

        def move(b0):
            w = b0 // PB % 2
            dve.wait(ends[(b0 + PB) // GB - 1])
            at = place[:, b0:b0 + PB]
            vrun(V.tensor_single_scalar(rc_i[:, 0, :], at, HC.bit_length() - 1, ALU.logical_shift_right))
            vrun(V.tensor_single_scalar(rc_i[:, 1, :], at, HC - 1, ALU.bitwise_and))
            rc_at = vrun(V.tensor_copy(rc[:, w, :, :], rc_i[:, :, :]))
            yield
            for k in range(POOL_MOVES, PB):
                b = b0 + k
                turn = nth[0] % MR
                nth[0] += 1
                dve.wait(*moved.get(turn, ()))
                dve.run(V.tensor_scalar(row_hot[:, turn, :, :], half_h[:, :, :], rc[:, w, 0, k:k + 1],
                                        code[:, b:b + 1], ALU.is_equal, ALU.mult))
                m = dve.run(V.tensor_scalar(col_hot[:, turn, :], iota_h[:, :], rc[:, w, 1, k:k + 1], None,
                                            ALU.is_equal))
                waiting.append((b, turn, m))
                if len(waiting) > MOVE_LAG:
                    add_moved()
                yield

        movers, nth = [], [0]

        def move_some(count):
            while movers and count:
                try:
                    next(movers[0])
                    count -= 1
                    yield
                except StopIteration:
                    movers.pop(0)

        def hot_rows(i):
            if i >= DR:
                freed[i % DR] = (looked[i - DR], ends[i - DR])
            made["hot", i] = hot(i * GB, GB, i % DR, True)

        def turn_blocks(i):
            pe.wait(*made["hot", i])
            if i >= 1:
                pe.wait(*spread[i - 1])
            for k in range(GB):
                m = pe.run(T.transpose(bank_t[:, k, :], oh[:, i % DR, k, :], ident_b[:, :]))
            turned[i] = m
            if i >= 1:
                pe.wait(hsum[i - 1])
            for k in range(GB):
                for j in range(k + 1):
                    m = pe.run(T.matmul(bank[3][:, k * NT:(k + 1) * NT], oh[:, i % DR, j, :],
                                        dhh[:, i % DR, j, :], start=(j == 0), stop=(j == k)))
            counted[i] = m
            act.wait(turned[i])
            if i >= 2:
                act.wait(eqs[i - 2])
            if i >= 4:
                act.wait(looked[i - 4])
            spread[i] = (act.run(S.activation(ohtb[:, i % 2, :, :], bank_t[:, :, :], ACT.Copy)),
                         act.run(S.activation(oht[:, i % 4, :, :], bank_t[:, :, :], ACT.Copy)))

        def compare(i):
            pe.wait(spread[i][0])
            if i >= 2:
                pe.wait(masked[i - 2])
            for k in range(GB):
                o = bank[1 + i % 2][:, k * P:(k + 1) * P]
                pe.run(T.matmul(o, ohtb[:, i % 2, k, :], ohtb[:, i % 2, k, :], start=True, stop=False))
                m = pe.run(T.matmul(o, ident_b[:, :], not_before[:, :], start=False, stop=True))
            eqs[i] = m
            act.wait(eqs[i])
            if i >= 3:
                act.wait(looked[i - 3])
            masked[i] = act.run(S.activation(eqm[:, i % 3, :, :],
                                             bank[1 + i % 2][:, :].rearrange("p (k e) -> p k e", k=GB), ACT.Relu))

        def add_counts(i):
            dve.wait(counted[i])
            if i >= 1:
                dve.wait(hsum[i - 1])
            if i >= 3:
                dve.wait(looked[i - 3])
            if i >= 4:
                dve.wait(looked[i - 4])
            hsum[i] = dve.run(V.tensor_tensor(
                hist[:, i % 4, :, :], bank[3][:, 0:GB * NT].rearrange("p (k t) -> p k t", k=GB),
                prev_hist(i)[:, None, :].broadcast_to([P, GB, NT]), ALU.add))

        def look_up(n):
            pe.wait(masked[n], hsum[n])
            if n >= 1:
                pe.wait(made["prod", n - 1])
            for k in range(GB):
                o = bank[4][:, k * NT:(k + 1) * NT]
                so_far = prev_hist(n) if k == 0 else hist[:, n % 4, k - 1, :]
                pe.run(T.matmul(o, oht[:, n % 4, k, :], so_far, start=True, stop=False))
                m = pe.run(T.matmul(o, eqm[:, n % 3, k, :], dhh[:, n % DR, k, :], start=False, stop=True))
            looked[n] = m

        for i in range(NG + 4):
            if i < NG:
                hot_rows(i)
            yield
            if i >= 4:
                n = i - 4
                dve.wait(looked[n])
                if n >= 1:
                    dve.wait(ends[n - 1])
                made["prod", n] = dve.run(V.tensor_tensor(
                    prod[:, :, :], bank[4][:, 0:GB * NT].rearrange("p (k t) -> p k t", k=GB),
                    dhh[:, n % DR, :, :], ALU.mult))
            if 3 <= i < NG + 3:
                look_up(i - 3)
            if 1 <= i <= NG:
                turn_blocks(i - 1)
            if 2 <= i < NG + 2:
                compare(i - 2)
            yield from move_some(2)
            if 1 <= i <= NG:
                add_counts(i - 1)
            if i >= 4:
                dve.wait(made["prod", n])
                with nc.allow_low_precision(reason="whole numbers under 2^24"):
                    ends[n] = dve.run(V.tensor_reduce(place[:, n * GB:(n + 1) * GB], prod[:, :, :], AXX, ALU.add))
                if (n + 1) * GB % PB == 0:
                    b0 = (n + 1) * GB - PB
                    scatters.extend((here[0], b0 + k, ends[n]) for k in range(POOL_MOVES))
                    movers.append(move(b0))
            yield from move_some(2 if i % LESS else 1)
        made["ranked"] = True
        yield
        scatter(NCH)
        yield from move_some(-1)
        while waiting:
            add_moved()
        sp.wait(made["scattered"])
        m = sp.dma("code_in", zeros[:, :], code_rows)
        dve.wait(m, made["moved"])
        half_bits = place[:, 0:C2 // 2].bitcast(F16)
        dve.run(V.tensor_tensor(half_bits[:, 0:512], bank[0][:, :], zeros[:, 0:512], ALU.add))
        vrun(V.tensor_tensor(half_bits[:, 512:1024], bank[5][:, :], zeros[:, 512:1024], ALU.add))
        made["sorted"] = vrun(V.tensor_scalar(srt[:, :], half_bits.bitcast(I16), -1024, None, ALU.add))

    work = rows[:, :, :].bitcast(F32)
    SELF0 = 2 + NT + 4
    xw_in, xw_turned, xw_tin, xw_out, xw_at, xw_stored = {}, {}, {}, {}, {}, {}

    def own_term(n):
        t = n
        if t < NT:
            if t == 0:
                sp.wait(found[-1], *xn_out)
                pe.wait(w_in, graph_at)
            else:
                sp.wait(*([xw_turned[t - 2]] if t >= 2 else []))
            xw_in[t] = sp.dma(f"xw_in{t % 2}", work[:, t % 2, 0:D], xn_d[t * P:(t + 1) * P, :])
        t = n - 1
        if 0 <= t < NT:
            pe.wait(xw_in[t])
            if t >= 1:
                pe.wait(xw_at[t - 1])
            for k in range(KD):
                m = pe.run(T.transpose(bank[6][:, k * P:(k + 1) * P], work[:, t % 2, k * P:(k + 1) * P], ident[:, :]))
            xw_turned[t] = m
            act.wait(m)
            if t >= 2:
                act.wait(xw_out[t - 2])
            xw_tin[t] = act.run(S.activation(work[:, t % 2, D:2 * D], bank[6][:, 0:D], ACT.Copy))
            pe.wait(xw_tin[t])
            for k in range(KD):
                m = pe.run(T.matmul(bank[6][:, D:2 * D], work[:, t % 2, D + k * P:D + (k + 1) * P], wself[:, k, :],
                                    start=(k == 0), stop=(k == KD - 1)))
            xw_out[t] = m
            act.wait(m)
            if t >= 2:
                act.wait(xw_stored[t - 2])
            xw_at[t] = act.run(S.activation(work[:, t % 2, 2 * D:3 * D], bank[6][:, D:2 * D], ACT.Copy))
            sp.wait(xw_at[t])
            xw_stored[t] = sp.dma(f"xw_out{t % 2}", self_d[t * P:(t + 1) * P, :], work[:, t % 2, 2 * D:3 * D])

    sort = sort_steps()
    pool.wait(src_in, pad_e, *xn_out)
    summed, stored = {}, {}
    prev = None
    paced = 0
    for c in range(NCH):
        s = c % RING
        if c >= RING:
            pool.wait(stored[c - RING], summed[c - RING + 1][0])
        for k in range(JC):
            j = c * JC + k
            got = pool.sent(f"gather{s}", G.indirect_dma_start(
                out=ring[:, s, k, :], out_offset=None, in_=xn_d, in_offset=at_rows(srci[:, j:j + 1])))
        here[0] = c
        scatter(c - RING + 2)
        if 2 <= c < 2 + NT:
            search(c - 2)
        marks_c = []
        for k in range(JC):
            j = c * JC + k
            dve.wait(got)
            if j > 0:
                dve.wait(prev[1])
                prev_row = prev[0]
                m = dve.run(V.scalar_tensor_tensor(out=ring[:, s, k, :], in0=prev_row, scalar=same_g[:, j:j + 1],
                                                   in1=ring[:, s, k, :], op0=ALU.mult, op1=ALU.add))
                prev = (ring[:, s, k, :], m)
            else:
                m = pad_e
                prev = (ring[:, s, k, :], m)
            marks_c.append(m)
            paced += PACE1 if not made.get("counted") else PACE2
            while paced >= 1 and "ranked" not in made:
                next(sort, None)
                paced -= 1
        summed[c] = (marks_c[0] if c else marks_c[1], marks_c[-1])
        sp.wait(summed[c][1])
        stored[c] = sp.dma(f"stored{s}", run_rows[:, c * JC:(c + 1) * JC, :],
                           ring[:, s, :, :])
        if c == 2 + NT:
            graph_at = graph_ends()
        if c >= SELF0:
            own_term(c - SELF0)

    def row_ends(count, row0, head, last, pos_i, far_i):
        m = vrun(V.tensor_scalar(sm[:, 9:10], head, 1.0, None, ALU.add))
        pe.wait(m)
        m = pe.run(T.matmul(bank[6][:, 400:401], up1[:, :], sm[:, 9:10], start=True, stop=True))
        dve.wait(m)
        vrun(V.tensor_scalar(sm[:, 10:11], bank[6][:, 400:401], -1.0, None, ALU.add))
        vrun(V.tensor_tensor(sm[:, 11:12], head, last, ALU.is_equal))
        vrun(V.tensor_tensor(sm[:, 12:13], head, sm[:, 10:11], ALU.is_equal))
        vrun(V.tensor_tensor(sm[:, 11:12], sm[:, 11:12], sm[:, 12:13], ALU.mult))
        vrun(V.tensor_copy(sm[:, 13:14], row0))
        vrun(V.scalar_tensor_tensor(out=sm[:, 13:14], in0=count, scalar=-1.0, in1=sm[:, 13:14],
                                    op0=ALU.add, op1=ALU.add))
        vrun(V.scalar_tensor_tensor(out=sm[:, 14:15], in0=sm[:, 11:12], scalar=float(FAR), in1=sm[:, 13:14],
                                    op0=ALU.mult, op1=ALU.add))
        vrun(V.tensor_copy(pos_i, sm[:, 13:14]))
        return vrun(V.tensor_copy(far_i, sm[:, 14:15]))

    dve.wait(found[-1], xw_stored[NT - 1], xw_stored[NT - 2], xw_at[NT - 1])
    vrun(V.tensor_scalar(rows[:, 0, :].bitcast(F32), dsti[:, :], sm[:, 0:1], None, ALU.is_equal))
    vrun(V.tensor_reduce(sm[:, 8:9], rows[:, 0, :].bitcast(F32), AXX, ALU.add))
    fix_at = row_ends(sm[:, 8:9], row_at[:, 0:1], sm[:, 0:1], sm[:, 1:2], smi[:, 0:1], smi[:, 1:2])
    m = broadcast_cols(sm[:, 0:1], (), bank[6][:, 0:P])
    dve.wait(m)
    m = vrun(V.scalar_tensor_tensor(out=tmask[:, :], in0=bank[6][:, 0:P], scalar=sm[:, 1:2], in1=before[:, :],
                                    op0=ALU.is_equal, op1=ALU.mult))
    sums_done = ("dve_done", dve.n)
    pe.wait(m, summed[NCH - 1][1])
    carried = pe.run(T.matmul(bank[6][:, 0:D], tmask[:, :], prev[0], start=True, stop=True))
    pool.wait(fix_at, *(stored[c] for c in range(NCH - RING, NCH)))
    m = pool.sent("fix_in", G.indirect_dma_start(out=cfix[:, :], out_offset=None, in_=run_d,
                                                 in_offset=at_rows(smi[:, 0:1])))
    while "ranked" not in made:
        next(sort)
    for _ in range(FIX_MOVES):
        next(sort, None)
    dve.wait(m, carried)
    m = vrun(V.tensor_tensor(cfix[:, :], cfix[:, :], bank[6][:, 0:D], ALU.add))
    pool.wait(m)
    run_fixed = pool.sent("fix_out", G.indirect_dma_start(
        out=run_d[0:P * C1 + 1, :], out_offset=at_rows(smi[:, 1:2]), in_=cfix[:, :], in_offset=None,
        bounds_check=P * C1 - 1, oob_is_err=False))

    for _ in range(FIX_MOVES):
        next(sort, None)

    pool.wait(run_fixed, graph_at, made["zero_out"])
    r3_free = [("dve_done", dve.n), ("pe_done", pe.n), ("act_done", act.n), made["zero_out"]]
    for e in (pool, sp, act, pe, dve):
        e.wait(*(m for m in r3_free if m[0] != e.name))
    agg_in, own_in, turned_in, tin_at, out_at, x1_at, x1_out = {}, {}, {}, {}, {}, {}, {}
    scaled, x2_at, x2_turned, xt_at, h_at, xt_out, feat_at, summed_own = {}, {}, {}, {}, {}, {}, {}, {}
    chunk_of = lambda t: t // 4
    last_of = lambda c: min(4 * c + 3, NT - 1)

    def fetch(t):
        if t >= 4:
            pool.wait(turned_in[t - 4])
            sp.wait(x1_at[t - 4])
        agg_in[t] = pool.sent(f"agg_in{t % 4}", G.indirect_dma_start(
            out=agg[:, t % 4, :], out_offset=None, in_=run_d, in_offset=at_rows(idx_g[:, t:t + 1])))
        own_in[t] = sp.dma(f"own_in{t % 4}", own[:, t % 4, :], self_d[t * P:(t + 1) * P, :])

    def turn_rows(t):
        pe.wait(agg_in[t])
        if t >= 2:
            pe.wait(tin_at[t - 2])
        tb = bank[1 + t % 2]
        for k in range(KD):
            m = pe.run(T.transpose(tb[:, k * P:(k + 1) * P], agg[:, t % 4, k * P:(k + 1) * P], ident[:, :]))
        turned_in[t] = m
        act.wait(m)
        if t >= 2:
            act.wait(out_at[t - 2])
        tin_at[t] = act.run(S.activation(tin[:, t % 2, :, :], tb[:, 0:D].rearrange("p (k n) -> p k n", k=KD), ACT.Copy))

    def layer(t):
        pe.wait(tin_at[t])
        if t >= 2:
            pe.wait(summed_own[t - 2])
        o = bank[3 + t % 2][:, 0:D]
        for k in range(KD):
            m = pe.run(T.matmul(o, tin[:, t % 2, k, :], wmsg[:, k, :], start=(k == 0), stop=(k == KD - 1)))
        out_at[t] = m
        dve.wait(m, own_in[t])
        o_own = own[:, t % 4, :]
        summed_own[t] = dve.run(V.tensor_tensor(o_own, o, o_own, ALU.add))

    def statistics(t, after):
        if t >= 0:
            dve.wait(x1_at[t])
            m = dve.run(V.bn_stats(stat[:, t % 4, :], xs[:, t, :]))
        if after < NT:
            dve.wait(summed_own[after])
            x1_at[after] = dve.run(V.scalar_tensor_tensor(
                out=xs[:, after, :], in0=own[:, after % 4, :], scalar=0.0, in1=xs[:, after, :],
                op0=ALU.max, op1=ALU.add))
            sp.wait(x1_at[after])
            x1_out[after] = sp.dma("x1_out", x1_d[after * P:(after + 1) * P, :], xs[:, after, :])
        if t >= 0:
            dve.wait(m)
            stat_at[t] = dve.run(V.bn_aggr(aggr[:, t, :], stat[:, t % 4, :]))

    stat_at = {}

    def scalars(t):
        if t == last_of(chunk_of(t)):
            dve.wait(stat_at[t])
            scaled[chunk_of(t)] = norm_scalars(aggr[:, 4 * chunk_of(t):t + 1, :])

    def norm(t):
        c, w = chunk_of(t), t % 4
        act.wait(scaled[c])
        if t >= 2:
            act.wait(x2_turned[t - 2])
        x2_at[t] = act.run(S.activation(x2[:, t % 2, :], xs[:, t, :], ACT.Identity, bias=aggr[:, t, 0:1],
                                        scale=aggr[:, t, 1:2]))
        pe.wait(x2_at[t])
        if t >= 1:
            pe.wait(xt_at[t - 1])
        for k in range(KD):
            m = pe.run(T.transpose(bank[6][:, k * P:(k + 1) * P], x2[:, t % 2, k * P:(k + 1) * P], ident[:, :]))
        x2_turned[t] = m
        act.wait(m)
        if w == 0 and c >= 2:
            act.wait(xt_out[c - 2], h_at[last_of(c - 2)])
        xt_at[t] = act.run(S.activation(xt[:, c % 2, :, w * P:(w + 1) * P],
                                        bank[6][:, 0:KD * P].rearrange("p (k n) -> p k n", k=KD), ACT.Copy))

    def heads(t):
        c, w = chunk_of(t), t % 4
        pe.wait(xt_at[t])
        hb = bank[7]
        if w == 0 and c >= 1:
            pe.wait(feat_at[c - 1])
        for k in range(KD):
            m = pe.run(T.matmul(hb[:, w * HX:(w + 1) * HX], xt[:, c % 2, k, w * P:(w + 1) * P], wgat[:, k, :],
                                start=(k == 0), stop=(k == KD - 1)))
        h_at[t] = m
        if t == last_of(c):
            sp.wait(xt_at[t])
            xt_out[c] = sp.dma(f"xt_out{c % 2}", xT_d[:, :, c * 4 * P:c * 4 * P + (w + 1) * P],
                               xt[:, c % 2, :, 0:(w + 1) * P])
            n = w + 1
            dve.wait(m)
            fc = feat[:, 4 * c:4 * c + n, :]
            feat_at[c] = vrun(V.tensor_copy(fc[:, :, 0:HX], hb[:, 0:n * HX].rearrange("p (t f) -> p t f", t=n)))
            scr = [cfix[:, 64 * k:64 * k + n * HX].rearrange("p (t f) -> p t f", t=n) for k in range(2)]
            for k in range(2):
                m = dve.run(V.tensor_tensor(scr[k], fc[:, :, 0:HX],
                                            attb[:, k:k + 1, :].broadcast_to([P, n, HX]), ALU.mult))
            dve.wait(m)
            for k in range(2):
                m = dve.run(V.tensor_reduce(fc[:, :, HX + HEADS * k:HX + HEADS * (k + 1)],
                                            scr[k].rearrange("p t (h e) -> p t h e", h=HEADS), AXX, ALU.add))
            dve.wait(m)
            features[c] = m
            sp.wait(m)
            with nc.allow_non_contiguous_dma(reason="rows of the table"):
                for lane, table, lo, hi in (("tab_out", tab_d, 0, FE), ("node_out", node_d, FE, FG)):
                    made[lane] = sp.dma(lane, table[4 * c * P:(4 * c + n) * P, :].rearrange("(t p) f -> p t f", p=P),
                                        fc[:, :, lo:hi])
            if c >= 1:
                start(c - 1)

    features = {}

    def start(c):
        pool.wait(features[c])
        for t in range(4 * c, last_of(c) + 1):
            made["start_out"] = pool.sent("start_out", G.indirect_dma_start(
                out=start_d, out_offset=at_rows(idx_s[:, t:t + 1]), in_=feat[:, t, FE:FG + 1], in_offset=None,
                bounds_check=E2 - 1, oob_is_err=False))

    def load_weights():
        sp.wait(got, sums_done, found[-1], dst_out)
        for e in range(NX):
            sp.dma("w12_in", w1s[:, e, :, :], W1[e].rearrange("(k p) f -> p k f", p=P))
            made["w12_in"] = sp.dma("w12_in", w2s[:, e, :, :], W2[e].rearrange("(f p) n -> p f n", p=P))

    pe.wait(w_in)
    dve.wait(w_in)
    act.wait(w_in)
    sp.wait(xw_stored[NT - 1], xw_stored[NT - 2])
    for t in range(4):
        fetch(t)
    for t in range(NT + LAG + 2):
        if t == W_AT:
            load_weights()
        if t < NT:
            turn_rows(t)
        if 1 <= t <= NT:
            layer(t - 1)
        if 1 <= t <= NT + 1:
            statistics(t - 2, t - 1)
            if t + 3 < NT:
                fetch(t + 3)
        if 4 <= t < NT + 4:
            scalars(t - 4)
        for _ in range(OUT_MOVES):
            next(sort, None)
        if LAG <= t < NT + LAG:
            norm(t - LAG)
        if LAG + 1 <= t < NT + LAG + 1:
            heads(t - LAG - 1)
    for _ in sort:
        pass
    start(chunk_of(NT - 1))
    tab_out, node_out, start_out = made["tab_out"], made["node_out"], made["start_out"]

    def expert_steps():
        chunks = [(c * 4, min(4, NT - c * 4)) for c in range(-(-NT // 4))]
        jobs = [(c, e) for c in range(len(chunks)) for e in range(NX)]
        loaded, activated, projected, y_used, y_out, l1_used = {}, {}, {}, {}, {}, {}
        sp.wait(("pe_done", pe.n), *(xt_out[c] for c in range(len(chunks))))
        pe.wait(("dve_done", dve.n), ("act_done", act.n), made["w12_in"])
        act.wait(("pe_done", pe.n), ("dve_done", dve.n))
        ny = 0
        nl = 0

        def load(c):
            t0, n = chunks[c]
            if c >= 2:
                sp.wait(projected[(c - 2, "l1")])
            loaded[c] = sp.dma(f"xt_in{c % 2}", xt[:, c % 2, :, 0:n * P], xT_d[:, :, t0 * P:(t0 + n) * P])

        load(0)
        load(1)
        for i in range(len(jobs) + 1):
            if i < len(jobs):
                c, e = jobs[i]
                t0, n = chunks[c]
                if e == 0 and 1 <= c and c + 1 < len(chunks):
                    load(c + 1)
                pe.wait(loaded[c])
                if i >= 2:
                    act.wait(projected[i - 2])
                for f in range(KF):
                    if nl >= 2:
                        pe.wait(l1_used[nl - 2])
                    o = bank[nl % 2][:, 0:n * P]
                    for k in range(KD):
                        m = pe.run(T.matmul(o, w1s[:, e, k, f * P:(f + 1) * P], xt[:, c % 2, k, 0:n * P],
                                            start=(k == 0), stop=(k == KD - 1)))
                    act.wait(m)
                    l1_used[nl] = act.run(S.activation(hh[:, i % 2, f, 0:n * P], o, ACT.Gelu,
                                                       bias=b1c[:, e, f:f + 1], scale=1.0))
                    nl += 1
                activated[i] = l1_used[nl - 1]
                if e == NX - 1:
                    projected[(c, "l1")] = m
            if i >= 1:
                c, e = jobs[i - 1]
                t0, n = chunks[c]
                pe.wait(activated[i - 1])
                for k in range(n):
                    if ny >= 2:
                        pe.wait(y_used[ny - 2])
                    o = bank[2 + ny % 2][:, 0:D]
                    for f in range(KF):
                        m = pe.run(T.matmul(o, hh[:, (i - 1) % 2, f, k * P:(k + 1) * P], w2s[:, e, f, :],
                                            start=(f == 0), stop=(f == KF - 1)))
                    dve.wait(m)
                    if ny >= 4:
                        dve.wait(y_out[ny - 4])
                    y_used[ny] = dve.run(V.tensor_tensor(yo[:, ny % 4, :], o, b2b[:, e, :], ALU.add))
                    sp.wait(y_used[ny])
                    y_out[ny] = sp.dma(f"y_out{ny % 4}", y_d[e, (t0 + k) * P:(t0 + k + 1) * P, :], yo[:, ny % 4, :])
                    ny += 1
                    yield
                projected[i - 1] = m
        made["y_out"] = [y_out[ny - 1 - k] for k in range(4)]

    def matrix_gathers():
        dve.wait(x1_out[NT - 1], ("act_done", act.n), ("pe_done", pe.n))
        source = srt[:, 0:PE_COLS]
        for k, (op, by) in enumerate(((ALU.bitwise_and, P - 1), (ALU.logical_shift_right, P.bit_length() - 1))):
            vrun(V.tensor_single_scalar(digit_i[:, :], source, by, op))
            vrun(V.tensor_copy(digits[:, k, :], digit_i[:, :]))
        table = feat[:, :, 0:FE].rearrange("p t f -> p f t")
        rest = picked[:, 0, :, :]
        vrun(V.tensor_copy(tab_parts[:, 0, :, :], table))
        vrun(V.tensor_tensor(rest, table, tab_parts[:, 0, :, :], ALU.subtract))
        vrun(V.tensor_copy(tab_parts[:, 1, :, :], rest))
        vrun(V.tensor_tensor(rest, rest, tab_parts[:, 1, :, :], ALU.subtract))
        split = vrun(V.tensor_copy(tab_parts[:, 2, :, :], rest))
        pe.wait(split)
        HF = FE // 2
        hots, turned_, copied, product, taken = {}, {}, {}, {}, {}
        for i in range(PE_COLS + 4):
            if i < PE_COLS:
                if i >= 2:
                    dve.wait(turned_[i - 2])
                dve.run(V.tensor_scalar(high_hot[:, i % 5, :], iota_b[:, 0:NT], digits[:, 1, i:i + 1], None,
                                        ALU.is_equal))
                hots[i] = dve.run(V.tensor_scalar(low_hot[:, i % 2, :], iota_b[:, :], digits[:, 0, i:i + 1], None,
                                                  ALU.is_equal))
            n = i - 1
            if 0 <= n < PE_COLS:
                pe.wait(hots[n])
                if n >= 1:
                    pe.wait(copied[n - 1])
                turned_[n] = pe.run(T.transpose(bank_t[:, 0, :], low_hot[:, n % 2, :], ident_b[:, :]))
                act.wait(turned_[n])
                if n >= 2:
                    act.wait(product[n - 2, 1])
                copied[n] = act.run(S.activation(low_turned[:, n % 2, :], bank_t[:, 0, :], ACT.Copy))
            for half in range(2):
                n = i - 2
                if 0 <= n < PE_COLS:
                    pe.wait(copied[n])
                    u = 2 * n + half
                    if u >= 3:
                        pe.wait(taken[u - 3])
                    for k in range(3):
                        m = pe.run(T.matmul(bank[4 + u % 3][:, 0:HF * NT], low_turned[:, n % 2, :],
                                            tab_parts[:, k, half * HF:(half + 1) * HF, :].rearrange("p f t -> p (f t)"),
                                            start=(k == 0), stop=(k == 2)))
                    product[n, half] = m
                n = i - 3
                if 0 <= n < PE_COLS:
                    u = 2 * n + half
                    dve.wait(product[n, half])
                    if n >= 2:
                        dve.wait(taken["sum", n - 2])
                    taken[u] = dve.run(V.tensor_tensor(
                        picked[:, n % 2, half * HF:(half + 1) * HF, :],
                        bank[4 + u % 3][:, 0:HF * NT].rearrange("p (f t) -> p f t", f=HF),
                        high_hot[:, n % 5, None, :].broadcast_to([P, HF, NT]), ALU.mult))
                yield
            n = i - 4
            if 0 <= n < PE_COLS:
                dve.wait(taken[2 * n + 1])
                taken["sum", n] = dve.run(V.tensor_reduce(g[:, n, 0:FE], picked[:, n % 2, :, :], AXX, ALU.add))
            yield

    pool.wait(made["sorted"], tab_out, x1_out[NT - 1])
    feat_in = {}

    def gather_features(c):
        for j in range(max(c * FC, PE_COLS), (c + 1) * FC):
            feat_in[c] = pool.sent(f"feat_in{c}", G.indirect_dma_start(
                out=g[:, j, 0:FE], out_offset=None, in_=tab_d, in_offset=at_rows(srt[:, j:j + 1])))

    gather_features(0)
    for c in range(1, LATE):
        gather_features(c)

    matrix_steps = matrix_gathers()
    owed = 0
    for _ in expert_steps():
        owed += 3 * (PE_COLS + 4) / (NT * NX)
        while owed >= 1:
            next(matrix_steps, None)
            owed -= 1
    for _ in matrix_steps:
        pass

    mlp_done = [("pe_done", pe.n), ("act_done", act.n), *made["y_out"]]
    sp.wait(start_out, ("dve_done", dve.n), *mlp_done)
    m = sp.dma("edge_in", edge_n[:, :, :].rearrange("p j f -> p (j f)"), start_d.rearrange("(p j) f -> p (j f)", p=P))
    dve.wait(m, *mlp_done)
    ids, a_dest = edge_n[:, :, HEADS], edge_n[:, :, 0:HEADS]
    HEAD, LAST = sm[:, 0:1], sm[:, 1:2]
    vrun(V.tensor_scalar(same_f[:, :], ids, 0.0, None, ALU.is_equal))
    vrun(V.tensor_scalar(reset_f[:, 0:C2], ids, 0.0, -BIG, ALU.is_gt, ALU.mult))
    vrun(V.tensor_reduce(sm[:, 2:3], ids, AXX, ALU.max))
    m = broadcast_cols(sm[:, 2:3], (), bank[6][:, 0:P])
    pe.wait(m)
    m = pe.run(T.transpose(bank[5][:, 0:P], before[:, :], ident[:, :]))
    dve.wait(m)
    vrun(V.tensor_copy(segm[:, 1, :], bank[5][:, 0:P]))
    vrun(V.tensor_tensor(segm[:, 0, :], bank[6][:, 0:P], segm[:, 1, :], ALU.mult))
    vrun(V.tensor_reduce(sm[:, 3:4], segm[:, 0, :], AXX, ALU.max))
    vrun(V.tensor_tensor(HEAD, edge_n[:, 0:1, HEADS], sm[:, 3:4], ALU.max))
    vrun(V.tensor_tensor(LAST, sm[:, 2:3], sm[:, 3:4], ALU.max))
    m = vrun(V.tensor_scalar(smi[:, 4:5], HEAD, -1.0, None, ALU.add))
    pool.wait(m, node_out)
    m_row = pool.sent("row_in", G.indirect_dma_start(out=sm[:, 80:84], out_offset=None, in_=node_d,
                                                     in_offset=at_rows(smi[:, 4:5])))
    for c in range(LATE, NCF):
        gather_features(c)
    vrun(V.tensor_tensor_scan(id_run[:, :], ids, ids, HEAD, ALU.max, ALU.max))
    vrun(V.tensor_scalar(first_f[:, :], id_run[:, :], HEAD, None, ALU.is_equal))
    vrun(V.tensor_reduce(sm[:, 8:9], first_f[:, :], AXX, ALU.add))
    fix_f = row_ends(sm[:, 8:9], row_at[:, 1:2], HEAD, LAST, smi[:, 2:3], smi[:, 3:4])
    m = broadcast_cols(LAST, (), bank[6][:, 0:P])
    dve.wait(m)
    vrun(V.scalar_tensor_tensor(out=segm[:, 0, :], in0=bank[6][:, 0:P], scalar=HEAD, in1=segm[:, 1, :],
                                op0=ALU.is_equal, op1=ALU.mult))
    vrun(V.tensor_scalar(segm[:, 1, :], segm[:, 0, :], -1.0, BIG, ALU.add, ALU.mult))
    dve.wait(m_row)
    for f in range(HEADS):
        m = dve.run(V.tensor_tensor_scan(edge_n[:, :, f], same_f[:, :], edge_n[:, :, f], sm[:, 80 + f:81 + f],
                                         ALU.mult, ALU.add))
    dve.wait(m)

    exps, summed_f, stored_f = {}, {}, {}
    sum_rows = sum_d.rearrange("(p j) f -> p j f", p=P)

    def weigh(c):
        a, b = c * FC, (c + 1) * FC
        e_, top_, st = g[:, a:b, HX:FE], g[:, a:b, FE:FG], step[:, c % 2, :, :]
        dve.wait(*([feat_in[c]] if c in feat_in else []))
        vrun(V.tensor_tensor(e_, e_, a_dest[:, a:b, :], ALU.add))
        vrun(V.scalar_tensor_tensor(out=e_, in0=e_, scalar=0.2, in1=e_, op0=ALU.mult, op1=ALU.max))
        for h in range(HEADS):
            m = dve.run(V.tensor_tensor_scan(g[:, a:b, FE + h], reset_f[:, a:b], g[:, a:b, HX + h],
                                             -BIG if c == 0 else g[:, a - 1:a, FE + h], ALU.add, ALU.max))
        if c >= 2:
            dve.wait(summed_f[c - 2])
        if c == 0:
            dve.run(V.memset(st[:, 0:1, :], -BIG))
            dve.wait(m)
            vrun(V.tensor_tensor(st[:, 1:FC, :], g[:, a:b - 1, FE:FG], g[:, a + 1:b, FE:FG], ALU.subtract))
        else:
            dve.wait(m)
            vrun(V.tensor_tensor(st, g[:, a - 1:b - 1, FE:FG], top_, ALU.subtract))
        dve.run(V.tensor_tensor(e_, e_, top_, ALU.subtract))
        m = vrun(V.tensor_scalar(st, st, 0.0, None, ALU.min))
        act.wait(m)
        act.run(S.activation(st, st, ACT.Exp))
        exps[c] = act.run(S.activation(e_, e_, ACT.Exp))

    def sum_up(c):
        a, b = c * FC, (c + 1) * FC
        st = step[:, c % 2, :, :]
        dve.wait(exps[c])
        m = dve.run(V.tensor_tensor(st, st, same_f[:, a:b, None].broadcast_to([P, FC, HEADS]), ALU.mult))
        for h in range(HEADS):
            o = g[:, a:b, h * NX:(h + 1) * NX]
            m = dve.run(V.tensor_tensor(o, o, g[:, a:b, HX + h:HX + h + 1].broadcast_to([P, FC, NX]), ALU.mult))
        dve.wait(m)
        for f in range(FE):
            h = f // NX if f < HX else f - HX
            m = dve.run(V.tensor_tensor_scan(g[:, a:b, f], st[:, :, h], g[:, a:b, f],
                                             0.0 if c == 0 else g[:, a - 1:a, f], ALU.mult, ALU.add))
        dve.wait(m)
        summed_f[c] = m
        if c % 2:
            sp.wait(m)
            stored_f[c] = sp.dma("sum_out", sum_rows[:, a - FC:b, :], g[:, a - FC:b, :])

    for c in range(NCF):
        weigh(c)
        if c >= 1:
            sum_up(c - 1)
    cm = sm[:, 20:20 + HEADS]
    w = hm[:, 0, :, :]
    hq = lambda ap: ap.rearrange("p (h q) -> p h q", h=HEADS)
    m = vrun(V.tensor_tensor(w, ident[:, None, :].broadcast_to([P, HEADS, P]),
                             g[:, C2 - 1, FE:FG, None].broadcast_to([P, HEADS, P]), ALU.mult))
    pe.wait(m)
    m = pe.run(T.matmul(bank[0][:, :], ones[:, :], w.rearrange("p h q -> p (h q)"), start=True, stop=True))
    sum_up(NCF - 1)
    m_sum = stored_f[NCF - 1]
    dve.wait(m)
    vrun(V.tensor_tensor(w, hq(bank[0][:, :]), segm[:, 0:1, :].broadcast_to([P, HEADS, P]), ALU.mult))
    vrun(V.tensor_tensor(w, w, segm[:, 1:2, :].broadcast_to([P, HEADS, P]), ALU.add))
    vrun(V.tensor_reduce(cm, w, AXX, ALU.max))
    m = vrun(V.tensor_tensor(w, w, cm[:, :, None].broadcast_to([P, HEADS, P]), ALU.subtract))
    act.wait(m)
    m = act.run(S.activation(w, w, ACT.Exp))
    dve.wait(m)
    m = vrun(V.tensor_tensor(w, w, segm[:, 0:1, :].broadcast_to([P, HEADS, P]), ALU.mult))
    pe.wait(m)
    for h in range(HEADS):
        m = pe.run(T.transpose(bank[1][:, h * P:(h + 1) * P], hm[:, 0, h, :], ident[:, :]))
    act.wait(m)
    m = act.run(S.activation(hm[:, 1, :, :], hq(bank[1][:, :]), ACT.Copy))
    pe.wait(m)
    for h in range(HEADS):
        pe.run(T.matmul(bank[2][:, h * NX:(h + 1) * NX], hm[:, 1, h, :], g[:, C2 - 1, h * NX:(h + 1) * NX],
                        start=True, stop=True))
        carried = pe.run(T.matmul(bank[2][:, HX + h:HX + h + 1], hm[:, 1, h, :], g[:, C2 - 1, HX + h:HX + h + 1],
                                  start=True, stop=True))
    pool.wait(m_sum, fix_f)
    m = pool.sent("fix_in", G.indirect_dma_start(out=sm[:, 32:32 + FG], out_offset=None, in_=sum_d,
                                                 in_offset=at_rows(smi[:, 2:3])))
    dve.wait(m, carried)
    top_row = sm[:, 32 + FE:32 + FG]
    vrun(V.tensor_tensor(sm[:, 68:72], top_row, cm, ALU.max))
    dve.run(V.tensor_tensor(sm[:, 60:64], top_row, sm[:, 68:72], ALU.subtract))
    m = vrun(V.tensor_tensor(sm[:, 64:68], cm, sm[:, 68:72], ALU.subtract))
    act.wait(m)
    m = act.run(S.activation(sm[:, 60:68], sm[:, 60:68], ACT.Exp))
    dve.wait(m)
    sums_s = sm[:, 32:32 + HX].rearrange("p (h e) -> p h e", h=HEADS)
    sums_c = cfix[:, 0:HX].rearrange("p (h e) -> p h e", h=HEADS)
    fac = lambda k: sm[:, 60 + 4 * k:64 + 4 * k]
    dve.run(V.tensor_copy(top_row, sm[:, 68:72]))
    dve.run(V.tensor_tensor(sums_s, sums_s, fac(0)[:, :, None].broadcast_to([P, HEADS, NX]), ALU.mult))
    dve.run(V.tensor_tensor(sm[:, 32 + HX:32 + FE], sm[:, 32 + HX:32 + FE], fac(0), ALU.mult))
    dve.run(V.tensor_tensor(sums_c, bank[2][:, 0:HX].rearrange("p (h e) -> p h e", h=HEADS),
                            fac(1)[:, :, None].broadcast_to([P, HEADS, NX]), ALU.mult))
    vrun(V.tensor_tensor(cfix[:, HX:FE], bank[2][:, HX:FE], fac(1), ALU.mult))
    m = vrun(V.tensor_tensor(sm[:, 32:32 + FE], sm[:, 32:32 + FE], cfix[:, 0:FE], ALU.add))
    pool.wait(m)
    m = pool.sent("fix_out", G.indirect_dma_start(
        out=sum_d, out_offset=at_rows(smi[:, 3:4]), in_=sm[:, 32:32 + FG], in_offset=None,
        bounds_check=E2 - 1, oob_is_err=False))
    pool.wait(m, ("dve_done", dve.n))
    PARTS = ((0, PART * XG), (PART * XG, NT))
    node_in = []
    for n, (t0, t1) in enumerate(PARTS):
        for t in range(t0, t1):
            m = pool.sent(f"node_in{n}", G.indirect_dma_start(out=fsum[:, t, :], out_offset=None, in_=sum_d,
                                                              in_offset=at_rows(idx_f[:, t:t + 1])))
        node_in.append(m)

    def gate(t0, t1):
        n = t1 - t0
        f_ = lambda i: fin[:, i, t0:t1, :]
        f4 = lambda i: fin[:, i, t0:t1, 0:HEADS]
        one = lambda i, k=0: fin[:, i, t0:t1, k:k + 1]
        ft, fs, hs = feat[:, t0:t1, :], fsum[:, t0:t1, :], has_f[:, t0:t1, None]
        full, four = [P, n, HX], [P, n, HEADS]
        a_s, a_d, top_ = ft[:, :, HX:FE], ft[:, :, FE:FG], fs[:, :, FE:FG]
        vrun(V.tensor_tensor(fs, fs, hs.broadcast_to([P, n, FG]), ALU.mult))
        vrun(V.tensor_scalar(one(6), hs, -1.0, BIG, ALU.add, ALU.mult))
        dve.run(V.tensor_tensor(top_, top_, one(6).broadcast_to(four), ALU.add))
        vrun(V.tensor_tensor(f4(4), a_s, a_d, ALU.add))
        vrun(V.scalar_tensor_tensor(out=f4(4), in0=f4(4), scalar=0.2, in1=f4(4), op0=ALU.mult, op1=ALU.max))
        vrun(V.tensor_tensor(f4(3), f4(4), top_, ALU.max))
        dve.run(V.tensor_tensor(f4(4), f4(4), f4(3), ALU.subtract))
        m = vrun(V.tensor_tensor(top_, top_, f4(3), ALU.subtract))
        act.wait(m)
        act.run(S.activation(f4(4), f4(4), ACT.Exp))
        m = act.run(S.activation(top_, top_, ACT.Exp))
        dve.wait(m)

        def heads_times(o, a, b):
            for h in range(HEADS):
                m = dve.run(V.tensor_tensor(o[:, :, h * NX:(h + 1) * NX], a[:, :, h * NX:(h + 1) * NX],
                                            b[:, :, h:h + 1].broadcast_to([P, n, NX]), ALU.mult))
            dve.wait(m)

        heads_times(f_(5), ft[:, :, 0:HX], f4(4))
        heads_times(fs, fs, top_)
        vrun(V.tensor_tensor(fs[:, :, HX:FE], fs[:, :, HX:FE], top_, ALU.mult))
        dve.run(V.tensor_tensor(f_(5), f_(5), fs[:, :, 0:HX], ALU.add))
        vrun(V.tensor_tensor(f4(6), f4(4), fs[:, :, HX:FE], ALU.add))
        vrun(V.tensor_scalar(f4(6), f4(6), 1e-16, None, ALU.add))
        vrun(V.reciprocal(f4(6), f4(6)))
        heads_times(f_(5), f_(5), f4(6))
        vrun(V.tensor_tensor(f_(5), f_(5), gln[:, 0:1, :].broadcast_to(full), ALU.add))
        vrun(V.tensor_reduce(fin[:, 6, t0:t1, 0], f_(5), AXX, ALU.add))
        vrun(V.tensor_scalar(one(6), one(6), 1.0 / HX, None, ALU.mult))
        vrun(V.tensor_tensor(f_(5), f_(5), one(6).broadcast_to(full), ALU.subtract))
        vrun(V.tensor_tensor(f_(2), f_(5), f_(5), ALU.mult))
        vrun(V.tensor_reduce(fin[:, 6, t0:t1, 1], f_(2), AXX, ALU.add))
        m = vrun(V.tensor_scalar(one(6, 1), one(6, 1), 1.0 / HX, EPS, ALU.mult, ALU.add))
        act.wait(m)
        m = act.run(S.activation(one(6, 1), one(6, 1), ACT.Sqrt))
        dve.wait(m)
        vrun(V.reciprocal(one(6, 1), one(6, 1)))
        vrun(V.tensor_tensor(f_(5), f_(5), one(6, 1).broadcast_to(full), ALU.mult))
        vrun(V.tensor_tensor(f_(5), f_(5), gln[:, 1:2, :].broadcast_to(full), ALU.mult))
        vrun(V.tensor_tensor(f_(5), f_(5), gln[:, 2:3, :].broadcast_to(full), ALU.add))
        sc, rank = fin[:, 7, t0:t1, 0:NX], fin[:, 1, t0:t1, 0:NX]
        by_expert = f_(5).rearrange("p t (h e) -> p t e h", h=HEADS)
        vrun(V.tensor_reduce(sc, by_expert, AXX, ALU.add))
        vrun(V.tensor_scalar(sc, sc, 1.0 / HEADS, None, ALU.mult))
        for e in range(NX):
            for k, (lo, hi, op) in enumerate(((0, e, ALU.is_ge), (e + 1, NX, ALU.is_gt))):
                if hi > lo:
                    m = dve.run(V.tensor_tensor(fin[:, 2, t0:t1, 4 * e + lo:4 * e + hi], sc[:, :, lo:hi],
                                                sc[:, :, e:e + 1].broadcast_to([P, n, hi - lo]), op))
            m = dve.run(V.memset(fin[:, 2, t0:t1, 4 * e + e:4 * e + e + 1], 0.0))
        dve.wait(m)
        vrun(V.tensor_reduce(rank, f_(2).rearrange("p t (e o) -> p t e o", o=NX), AXX, ALU.add))
        dve.run(V.tensor_scalar(rank, rank, 1.5, None, ALU.is_lt))
        vrun(V.tensor_reduce(fin[:, 6, t0:t1, 0], sc, AXX, ALU.max))
        m = vrun(V.tensor_tensor(sc, sc, one(6).broadcast_to([P, n, NX]), ALU.subtract))
        act.wait(m)
        m = act.run(S.activation(sc, sc, ACT.Exp))
        dve.wait(m)
        vrun(V.tensor_tensor(sc, sc, rank, ALU.mult))
        vrun(V.tensor_reduce(fin[:, 6, t0:t1, 0], sc, AXX, ALU.add))
        vrun(V.reciprocal(one(6), one(6)))
        return vrun(V.tensor_tensor(sc, sc, one(6).broadcast_to([P, n, NX]), ALU.mult))

    sp.wait(carried, m_sum, ("dve_done", dve.n), x1_out[NT - 1], *made["y_out"])
    outs, loaded = {}, {}

    def load_comb(c):
        s = c % CR
        if c >= CR:
            sp.wait(outs[c - CR])
        rows_ = slice(c * XG * P, (c + 1) * XG * P)
        for e in range(NX):
            sp.dma(f"comb_in{s}", comb[:, s, e, :, :], y_d[e, rows_, :].rearrange("(t p) d -> p t d", p=P))
        loaded[c] = sp.dma(f"comb_in{s}", comb[:, s, NX, :, :], x1_d[rows_, :].rearrange("(t p) d -> p t d", p=P))

    for c in range(CR):
        load_comb(c)
    for c in range(NT // XG):
        for part, (t0, t1) in zip(node_in, PARTS):
            if c * XG == t0:
                dve.wait(part)
                gates = gate(t0, t1)
        s = c % CR
        dve.wait(loaded[c])
        act.wait(loaded[c], gates)
        for e in range(NX):
            for k in range(XG - POOL_TILES, XG):
                y = comb[:, s, e, k, :]
                m_act = act.run(S.activation(y, y, ACT.Copy, scale=fin[:, 7, c * XG + k, e:e + 1]))
            pool.wait(m_act)
            for k in range(XG - POOL_TILES, XG):
                o = comb[:, s, NX, k, :]
                m = pool.run(G.tensor_tensor(o, o, comb[:, s, e, k, :], ALU.add))
            pool.wait(m)
            for k in range(XG - POOL_TILES):
                mv = dve.run(V.scalar_tensor_tensor(
                    out=comb[:, s, NX, k, :], in0=comb[:, s, e, k, :], scalar=fin[:, 7, c * XG + k, e:e + 1],
                    in1=comb[:, s, NX, k, :], op0=ALU.mult, op1=ALU.add))
            dve.wait(mv)
        sp.wait(mv, m)
        n = min(XG, FULL // P - c * XG)
        outs[c] = sp.dma(f"out{s}", out[c * XG * P:(c * XG + n) * P, :].rearrange("(t p) d -> p t d", p=P),
                          comb[:, s, NX, 0:n, :])
        if n < XG:
            outs[c] = sp.dma(f"out{s}", out[FULL:N, :], comb[0:N - FULL, s, NX, n, :])
        if c + CR < NT // XG:
            load_comb(c + CR)
    for lane in sorted(Queue.lanes):
        act.wait((lane, Queue.lanes[lane]))


_INS = ["x", "src", "dst", "L0_gnn_W", "L0_gnn_M", "L0_ffn_W_gat", "L0_ffn_att_src", "L0_ffn_att_dst",
        "L0_ffn_b_gat", "L0_ffn_ln_gamma", "L0_ffn_ln_beta", "L0_ffn_W1", "L0_ffn_b1", "L0_ffn_W2",
        "L0_ffn_b2", "L0_ffn_edge_index"]


def kernel(**inputs):
    import numpy as np
    import concourse.bacc as bacc
    from concourse.bass_utils import run_bass_kernel_spmd

    nc = bacc.Bacc("TRN2", target_bir_lowering=False, num_devices=1)
    arrays, args = {}, []
    for name in _INS:
        a = np.ascontiguousarray(inputs[name])
        arrays[f"in_{name}"] = a
        args.append(nc.dram_tensor(f"in_{name}", a.shape, mybir.dt.from_np(a.dtype), kind="ExternalInput").ap())
    args.append(nc.dram_tensor("out_x", inputs["x"].shape, F32, kind="ExternalOutput").ap())
    build(nc, *args)
    r = run_bass_kernel_spmd(nc, [arrays], core_ids=[0])
    return r.results[0]["out_x"]
```
